# Optimizing a Trainium2 kernel written in Bass

```python
import numpy as np
import jax
import jax.numpy as jnp

def _softmax(x, axis=-1):
    return jax.nn.softmax(x, axis=axis)

def _gelu(x):
    return jax.nn.gelu(x, approximate=True)

def _silu(x):
    return jax.nn.silu(x)

def _sigmoid(x):
    return jax.nn.sigmoid(x)

def _layernorm(x, axis=-1, eps=1e-05):
    m = jnp.mean(x, axis=axis, keepdims=True)
    v = jnp.var(x, axis=axis, keepdims=True)
    return (x - m) / jnp.sqrt(v + eps)

def _scatter_add(tgt, idx, src, axis=0):
    return tgt.at[idx].add(src)

def _segment_sum(src, seg, n):
    return jax.ops.segment_sum(src, seg, n)
kernel_name = 'mk_audio_tower_d1_tok_audfeat512_r4_6028d5'

def setup_inputs(seed: int=0):
    np.random.seed(seed)
    _w = jnp.asarray

    def _rec_inputs():
        import jax
        import jax.numpy as jnp
        _rk = jax.random.key(seed)
        x = -0.000124254 + 0.999853 * jax.random.normal(jax.random.fold_in(_rk, 1), (8, 375, 128), jnp.float32)
        return x
    x = _rec_inputs()

    def _L0_tok_setup():
        import jax, jax.numpy as jnp
        import numpy as np
        CONTEXT = 5
        DILATION = 1
        IN_DIM = 128
        OUT_DIM = 128
        EPS = 1e-05

        def _tdnn(x, W, b, gamma, beta):
            K = W.reshape(OUT_DIM, CONTEXT, IN_DIM).transpose(1, 2, 0)
            y = jax.lax.conv_general_dilated(x, K, window_strides=(1,), padding='VALID', rhs_dilation=(DILATION,), dimension_numbers=('NWC', 'WIO', 'NWC')) + b
            mean = jnp.mean(y, axis=(0, 1))
            var = jnp.mean(jnp.square(y - mean), axis=(0, 1))
            y = (y - mean) * (gamma * jax.lax.rsqrt(var + EPS)) + beta
            return jax.nn.relu(y)
        key = jax.random.key(seed)
        k1, k2, k3, k4, k5 = jax.random.split(key, 5)
        x = jax.random.normal(k1, (64, 250, IN_DIM), dtype=jnp.float32)
        fan_in = IN_DIM * CONTEXT
        bound = 1.0 / np.sqrt(fan_in)
        W = jax.random.uniform(k2, (OUT_DIM, fan_in), minval=-bound, maxval=bound, dtype=jnp.float32)
        b = jax.random.uniform(k3, (OUT_DIM,), minval=-bound, maxval=bound, dtype=jnp.float32)
        gamma = jnp.ones((OUT_DIM,), dtype=jnp.float32)
        beta = jnp.zeros((OUT_DIM,), dtype=jnp.float32)
        return {'x': x, 'W': W, 'b': b, 'gamma': gamma, 'beta': beta}
    _L0_tok_all = _L0_tok_setup()
    _L0_tok_in = {k: v for k, v in _L0_tok_all.items() if k in ('W', 'b', 'gamma', 'beta')}
    del _L0_tok_all

    def _L0_attn_setup():
        import jax, jax.numpy as jnp
        import numpy as np
        from jax import lax
        D_MODEL, D_STATE, EXPAND = (128, 16, 2)
        D_INNER = D_MODEL * EXPAND
        B_SZ, L = (1, 1024)
        EPS = 1e-05

        def _layernorm(y, g, b):
            mu = jnp.mean(y, axis=-1, keepdims=True)
            var = jnp.var(y, axis=-1, keepdims=True)
            return (y - mu) * lax.rsqrt(var + EPS) * g + b

        def _scan_combine(left, right):
            a_l, b_l = left
            a_r, b_r = right
            return (a_r * a_l, a_r * b_l + b_r)
        key = jax.random.key(seed)
        ks = jax.random.split(key, 8)
        s = 0.02
        x = jax.random.normal(ks[0], (B_SZ, L, D_MODEL), dtype=jnp.float32)
        in_proj_w = jax.random.normal(ks[1], (2 * D_INNER, D_MODEL), dtype=jnp.float32) * s
        x_proj_w = jax.random.normal(ks[2], (2 * D_STATE + 1, D_INNER), dtype=jnp.float32) * s
        dt_w = jax.random.normal(ks[3], (D_INNER, 1), dtype=jnp.float32) * s
        dt_b = jax.random.normal(ks[4], (D_INNER,), dtype=jnp.float32) * s
        conv_w = jax.random.normal(ks[5], (D_INNER, 1, 3), dtype=jnp.float32) * s
        conv_b = jax.random.normal(ks[6], (D_INNER,), dtype=jnp.float32) * s
        A_log = jnp.broadcast_to(jnp.log(jnp.arange(1, D_STATE + 1, dtype=jnp.float32))[None, :], (D_INNER, D_STATE))
        D_param = jnp.ones((D_INNER,), dtype=jnp.float32)
        out_w = jax.random.normal(ks[7], (D_MODEL, D_INNER), dtype=jnp.float32) * s
        ln_g = jnp.ones((D_INNER,), dtype=jnp.float32)
        ln_b = jnp.zeros((D_INNER,), dtype=jnp.float32)
        return {'x': x, 'in_proj_w': in_proj_w, 'x_proj_w': x_proj_w, 'dt_w': dt_w, 'dt_b': dt_b, 'conv_w': conv_w, 'conv_b': conv_b, 'A_log': A_log, 'D_param': D_param, 'out_w': out_w, 'ln_g': ln_g, 'ln_b': ln_b}
    _L0_attn_all = _L0_attn_setup()
    _L0_attn_in = {k: v for k, v in _L0_attn_all.items() if k in ('in_proj_w', 'x_proj_w', 'dt_w', 'dt_b', 'conv_w', 'conv_b', 'A_log', 'D_param', 'out_w', 'ln_g', 'ln_b')}
    del _L0_attn_all

    def _L0_ffn_setup():
        import jax, jax.numpy as jnp
        import numpy as np
        B, T, DIM = (2, 64, 128)
        E, H, K = (64, 256, 42)
        key = jax.random.key(seed)
        ks = jax.random.split(key, 7)
        s1 = 1.0 / np.sqrt(DIM).astype(np.float32)
        s2 = 1.0 / np.sqrt(H).astype(np.float32)
        return {'x': jax.random.normal(ks[0], (B, T, DIM), jnp.float32), 'w1': jax.random.uniform(ks[1], (E, DIM, H), jnp.float32, -s1, s1), 'b1': jax.random.uniform(ks[2], (E, H), jnp.float32, -s1, s1), 'w2': jax.random.uniform(ks[3], (E, H, DIM), jnp.float32, -s2, s2), 'b2': jax.random.uniform(ks[4], (E, DIM), jnp.float32, -s2, s2), 'router_w': jax.random.uniform(ks[5], (DIM, E), jnp.float32, -s1, s1), 'router_b': jax.random.uniform(ks[6], (E,), jnp.float32, -s1, s1)}
    _L0_ffn_all = _L0_ffn_setup()
    _L0_ffn_in = {k: v for k, v in _L0_ffn_all.items() if k in ('w1', 'b1', 'w2', 'b2', 'router_w', 'router_b')}
    del _L0_ffn_all
    return {'x': x, 'L0_tok_W': _L0_tok_in['W'], 'L0_tok_b': _L0_tok_in['b'], 'L0_tok_gamma': _L0_tok_in['gamma'], 'L0_tok_beta': _L0_tok_in['beta'], 'L0_attn_in_proj_w': _L0_attn_in['in_proj_w'], 'L0_attn_x_proj_w': _L0_attn_in['x_proj_w'], 'L0_attn_dt_w': _L0_attn_in['dt_w'], 'L0_attn_dt_b': _L0_attn_in['dt_b'], 'L0_attn_conv_w': _L0_attn_in['conv_w'], 'L0_attn_conv_b': _L0_attn_in['conv_b'], 'L0_attn_A_log': _L0_attn_in['A_log'], 'L0_attn_D_param': _L0_attn_in['D_param'], 'L0_attn_out_w': _L0_attn_in['out_w'], 'L0_attn_ln_g': _L0_attn_in['ln_g'], 'L0_attn_ln_b': _L0_attn_in['ln_b'], 'L0_ffn_w1': _L0_ffn_in['w1'], 'L0_ffn_b1': _L0_ffn_in['b1'], 'L0_ffn_w2': _L0_ffn_in['w2'], 'L0_ffn_b2': _L0_ffn_in['b2'], 'L0_ffn_router_w': _L0_ffn_in['router_w'], 'L0_ffn_router_b': _L0_ffn_in['router_b']}

def reference(x, L0_tok_W, L0_tok_b, L0_tok_gamma, L0_tok_beta, L0_attn_in_proj_w, L0_attn_x_proj_w, L0_attn_dt_w, L0_attn_dt_b, L0_attn_conv_w, L0_attn_conv_b, L0_attn_A_log, L0_attn_D_param, L0_attn_out_w, L0_attn_ln_g, L0_attn_ln_b, L0_ffn_w1, L0_ffn_b1, L0_ffn_w2, L0_ffn_b2, L0_ffn_router_w, L0_ffn_router_b):
    import jax
    import jax.numpy as jnp

    def _L0_tok_ref(x, W, b, gamma, beta):
        import jax, jax.numpy as jnp
        import numpy as np
        CONTEXT = 5
        DILATION = 1
        IN_DIM = 128
        OUT_DIM = 128
        EPS = 1e-05

        def _tdnn(x, W, b, gamma, beta):
            K = W.reshape(OUT_DIM, CONTEXT, IN_DIM).transpose(1, 2, 0)
            y = jax.lax.conv_general_dilated(x, K, window_strides=(1,), padding='VALID', rhs_dilation=(DILATION,), dimension_numbers=('NWC', 'WIO', 'NWC')) + b
            mean = jnp.mean(y, axis=(0, 1))
            var = jnp.mean(jnp.square(y - mean), axis=(0, 1))
            y = (y - mean) * (gamma * jax.lax.rsqrt(var + EPS)) + beta
            return jax.nn.relu(y)
        return _tdnn(x, W, b, gamma, beta)

    def _L0_attn_ref(x, in_proj_w, x_proj_w, dt_w, dt_b, conv_w, conv_b, A_log, D_param, out_w, ln_g, ln_b):
        import jax, jax.numpy as jnp
        import numpy as np
        from jax import lax
        D_MODEL, D_STATE, EXPAND = (128, 16, 2)
        D_INNER = D_MODEL * EXPAND
        B_SZ, L = (1, 1024)
        EPS = 1e-05

        def _layernorm(y, g, b):
            mu = jnp.mean(y, axis=-1, keepdims=True)
            var = jnp.var(y, axis=-1, keepdims=True)
            return (y - mu) * lax.rsqrt(var + EPS) * g + b

        def _scan_combine(left, right):
            a_l, b_l = left
            a_r, b_r = right
            return (a_r * a_l, a_r * b_l + b_r)
        d_state = A_log.shape[1]
        xz = jnp.einsum('bld,ed->ble', x, in_proj_w)
        x_in, z = jnp.split(xz, 2, axis=-1)
        xc = lax.conv_general_dilated(jnp.transpose(x_in, (0, 2, 1)), conv_w, window_strides=(1,), padding=[(1, 1)], feature_group_count=conv_w.shape[0])
        xc = jnp.transpose(xc + conv_b[None, :, None], (0, 2, 1))
        xc = jax.nn.silu(xc)
        dbc = jnp.einsum('bli,ei->ble', xc, x_proj_w)
        delta = dbc[..., :1]
        B_mat = dbc[..., 1:1 + d_state]
        C_mat = dbc[..., 1 + d_state:]
        delta = jax.nn.softplus(delta @ dt_w.T + dt_b)
        A = -jnp.exp(A_log)
        dA = jnp.exp(delta[..., None] * A[None, None])
        x_c = (delta * xc)[..., None] * B_mat[:, :, None, :]
        _, h = lax.associative_scan(_scan_combine, (dA, x_c), axis=1)
        y = jnp.einsum('blis,bls->bli', h, C_mat)
        y = y + xc * D_param
        y = y * jax.nn.silu(z)
        y = _layernorm(y, ln_g, ln_b)
        return jnp.einsum('bli,di->bld', y, out_w)

    def _L0_ffn_ref(x, w1, b1, w2, b2, router_w, router_b):
        import jax, jax.numpy as jnp
        import numpy as np
        B, T, DIM = (2, 64, 128)
        E, H, K = (64, 256, 42)
        Bb, Tt, C = x.shape
        N = Bb * Tt
        logits = x @ router_w + router_b
        probs = jax.nn.softmax(logits, axis=-1)
        top_w, top_idx = jax.lax.top_k(probs, K)
        top_w = jax.nn.softmax(top_w, axis=-1)
        xt = x.reshape(N, C)
        top_w = top_w.reshape(N, K)
        top_idx = top_idx.reshape(N, K)
        comb = jnp.zeros((N, E), x.dtype).at[jnp.arange(N)[:, None], top_idx].set(top_w)
        h = jax.nn.gelu(jnp.einsum('td,edh->teh', xt, w1) + b1, approximate=False)
        y = jnp.einsum('teh,ehd->ted', h, w2) + b2
        out = jnp.einsum('ted,te->td', y, comb)
        return out.reshape(Bb, Tt, C)
    h = _L0_tok_ref(x, L0_tok_W, L0_tok_b, L0_tok_gamma, L0_tok_beta)
    h = h + _L0_attn_ref(_layernorm(h, axis=-1), L0_attn_in_proj_w, L0_attn_x_proj_w, L0_attn_dt_w, L0_attn_dt_b, L0_attn_conv_w, L0_attn_conv_b, L0_attn_A_log, L0_attn_D_param, L0_attn_out_w, L0_attn_ln_g, L0_attn_ln_b)
    h = h + _L0_ffn_ref(_layernorm(h, axis=-1), L0_ffn_w1, L0_ffn_b1, L0_ffn_w2, L0_ffn_b2, L0_ffn_router_w, L0_ffn_router_b)
    return h

_drawn_inputs = setup_inputs


def setup_inputs(seed=0):
    import zlib

    import numpy as np

    out = dict(_drawn_inputs(seed))
    spreads = {'L0_tok_gamma': (1.0, 0.2),
     'L0_tok_beta': (0.0, 0.1),
     'L0_attn_D_param': (1.0, 0.2),
     'L0_attn_ln_g': (1.0, 0.2),
     'L0_attn_ln_b': (0.0, 0.1)}
    factors = {'L0_tok_b': 200.0,
     'L0_attn_x_proj_w': 64.0,
     'L0_attn_dt_w': 200.0,
     'L0_attn_dt_b': 200.0,
     'L0_attn_A_log': 200.0,
     'L0_ffn_b1': 8.0,
     'L0_ffn_b2': 8.0,
     'L0_ffn_router_b': 7.975}
    for name, (base, spread) in spreads.items():
        noise = np.random.default_rng([zlib.crc32(name.encode()), seed]).standard_normal(out[name].shape)
        drawn = base * np.exp(spread * noise) if base else spread * noise
        out[name] = jnp.asarray(drawn.astype(out[name].dtype))
    for name, factor in factors.items():
        out[name] = (out[name] * factor).astype(out[name].dtype)
    return out
```

```python
from contextlib import ExitStack

import numpy as np

import concourse.bass as bass
from concourse import mybir

F32 = mybir.dt.float32
F16 = mybir.dt.float16
BF16 = mybir.dt.bfloat16
ALU = mybir.AluOpType
ACT = mybir.ActivationFunctionType
AX = mybir.AxisListType

P = 128
SEQS, FRAMES, DIM = 8, 375, 128
TAPS = 5
T = FRAMES - TAPS + 1
TOKENS = SEQS * T
INNER, HALVES = 256, 2
STATES = 16
EXPERTS, HIDDEN, TOPK = 64, 256, 42
EPS = 1e-5
BIAS = 4
A_LOG_CAP = 84.0

ROWS = SEQS * FRAMES
ROW_TILES = -(-ROWS // P)
LAST_ROWS = ROWS - (ROW_TILES - 1) * P

ROUTE_AT = [0, P, T - P]
OUT_TILES = [(0, P), (P, P), (2 * P, T - 2 * P)]
ROUNDS = -(-(EXPERTS - TOPK) // 8)
SENTINELS = 8 * ROUNDS - (EXPERTS - TOPK)
QCOLS = EXPERTS + SENTINELS

XSCALE, WSCALE = 16.0, 16.0
CSCALE = 1024.0
SELSCALE = 1.0 / 16.0
MSCALE = CSCALE * SELSCALE

def _series():
    f = lambda v: 2 * np.arctanh(np.sqrt(v + 1e-30)) / np.sqrt(v + 1e-30)
    c = np.polynomial.chebyshev.Chebyshev.interpolate(f, 4, domain=[0, 1 / 9])
    return [float(a) for a in c.convert(kind=np.polynomial.Polynomial).coef]


SERIES = _series()


def done(turn):
    return turn + 1 + BIAS


def build(nc, x, tok_w, tok_b, gamma, beta, in_w, xproj_w, dt_w, dt_b, conv_w, conv_b, a_log, d_par,
          out_w, ln_g, ln_b, w1, b1, w2, b2, router_w, router_b, out):
    with ExitStack() as kept:
        def keep(name, shape, dt=F32):
            return kept.enter_context(nc.sbuf_tensor(name, shape, dt))

        hT = keep("hT", [P, TOKENS])
        ident = keep("ident", [P, P])
        ones_ln = keep("ones_ln", [P, P])
        x_hi = keep("x_hi", [P, TOKENS], F16)
        x_lo = keep("x_lo", [P, TOKENS], F16)
        comb = keep("comb", [P, TOKENS], F16)
        front(nc, kept, hT, ident, ones_ln, x, tok_w, tok_b, gamma, beta)
        tower(nc, hT, ident, ones_ln, x_hi, x_lo, comb, in_w, xproj_w, dt_w, dt_b, conv_w, conv_b,
              a_log, d_par, out_w, ln_g, ln_b, router_w, router_b)
        experts(nc, hT, ident, x_hi, x_lo, comb, w1, b1, w2, b2, out)


def clear(nc, sems):
    nums = sorted(s.num for s in sems)
    first = nums[0]
    for at, num in enumerate(nums):
        if at + 1 == len(nums) or nums[at + 1] != num + 1:
            nc.gpsimd.sem_clear(range(first, num + 1))
            first = nums[min(at + 1, len(nums) - 1)]
    nc.all_engine_barrier()


def front(nc, kept, hT, ident, ones_ln, x, tok_w, tok_b, gamma, beta):
    sems = []
    with ExitStack() as ctx:
        ctx.callback(clear, nc, sems)

        def sb(name, shape, dt=F32):
            return ctx.enter_context(nc.sbuf_tensor(name, shape, dt))

        def sem(name):
            sems.append(ctx.enter_context(nc.semaphore(name)))
            return sems[-1]

        rows = sb("rows", [P, ROW_TILES, DIM])
        wrow = sb("wrow", [P, TAPS * DIM])
        xT = sb("xT", [P, ROW_TILES * P])
        wT = sb("wT", [P, TAPS, P])
        vecs = sb("vecs", [P, 3])
        stats = sb("stats", [P, SEQS, 6])
        mv = sb("mv", [P, 2])
        rstd = sb("rstd", [P, 1])
        gain = sb("gain", [P, 1])
        veps, lnv, r0, r0sq, newton = (sb(n, [P, 1]) for n in ("veps", "lnv", "r0", "r0sq", "newton"))
        flip = [ctx.enter_context(nc.psum_tensor(f"flip{i}", [P, 4, P], F32)) for i in range(2)]
        conv = [ctx.enter_context(nc.psum_tensor(f"conv{i}", [P, 512], F32)) for i in range(4)]

        x_in = [sem(f"x_in{i}") for i in range(4)]
        w_in, vecs_in = sem("w_in"), sem("vecs_in")
        zeroed, ident_ready, ones_ready = sem("zeroed"), sem("ident_ready"), sem("ones_ready")
        flipped, flip_copied = sem("flipped"), sem("flip_copied")
        conv_ready, y_ready, stats_ready = sem("conv_ready"), sem("y_ready"), sem("stats_ready")
        moments_ready, rstd_ready, gain_ready = sem("moments_ready"), sem("rstd_ready"), sem("gain_ready")
        veps_ready, ln_taken, r0_ready, r0_squared, newton_ready = (
            sem(n) for n in ("veps_ready", "ln_taken", "r0_ready", "r0_squared", "newton_ready"))
        scaled, normed = sem("scaled"), sem("normed")

        x_rows = x.rearrange("b t d -> (b t) d")
        GROUPS = -(-ROW_TILES // 4)
        WGROUPS = -(-TAPS // 4)
        load_tiles = [(0, 4), (4, 12), (12, ROW_TILES - 1)]

        block = ctx.enter_context(nc.Block())

        @block.sync
        def _(sp):
            sp.dma_start(wrow[:], tok_w).then_inc(w_in, 16)
            for i, (a, z) in enumerate(load_tiles):
                sp.dma_start(rows[:, a:z, :], x_rows[a * P:z * P, :].rearrange("(n p) d -> p n d", p=P)
                             ).then_inc(x_in[i], 16)
            sp.dma_start(rows[0:LAST_ROWS, ROW_TILES - 1, :], x_rows[(ROW_TILES - 1) * P:ROWS, :]).then_inc(x_in[3], 16)
            for i, v in enumerate((tok_b, gamma, beta)):
                sp.dma_start(vecs[:, i:i + 1], v).then_inc(vecs_in, 16)

        @block.gpsimd
        def _(pool):
            pool.memset(ident[:], 0.0).then_inc(zeroed, 1)
            pool.wait_ge(zeroed, 1)
            pool.affine_select(out=ident[:], in_=ident[:], compare_op=ALU.not_equal, fill=1.0, base=0,
                               pattern=[[-1, P]], channel_multiplier=1).then_inc(ident_ready, 1)
            pool.memset(ones_ln[:], 1.0 / DIM).then_inc(ones_ready, 1)

        @block.tensor
        def _(pe):
            pe.wait_ge(ident_ready, 1)
            pe.wait_ge(w_in, 16)
            for g in range(WGROUPS):
                for k in range(4 * g, min(4 * g + 4, TAPS)):
                    last = pe.transpose(flip[g % 2][:, k % 4, :], wrow[:, k * DIM:(k + 1) * DIM], ident[:])
                last.then_inc(flipped, 1)
            for g in range(GROUPS):
                pe.wait_ge(flip_copied, g + WGROUPS - 1)
                for n in range(4 * g, min(4 * g + 4, ROW_TILES)):
                    for i, (a, _z) in enumerate(load_tiles):
                        if n == a:
                            pe.wait_ge(x_in[i], 16)
                    if n < ROW_TILES - 1:
                        last = pe.transpose(flip[(g + WGROUPS) % 2][:, n % 4, :], rows[:, n, :], ident[:])
                    else:
                        pe.wait_ge(x_in[3], 16)
                        last = pe.transpose(flip[(g + WGROUPS) % 2][:, n % 4, 0:LAST_ROWS],
                                            rows[0:LAST_ROWS, n, :], ident[0:LAST_ROWS, 0:LAST_ROWS])
                last.then_inc(flipped, 1)
            for b in range(SEQS):
                need = -(-((b + 1) * FRAMES) // (4 * P))
                pe.wait_ge(flip_copied, WGROUPS + need)
                if b >= 4:
                    pe.wait_ge(y_ready, b - 3)
                for k in range(TAPS):
                    last = pe.matmul(conv[b % 4][:, 0:T], wT[:, k, :], xT[:, b * FRAMES + k:b * FRAMES + k + T],
                                     start=(k == 0), stop=(k == TAPS - 1))
                last.then_inc(conv_ready, 1)

        @block.scalar
        def _(act):
            for g in range(WGROUPS):
                n = min(4, TAPS - 4 * g)
                act.wait_ge(flipped, g + 1)
                act.copy(wT[:, 4 * g:4 * g + n, :], flip[g % 2][:, 0:n, :]).then_inc(flip_copied, 1)
            for g in range(GROUPS):
                act.wait_ge(flipped, g + 1 + WGROUPS)
                z = min(4 * P, ROWS - 4 * P * g)
                act.copy(xT[:, 4 * P * g:4 * P * g + z],
                         flip[(g + WGROUPS) % 2][:].rearrange("p a b -> p (a b)")[:, 0:z]).then_inc(flip_copied, 1)
            act.wait_ge(vecs_in, 48)
            for b in range(SEQS):
                act.wait_ge(conv_ready, b + 1)
                act.activation(hT[:, b * T:(b + 1) * T], conv[b % 4][:, 0:T], ACT.Identity,
                               bias=vecs[:, 0:1]).then_inc(y_ready, 1)
            act.wait_ge(veps_ready, 1)
            act.activation(lnv[:], veps[:], ACT.Ln).then_inc(ln_taken, 1)
            act.wait_ge(ln_taken, 1)
            act.activation(r0[:], lnv[:], ACT.Exp, scale=-0.5).then_inc(r0_ready, 1)
            act.wait_ge(r0_ready, 1)
            act.activation(r0sq[:], r0[:], ACT.Square).then_inc(r0_squared, 1)
            for b in range(SEQS):
                act.wait_ge(scaled, b + 1)
                act.activation(hT[:, b * T:(b + 1) * T], hT[:, b * T:(b + 1) * T], ACT.Relu,
                               bias=vecs[:, 2:3]).then_inc(normed, 1)

        @block.vector
        def _(dve):
            for b in range(SEQS):
                dve.wait_ge(y_ready, b + 1)
                dve.bn_stats(stats[:, b, :], hT[:, b * T:(b + 1) * T]).then_inc(stats_ready, 1)
            dve.wait_ge(stats_ready, SEQS)
            dve.bn_aggr(mv[:], stats[:].rearrange("p b s -> p (b s)")).then_inc(moments_ready, 1)
            dve.wait_ge(moments_ready, 1)
            dve.tensor_scalar(veps[:], mv[:, 1:2], EPS, None, ALU.add).then_inc(veps_ready, 1)
            dve.wait_ge(r0_squared, 1)
            dve.wait_ge(veps_ready, 1)
            dve.tensor_tensor(newton[:], r0sq[:], veps[:], ALU.mult).then_inc(newton_ready, 1)
            dve.wait_ge(newton_ready, 1)
            dve.tensor_scalar(newton[:], newton[:], -0.5, 1.5, ALU.mult, ALU.add).then_inc(newton_ready, 1)
            dve.wait_ge(newton_ready, 2)
            dve.tensor_tensor(rstd[:], newton[:], r0[:], ALU.mult).then_inc(rstd_ready, 1)
            dve.wait_ge(rstd_ready, 1)
            dve.wait_ge(vecs_in, 48)
            dve.tensor_tensor(gain[:], rstd[:], vecs[:, 1:2], ALU.mult).then_inc(gain_ready, 1)
            dve.wait_ge(gain_ready, 1)
            for b in range(SEQS):
                s = hT[:, b * T:(b + 1) * T]
                dve.tensor_scalar(s, s, mv[:, 0:1], gain[:, 0:1], ALU.subtract, ALU.mult).then_inc(scaled, 1)


def tower(nc, hT, ident, ones_ln, x_hi, x_lo, comb, in_w, xproj_w, dt_w, dt_b, conv_w, conv_b,
          a_log, d_par, out_w, ln_g, ln_b, router_w, router_b):
    sems = []
    with ExitStack() as ctx:
        ctx.callback(clear, nc, sems)

        def sb(name, shape, dt=F32):
            return ctx.enter_context(nc.sbuf_tensor(name, shape, dt))

        def bank(name, shape=(P, 512)):
            return ctx.enter_context(nc.psum_tensor(name, list(shape), F32))

        in_rows = sb("in_rows", [P, 4, DIM])
        xp_rows = sb("xp_rows", [1 + 2 * STATES, INNER])
        out_rows = sb("out_rows", [P, INNER])
        in_T = sb("in_T", [P, 4, P])
        xp_T = sb("xp_T", [P, HALVES, P])
        out_T = sb("out_T", [P, HALVES, P])
        out_gT = sb("out_gT", [P, HALVES, P])
        out_bias = sb("out_bias", [P, 1])
        a_raw = sb("a_raw", [P, HALVES, STATES])
        a_capped = sb("a_capped", [P, HALVES, STATES])
        a_exp = sb("a_exp", [P, HALVES, STATES])
        a_neg = sb("a_neg", [P, HALVES, STATES])
        taps = sb("taps", [P, HALVES, 3])
        vec = sb("vec", [P, 5, HALVES])
        dt_row = sb("dt_row", [1, INNER])
        rw = sb("rw", [P, EXPERTS])
        rb = sb("rb", [1, EXPERTS])
        ones_row = sb("ones_row", [1, P])
        ones_inner = sb("ones_inner", [P, P])
        pick_raw = sb("pick_raw", [P, 2 * STATES])
        pick = sb("pick", [P, 2 * STATES], BF16)

        cen1, sq1, rs1, xn1 = (sb(n, [P, T]) for n in ("cen1", "sq1", "rs1", "xn1"))
        xpad = sb("xpad", [P, HALVES, T + 2])
        cv = sb("cv", [P, HALVES, T])
        cexp, cden = sb("cexp", [P, HALVES, T]), sb("cden", [P, HALVES, T])
        zt, zexp, zden = (sb(n, [P, HALVES, T]) for n in ("zt", "zexp", "zden"))
        zrec, crec, dtrec = (sb(n, [P, HALVES, T]) for n in ("zrec", "crec", "dtrec"))
        d_row = sb("d_row", [1, T])
        rest = sb("rest", [P, T])
        dt_pos, dt_abs, dt_exp, dt_den, dt_s, dt_s2, dt_poly = (
            sb(n, [P, HALVES, T]) for n in ("dt_pos", "dt_abs", "dt_exp", "dt_den", "dt_s", "dt_s2", "dt_poly"))
        xc = [sb(f"xc{i}", [P, HALVES, T]) for i in range(2)]
        zg = [sb(f"zg{i}", [P, HALVES, T]) for i in range(2)]
        bc = [sb(f"bc{i}", [P, T], BF16) for i in range(2)]
        delta = [sb(f"delta{i}", [P, HALVES, T]) for i in range(2)]
        dx = [sb(f"dx{i}", [P, HALVES, T]) for i in range(2)]
        dA = [sb(f"dA{i}", [P, HALVES, T]) for i in range(2)]
        bx = [sb(f"bx{i}", [P, HALVES, T]) for i in range(2)]
        hs = [sb(f"hs{i}", [P, HALVES, T]) for i in range(2)]
        cs = [sb(f"cs{i}", [P, T]) for i in range(2)]
        hc = [sb(f"hc{i}", [P, HALVES, T]) for i in range(2)]
        yb, yz, cen2, sq2, yn = (sb(n, [P, HALVES, T]) for n in ("yb", "yz", "cen2", "sq2", "yn"))
        rs2, cen3, sq3, rs3, xn3 = (sb(n, [P, T]) for n in ("rs2", "cen3", "sq3", "rs3", "xn3"))
        eps = sb("eps", [P, 1])
        lnv, r0, r0sq, newton = ([sb(f"{n}{i}", [P, T]) for i in range(4)] for n in ("lnv", "r0_", "r0sq", "newton"))
        top, ssum, srec, wsum, wrec = (sb(n, [P, 3]) for n in ("top", "ssum", "srec", "wsum", "wrec"))
        lg, ex, ew, wm = (sb(n, [P, 3, EXPERTS]) for n in ("lg", "ex", "ew", "wm"))
        qn = sb("qn", [P, 3, QCOLS])
        low8 = sb("low8", [P, 3, 8])
        cw = sb("cw", [P, 3, 2, EXPERTS])

        bank_b, bank_c = bank("bank_b"), bank("bank_c")
        ysum = [bank(f"ysum{i}") for i in range(HALVES)]
        pre = [bank(f"pre{i}") for i in range(2)]
        post = [bank(f"post{i}") for i in range(2)]

        def sem(name):
            sems.append(ctx.enter_context(nc.semaphore(name)))
            return sems[-1]

        weights_in = sem("weights_in")
        xp_zeroed, inner_ready, row_ready, pick_zeroed, pick_made, pick_ready = (
            sem(n) for n in ("xp_zeroed", "inner_ready", "row_ready", "pick_zeroed", "pick_made", "pick_ready"))
        eps_ready, waited = sem("eps_ready"), sem("waited")
        zero_ready, a_capped_ready, a_exp_ready, a_neg_ready = (
            sem(n) for n in ("zero_ready", "a_capped_ready", "a_exp_ready", "a_neg_ready"))
        in_flipped, xp_flipped, out_flipped = sem("in_flipped"), sem("xp_flipped"), sem("out_flipped")
        in_copied, xp_copied, out_copied = sem("in_copied"), sem("xp_copied"), sem("out_copied")
        bias_summed, bias_ready = sem("bias_summed"), sem("bias_ready")
        pe_events = {n: sem(n) for n in (
            "mean1", "var1", "xin_ready", "z_ready", "dbc_ready", "dt_ready", "b_cast", "c_cast",
            "summed", "ysum_ready", "mean2", "var2", "proj_ready", "mean3", "var3", "logits_ready",
            "comb_flipped")}
        act_events = {n: sem(n) for n in (
            "sq1_ready", "xin_copied", "zexp_ready", "cexp_ready", "drow_ready", "dtabs_ready", "dtexp_ready",
            "dts2_ready", "dA_ready", "c_copied", "sq2_ready", "sq3_ready", "xhi_ready", "ex_ready",
            "ew_ready", "comb_hi_ready", "bc_hi_ready", "bc_mid_ready",
            *(f"{n}{i}" for n in ("ln_taken", "r0_ready", "r0_squared") for i in (1, 2, 3)))}
        dve_events = {n: sem(n) for n in (
            "cen1_ready", "rs1_ready", "xn1_ready", "tap0_done", "tap1_done", "conv_ready2", "xc_ready", "zg_ready",
            "rest_ready", "dts_ready", "poly_done", "delta_ready", "bx_ready", "scan_done",
            "y_ready2", "cen2_ready", "rs2_ready", "h_ready", "cen3_ready", "rs3_ready", "xn3_ready",
            "xlo_ready", "top_ready", "lg_ready", "ssum_ready", "srec_ready", "nsrec_ready", "qn_ready",
            "low_found", "low_dropped", "wm_ready", "wsum_ready", "wrec_ready", "bc_ready", "cw_ready", "comb_ready", "zrec_ready", "crec_ready", "dtrec_ready",
            *(f"{n}{i}" for n in ("vr_ready", "newton_ready") for i in (1, 2, 3)))}
        pool_events = {n: sem(n) for n in (
            "cden_ready", "zden_ready", "dtden_ready", "dx_ready", "hc_ready",
            "gated", "yn_ready")}
        ev = {**pe_events, **act_events, **dve_events, **pool_events}

        def tokens(buf, b, at=0, n=T, parts=slice(0, P)):
            return buf[parts, bass.ds(b * T + at, n)]

        def over_halves(ap):
            return ap.unsqueeze(1).broadcast_to([P, HALVES, T])

        def over_experts(ap):
            return ap.unsqueeze(2).broadcast_to([P, 3, EXPERTS])

        NS = STATES

        def wait_apart(eng, event, value):
            eng.wait_ge(ev[event], value)
            eng.sem_inc(waited, 1)

        def rsqrt_scalar(act, i, b, var):
            act.wait_ge(ev[f"var{i}"], done(b))
            act.wait_ge(ev[f"rs{i}_ready"], done(b - 1))
            act.activation(lnv[i][:], var, ACT.Ln, bias=eps[:]).then_inc(ev[f"ln_taken{i}"], 1)
            act.wait_ge(ev[f"ln_taken{i}"], done(b))
            act.activation(r0[i][:], lnv[i][:], ACT.Exp, scale=-0.5).then_inc(ev[f"r0_ready{i}"], 1)
            act.wait_ge(ev[f"r0_ready{i}"], done(b))
            act.activation(r0sq[i][:], r0[i][:], ACT.Square).then_inc(ev[f"r0_squared{i}"], 1)

        def rsqrt_vector(dve, i, b, var, rs):
            dve.wait_ge(ev[f"r0_squared{i}"], done(b))
            dve.scalar_tensor_tensor(out=newton[i][:], in0=var, scalar=EPS, in1=r0sq[i][:],
                                     op0=ALU.add, op1=ALU.mult).then_inc(ev[f"vr_ready{i}"], 1)
            dve.wait_ge(ev[f"vr_ready{i}"], done(b))
            dve.tensor_scalar(newton[i][:], newton[i][:], -0.5, 1.5, ALU.mult, ALU.add).then_inc(ev[f"newton_ready{i}"], 1)
            dve.wait_ge(ev[f"newton_ready{i}"], done(b))
            dve.tensor_tensor(rs[:], newton[i][:], r0[i][:], ALU.mult).then_inc(ev[f"rs{i}_ready"], 1)

        def pre_tensor(pe, b, k):
            q = parity(b)
            b = turn(b)
            if k == 0:
                pe.wait_ge(ev["dtabs_ready"], done(b - 1))
                pe.matmul(pre[0][:, 0:T], ones_ln[:], tokens(hT, b), start=True, stop=True).then_inc(ev["mean1"], 1)
            if k == 1:
                pe.wait_ge(ev["sq1_ready"], done(b))
                pe.matmul(pre[1][:, 0:T], ones_ln[:], sq1[:], start=True, stop=True).then_inc(ev["var1"], 1)
            if k == 2:
                pe.wait_ge(ev["xn1_ready"], done(b))
                for h in range(HALVES):
                    last = pe.matmul(pre[h][:, 0:T], in_T[:, h, :], xn1[:], start=True, stop=True)
                last.then_inc(ev["xin_ready"], 1)
            if k == 3:
                pe.wait_ge(ev["xin_copied"], done(b))
                for h in range(HALVES):
                    last = pe.matmul(pre[h][:, 0:T], in_T[:, HALVES + h, :], xn1[:], start=True, stop=True)
                last.then_inc(ev["z_ready"], 1)
            if k == 7:
                pe.wait_ge(ev["zexp_ready"], done(b))
                pe.wait_ge(ev["xc_ready"], done(b))
                for h in range(HALVES):
                    last = pe.matmul(pre[0][:, 0:T], xp_T[:, h, :], xc[q][:, h, :], start=(h == 0), stop=(h == 1))
                last.then_inc(ev["dbc_ready"], 1)
            if k == 8:
                pe.wait_ge(ev["drow_ready"], done(b))
                pe.wait_ge(ev["rest_ready"], done(b))
                for h in range(HALVES):
                    last = pe.matmul(pre[h][:, 0:T], dt_row[0:1, h * P:(h + 1) * P], d_row[0:1, :], start=True, stop=True)
                last.then_inc(ev["dt_ready"], 1)

        def pre_scalar(act, b, k):
            q = parity(b)
            b = turn(b)
            if k == 0:
                act.wait_ge(ev["cen1_ready"], done(b))
                act.activation(sq1[:], cen1[:], ACT.Square).then_inc(ev["sq1_ready"], 1)
            if k == 1:
                rsqrt_scalar(act, 1, b, pre[1][:, 0:T])
            if k == 2:
                act.wait_ge(ev["xin_ready"], done(b))
                act.copy(xpad[:, 0, 1:T + 1], pre[0][:, 0:T])
                act.copy(xpad[:, 1, 1:T + 1], pre[1][:, 0:T]).then_inc(ev["xin_copied"], 1)
            if k == 3:
                act.wait_ge(ev["z_ready"], done(b))
                act.wait_ge(ev["zg_ready"], done(b - 1))
                for h in range(HALVES):
                    act.copy(zt[:, h, :], pre[h][:, 0:T])
                    last = act.activation(zexp[:, h, :], pre[h][:, 0:T], ACT.Exp, scale=-1.0)
                last.then_inc(ev["zexp_ready"], 1)
            if k == 5:
                act.wait_ge(ev["conv_ready2"], done(b))
                act.activation(cexp[:], cv[:], ACT.Exp, scale=-1.0).then_inc(ev["cexp_ready"], 1)
            if k == 7:
                act.wait_ge(ev["dbc_ready"], done(b))
                act.copy(d_row[0:1, :], pre[0][0:1, 0:T]).then_inc(ev["drow_ready"], 1)
                act.wait_ge(ev["ysum_ready"], done(b - 2))
                act.copy(bc[q][:], pre[0][:, 0:T]).then_inc(ev["bc_hi_ready"], 1)
            if k == 8:
                act.wait_ge(ev["rest_ready"], done(b))
                act.copy(bc[q][64:128, :], rest[64:128, :]).then_inc(ev["bc_mid_ready"], 1)
                act.wait_ge(ev["dt_ready"], done(b))
                act.wait_ge(ev["delta_ready"], done(b - 1))
                for h in range(HALVES):
                    act.activation(dt_pos[:, h, :], pre[h][:, 0:T], ACT.Relu, bias=vec[:, 1, h:h + 1])
                    last = act.activation(dt_abs[:, h, :], pre[h][:, 0:T], ACT.Abs, bias=vec[:, 1, h:h + 1])
                last.then_inc(ev["dtabs_ready"], 1)
                act.wait_ge(ev["dtabs_ready"], done(b))
                act.activation(dt_exp[:], dt_abs[:], ACT.Exp, scale=-1.0).then_inc(ev["dtexp_ready"], 1)
            if k == 10:
                act.wait_ge(ev["dts_ready"], done(b))
                act.activation(dt_s2[:], dt_s[:], ACT.Square).then_inc(ev["dts2_ready"], 1)

        def pre_vector(dve, b, k):
            q = parity(b)
            b = turn(b)
            if k == 0:
                dve.wait_ge(ev["mean1"], done(b))
                dve.tensor_tensor(cen1[:], tokens(hT, b), pre[0][:, 0:T], ALU.subtract).then_inc(ev["cen1_ready"], 1)
            if k == 1:
                rsqrt_vector(dve, 1, b, pre[1][:, 0:T], rs1)
                dve.wait_ge(ev["rs1_ready"], done(b))
                dve.tensor_tensor(xn1[:], cen1[:], rs1[:], ALU.mult).then_inc(ev["xn1_ready"], 1)
            if k == 3:
                dve.wait_ge(ev["xin_copied"], done(b))
                dve.wait_ge(ev["cexp_ready"], done(b - 1))
                for h in range(HALVES):
                    last = dve.tensor_scalar(cv[:, h, :], xpad[:, h, 0:T], taps[:, h, 0:1], vec[:, 0, h:h + 1],
                                             ALU.mult, ALU.add)
                last.then_inc(ev["tap0_done"], 1)
                dve.wait_ge(ev["tap0_done"], done(b))
                for h in range(HALVES):
                    last = dve.scalar_tensor_tensor(out=cv[:, h, :], in0=xpad[:, h, 1:T + 1], scalar=taps[:, h, 1:2],
                                                    in1=cv[:, h, :], op0=ALU.mult, op1=ALU.add)
                last.then_inc(ev["tap1_done"], 1)
                dve.wait_ge(ev["tap1_done"], done(b))
                for h in range(HALVES):
                    last = dve.scalar_tensor_tensor(out=cv[:, h, :], in0=xpad[:, h, 2:T + 2], scalar=taps[:, h, 2:3],
                                                    in1=cv[:, h, :], op0=ALU.mult, op1=ALU.add)
                last.then_inc(ev["conv_ready2"], 1)
            if k == 5:
                dve.wait_ge(ev["zden_ready"], done(b))
                dve.wait_ge(ev["gated"], done(b - 2))
                dve.reciprocal(zrec[:], zden[:]).then_inc(ev["zrec_ready"], 1)
                dve.wait_ge(ev["zrec_ready"], done(b))
                dve.tensor_tensor(zg[q][:], zt[:], zrec[:], ALU.mult).then_inc(ev["zg_ready"], 1)
            if k == 6:
                dve.wait_ge(ev["cden_ready"], done(b))
                dve.wait_ge(ev["ysum_ready"], done(b - 2))
                dve.reciprocal(crec[:], cden[:]).then_inc(ev["crec_ready"], 1)
                dve.wait_ge(ev["crec_ready"], done(b))
                dve.tensor_tensor(xc[q][:], cv[:], crec[:], ALU.mult).then_inc(ev["xc_ready"], 1)
            if k == 7:
                dve.wait_ge(ev["bc_hi_ready"], done(b))
                dve.tensor_tensor(rest[:], pre[0][:, 0:T], bc[q][:], ALU.subtract).then_inc(ev["rest_ready"], 1)
            if k == 8:
                dve.wait_ge(ev["bc_mid_ready"], done(b))
                dve.tensor_tensor(bc[q][96:128, :], rest[96:128, :], bc[q][96:128, :], ALU.subtract
                                  ).then_inc(ev["bc_ready"], 1)
            if k == 10:
                dve.wait_ge(ev["dtden_ready"], done(b))
                dve.reciprocal(dtrec[:], dt_den[:]).then_inc(ev["dtrec_ready"], 1)
                dve.wait_ge(ev["dtrec_ready"], done(b))
                dve.tensor_tensor(dt_s[:], dt_exp[:], dtrec[:], ALU.mult).then_inc(ev["dts_ready"], 1)
            if k == 11:
                dve.wait_ge(ev["dts2_ready"], done(b))
                dve.tensor_scalar(dt_poly[:], dt_s2[:], SERIES[4], None, ALU.mult).then_inc(ev["poly_done"], 1)
                for i, c in enumerate(SERIES[3:0:-1]):
                    dve.wait_ge(ev["poly_done"], done(5 * b + i))
                    dve.scalar_tensor_tensor(out=dt_poly[:], in0=dt_poly[:], scalar=c, in1=dt_s2[:],
                                             op0=ALU.add, op1=ALU.mult).then_inc(ev["poly_done"], 1)
            if k == 12:
                dve.wait_ge(ev["poly_done"], done(5 * b + 3))
                dve.scalar_tensor_tensor(out=dt_poly[:], in0=dt_poly[:], scalar=SERIES[0], in1=dt_s[:],
                                         op0=ALU.add, op1=ALU.mult).then_inc(ev["poly_done"], 1)
                dve.wait_ge(ev["poly_done"], done(5 * b + 4))
                dve.wait_ge(ev["ysum_ready"], done(b - 2))
                dve.tensor_tensor(delta[q][:], dt_poly[:], dt_pos[:], ALU.add).then_inc(ev["delta_ready"], 1)

        def pre_gpsimd(pool, b, k):
            q = parity(b)
            b = turn(b)
            if k == 4:
                wait_apart(pool, "zexp_ready", done(b))
                pool.tensor_scalar(zden[:], zexp[:], 1.0, None, ALU.add).then_inc(ev["zden_ready"], 1)
            if k == 5:
                wait_apart(pool, "cexp_ready", done(b))
                pool.tensor_scalar(cden[:], cexp[:], 1.0, None, ALU.add).then_inc(ev["cden_ready"], 1)
            if k == 9:
                wait_apart(pool, "dtexp_ready", done(b))
                pool.tensor_scalar(dt_den[:], dt_exp[:], 2.0, None, ALU.add).then_inc(ev["dtden_ready"], 1)
            if k == 13:
                pool.wait_ge(ev["delta_ready"], done(b))
                pool.tensor_tensor(dx[q][:], delta[q][:], xc[q][:], ALU.mult).then_inc(ev["dx_ready"], 1)

        def sum_states(pe, b, s):
            n = NS * turn(b) + s
            if s == 0:
                pe.wait_ge(ev["y_ready2"], done(turn(b) - 1))
            pe.wait_ge(ev["hc_ready"], done(n))
            for h in range(HALVES):
                last = pe.matmul(ysum[h][:, 0:T], ident[:], hc[s % 2][:, h, :], start=(s == 0), stop=(s == NS - 1))
            last.then_inc(ev["summed"], 1)
            if s == NS - 1:
                pe.wait_ge(ev["summed"], done(n))
                pe.sem_inc(ev["ysum_ready"], 1)

        def scan_tensor(pe, b, s):
            q, n = parity(b), NS * turn(b) + s
            if s == 0:
                pe.wait_ge(ev["bc_ready"], done(turn(b)))
            pe.wait_ge(ev["bx_ready"], done(n - 1))
            pe.matmul(bank_b[:, 0:T], pick[:, s:s + 1].broadcast_to([P, P]), bc[q][:], start=True, stop=True
                      ).then_inc(ev["b_cast"], 1)
            pe.wait_ge(ev["c_copied"], done(n - 1))
            pe.matmul(bank_c[:, 0:T], pick[:, NS + s:NS + s + 1].broadcast_to([P, P]), bc[q][:], start=True, stop=True
                      ).then_inc(ev["c_cast"], 1)
            if s > 0:
                sum_states(pe, b, s - 1)

        def scan_scalar(act, b, s):
            q, n = parity(b), NS * turn(b) + s
            if s == 0:
                act.wait_ge(ev["delta_ready"], done(turn(b)))
            act.wait_ge(ev["scan_done"], done(n - 2))
            for h in range(HALVES):
                last = act.activation(dA[s % 2][:, h, 1:T], delta[q][:, h, 1:T], ACT.Exp, scale=a_neg[:, h, s:s + 1])
            last.then_inc(ev["dA_ready"], 1)
            act.wait_ge(ev["c_cast"], done(n))
            act.wait_ge(ev["hc_ready"], done(n - 2))
            act.copy(cs[s % 2][:], bank_c[:, 0:T]).then_inc(ev["c_copied"], 1)

        def scan_vector(dve, b, s):
            q, n = parity(b), NS * turn(b) + s
            if s == 0:
                dve.wait_ge(ev["dx_ready"], done(turn(b)))
            dve.wait_ge(ev["b_cast"], done(n))
            dve.tensor_tensor(bx[s % 2][:], dx[q][:], over_halves(bank_b[:, 0:T]), ALU.mult).then_inc(ev["bx_ready"], 1)
            dve.wait_ge(ev["bx_ready"], done(n))
            dve.wait_ge(ev["dA_ready"], done(n))
            dve.wait_ge(ev["hc_ready"], done(n - 2))
            dve.tensor_tensor_scan(hs[s % 2][:].rearrange("p h t -> p (h t)"), dA[s % 2][:].rearrange("p h t -> p (h t)"),
                                   bx[s % 2][:].rearrange("p h t -> p (h t)"), 0.0, ALU.mult, ALU.add
                                   ).then_inc(ev["scan_done"], 1)

        def scan_gpsimd(pool, b, s):
            n = NS * turn(b) + s
            pool.wait_ge(ev["scan_done"], done(n))
            pool.wait_ge(ev["c_copied"], done(n))
            pool.wait_ge(ev["summed"], done(n - 2))
            pool.tensor_tensor(hc[s % 2][:], hs[s % 2][:], over_halves(cs[s % 2][:]), ALU.mult
                               ).then_inc(ev["hc_ready"], 1)

        def post_tensor(pe, b, k):
            b = turn(b)
            if k == 1:
                pe.wait_ge(ev["gated"], done(b))
                pe.wait_ge(ev["comb_ready"], done(b - 1))
                for h in range(HALVES):
                    last = pe.matmul(post[0][:, 0:T], ones_inner[:], yz[:, h, :], start=(h == 0), stop=(h == 1))
                last.then_inc(ev["mean2"], 1)
            if k == 2:
                pe.wait_ge(ev["sq2_ready"], done(b))
                for h in range(HALVES):
                    last = pe.matmul(post[1][:, 0:T], ones_inner[:], sq2[:, h, :], start=(h == 0), stop=(h == 1))
                last.then_inc(ev["var2"], 1)
            if k == 4:
                pe.wait_ge(ev["yn_ready"], done(b))
                for h in range(HALVES):
                    last = pe.matmul(post[0][:, 0:T], out_gT[:, h, :], yn[:, h, :], start=(h == 0), stop=(h == 1))
                last.then_inc(ev["proj_ready"], 1)
            if k == 5:
                pe.wait_ge(ev["h_ready"], done(b))
                pe.matmul(post[1][:, 0:T], ones_ln[:], tokens(hT, b), start=True, stop=True).then_inc(ev["mean3"], 1)
            if k == 6:
                pe.wait_ge(ev["sq3_ready"], done(b))
                pe.matmul(post[0][:, 0:T], ones_ln[:], sq3[:], start=True, stop=True).then_inc(ev["var3"], 1)
            if k == 7:
                pe.wait_ge(ev["xn3_ready"], done(b))
                for i, at in enumerate(ROUTE_AT):
                    pe.matmul(post[1][:, i * EXPERTS:(i + 1) * EXPERTS], xn3[:, at:at + P], rw[:], start=True, stop=False)
                    last = pe.matmul(post[1][:, i * EXPERTS:(i + 1) * EXPERTS], ones_row[:], rb[:], start=False, stop=True)
                last.then_inc(ev["logits_ready"], 1)
            if k == 14:
                pe.wait_ge(ev["cw_ready"], done(b))
                for i, at in enumerate(ROUTE_AT):
                    last = pe.transpose(post[0][:, at:at + P], cw[:, i, :, :].rearrange("p a e -> p (a e)"), ident[:])
                last.then_inc(ev["comb_flipped"], 1)

        def post_scalar(act, b, k):
            b = turn(b)
            if k == 1:
                act.wait_ge(ev["cen2_ready"], done(b))
                act.activation(sq2[:], cen2[:], ACT.Square).then_inc(ev["sq2_ready"], 1)
            if k == 2:
                rsqrt_scalar(act, 2, b, post[1][:, 0:T])
            if k == 6:
                rsqrt_scalar(act, 3, b, post[0][:, 0:T])
            if k == 5:
                act.wait_ge(ev["cen3_ready"], done(b))
                act.activation(sq3[:], cen3[:], ACT.Square).then_inc(ev["sq3_ready"], 1)
            if k == 7:
                act.wait_ge(ev["xn3_ready"], done(b))
                act.activation(tokens(x_hi, b), xn3[:], ACT.Copy, scale=XSCALE).then_inc(ev["xhi_ready"], 1)
            if k == 8:
                act.wait_ge(ev["lg_ready"], done(b))
                act.activation(ex[:], lg[:], ACT.Exp).then_inc(ev["ex_ready"], 1)
            if k == 10:
                act.wait_ge(ev["qn_ready"], done(b))
                for i in range(3):
                    last = act.activation(ew[:, i, :], qn[:, i, 0:EXPERTS], ACT.Exp, scale=-1.0, bias=srec[:, i:i + 1])
                last.then_inc(ev["ew_ready"], 1)
            if k == 14:
                act.wait_ge(ev["comb_flipped"], done(b))
                act.activation(tokens(comb, b), post[0][:, 0:T], ACT.Copy, scale=CSCALE).then_inc(ev["comb_hi_ready"], 1)

        def post_vector(dve, b, k):
            q = parity(b)
            b = turn(b)
            if k == 0:
                dve.wait_ge(ev["ysum_ready"], done(b))
                for h in range(HALVES):
                    last = dve.scalar_tensor_tensor(out=yb[:, h, :], in0=xc[q][:, h, :], scalar=vec[:, 2, h:h + 1],
                                                    in1=ysum[h][:, 0:T], op0=ALU.mult, op1=ALU.add)
                last.then_inc(ev["y_ready2"], 1)
            if k == 1:
                dve.wait_ge(ev["mean2"], done(b))
                dve.tensor_tensor(cen2[:], yz[:], over_halves(post[0][:, 0:T]), ALU.subtract).then_inc(ev["cen2_ready"], 1)
            if k == 2:
                dve.wait_ge(ev["yn_ready"], done(b - 1))
                rsqrt_vector(dve, 2, b, post[1][:, 0:T], rs2)
            if k == 4:
                dve.wait_ge(ev["proj_ready"], done(b))
                dve.scalar_tensor_tensor(out=tokens(hT, b), in0=post[0][:, 0:T], scalar=out_bias[:, 0:1],
                                         in1=tokens(hT, b), op0=ALU.add, op1=ALU.add).then_inc(ev["h_ready"], 1)
            if k == 5:
                dve.wait_ge(ev["mean3"], done(b))
                dve.tensor_tensor(cen3[:], tokens(hT, b), post[1][:, 0:T], ALU.subtract).then_inc(ev["cen3_ready"], 1)
            if k == 6:
                rsqrt_vector(dve, 3, b, post[0][:, 0:T], rs3)
                dve.wait_ge(ev["rs3_ready"], done(b))
                dve.wait_ge(ev["logits_ready"], done(b - 1))
                dve.tensor_tensor(xn3[:], cen3[:], rs3[:], ALU.mult).then_inc(ev["xn3_ready"], 1)
            if k == 7:
                dve.wait_ge(ev["xhi_ready"], done(b))
                dve.scalar_tensor_tensor(out=tokens(x_lo, b), in0=xn3[:], scalar=XSCALE, in1=tokens(x_hi, b),
                                         op0=ALU.mult, op1=ALU.subtract).then_inc(ev["xlo_ready"], 1)
            if k == 8:
                dve.wait_ge(ev["logits_ready"], done(b))
                logits = post[1][:, 0:3 * EXPERTS].rearrange("p (i e) -> p i e", e=EXPERTS)
                dve.tensor_reduce(top[:], logits, AX.X, ALU.max).then_inc(ev["top_ready"], 1)
                dve.wait_ge(ev["top_ready"], done(b))
                dve.tensor_tensor(lg[:], logits, over_experts(top[:]), ALU.subtract).then_inc(ev["lg_ready"], 1)
            if k == 9:
                dve.wait_ge(ev["ex_ready"], done(b))
                dve.tensor_reduce(ssum[:], ex[:], AX.X, ALU.add).then_inc(ev["ssum_ready"], 1)
                dve.wait_ge(ev["ssum_ready"], done(b))
                dve.wait_ge(ev["ew_ready"], done(b - 1))
                dve.reciprocal(wrec[:], ssum[:]).then_inc(ev["srec_ready"], 1)
                dve.wait_ge(ev["srec_ready"], done(b))
                dve.tensor_scalar(srec[:], wrec[:], -1.0, None, ALU.mult).then_inc(ev["nsrec_ready"], 1)
                dve.wait_ge(ev["nsrec_ready"], done(b))
                dve.tensor_tensor(qn[:, :, 0:EXPERTS], ex[:], over_experts(srec[:]), ALU.mult)
                dve.memset(qn[:, :, EXPERTS:QCOLS], 1.0).then_inc(ev["qn_ready"], 1)
            if k == 11:
                for r in range(ROUNDS):
                    if r == 0:
                        wait_apart(dve, "ew_ready", done(b))
                    else:
                        wait_apart(dve, "low_dropped", done(ROUNDS * b + r - 1))
                    for i in range(3):
                        last = dve.max(low8[:, i, :], qn[:, i, :])
                    last.then_inc(ev["low_found"], 1)
                    wait_apart(dve, "low_found", done(ROUNDS * b + r))
                    for i in range(3):
                        last = dve.match_replace(qn[:, i, :], low8[:, i, :], qn[:, i, :], -5.0)
                    last.then_inc(ev["low_dropped"], 1)
            if k == 12:
                dve.wait_ge(ev["low_dropped"], done(ROUNDS * b + ROUNDS - 1))
                dve.scalar_tensor_tensor(out=wm[:], in0=qn[:, :, 0:EXPERTS], scalar=-2.0, in1=ew[:],
                                         op0=ALU.is_gt, op1=ALU.mult).then_inc(ev["wm_ready"], 1)
                dve.wait_ge(ev["wm_ready"], done(b))
                dve.tensor_reduce(wsum[:], wm[:], AX.X, ALU.add).then_inc(ev["wsum_ready"], 1)
                dve.wait_ge(ev["wsum_ready"], done(b))
                dve.reciprocal(wrec[:], wsum[:]).then_inc(ev["wrec_ready"], 1)
                dve.wait_ge(ev["wrec_ready"], done(b))
                dve.wait_ge(ev["comb_flipped"], done(b - 1))
                for a in range(2):
                    last = dve.tensor_tensor(cw[:, :, a, :], wm[:], over_experts(wrec[:]), ALU.mult)
                last.then_inc(ev["cw_ready"], 1)
            if k == 14:
                dve.wait_ge(ev["comb_hi_ready"], done(b))
                low = tokens(comb, b, parts=slice(EXPERTS, P))
                dve.scalar_tensor_tensor(out=low, in0=post[0][EXPERTS:P, 0:T], scalar=CSCALE, in1=low,
                                         op0=ALU.mult, op1=ALU.subtract).then_inc(ev["comb_ready"], 1)

        def post_gpsimd(pool, b, k):
            q = parity(b)
            b = turn(b)
            if k == 0:
                pool.wait_ge(ev["y_ready2"], done(b))
                pool.tensor_tensor(yz[:], yb[:], zg[q][:], ALU.mult).then_inc(ev["gated"], 1)
            if k == 3:
                pool.wait_ge(ev["rs2_ready"], done(b))
                pool.tensor_tensor(yn[:], cen2[:], over_halves(rs2[:]), ALU.mult).then_inc(ev["yn_ready"], 1)

        def turn(b):
            return b[0]

        def parity(b):
            return b[1]

        def steps(eng, pre_stage, scan_stage, post_stage, b, with_pre=True, with_post=True):
            t, q = b
            for k in range(NS):
                scan_stage(eng, b, k)
                if with_post:
                    post_stage(eng, (t - 1, 1 - q), k)
                if with_pre:
                    pre_stage(eng, (t + 1, 1 - q), k)
            if scan_stage is scan_tensor:
                sum_states(eng, b, NS - 1)

        def alone(eng, stage, b):
            for k in range(NS):
                stage(eng, b, k)

        def run(eng, pre_stage, scan_stage, post_stage):
            alone(eng, pre_stage, (0, 0))
            steps(eng, pre_stage, scan_stage, post_stage, (0, 0), with_post=False)
            with eng.Fori(0, SEQS // 2 - 1) as i:
                steps(eng, pre_stage, scan_stage, post_stage, (2 * i + 1, 1))
                steps(eng, pre_stage, scan_stage, post_stage, (2 * i + 2, 0))
            steps(eng, pre_stage, scan_stage, post_stage, (SEQS - 1, 1), with_pre=False)
            alone(eng, post_stage, (SEQS - 1, 1))

        def start(eng, events):
            for name in events:
                eng.sem_inc(ev[name], BIAS)

        block = ctx.enter_context(nc.Block())
        N_WEIGHTS = 13

        @block.sync
        def _(sp):
            loads = [
                (in_rows[:], in_w.rearrange("(n p) d -> p n d", p=P)),
                (xp_rows[:], xproj_w),
                (out_rows[:], out_w),
                (a_raw[:], a_log.rearrange("(h p) s -> p h s", p=P)),
                (taps[:], conv_w.rearrange("(h p) a k -> p h (a k)", p=P)),
                (vec[:, 0, :], conv_b),
                (vec[:, 1, :], dt_b),
                (vec[:, 2, :], d_par),
                (vec[:, 3, :], ln_g),
                (vec[:, 4, :], ln_b),
                (dt_row[:], dt_w),
                (rw[:], router_w),
                (rb[:], router_b.rearrange("(a e) -> a e", a=1)),
            ]
            assert len(loads) == N_WEIGHTS
            for dst, src in loads:
                sp.dma_start(dst, src).then_inc(weights_in, 16)

        LOADED = 16 * N_WEIGHTS

        @block.gpsimd
        def _(pool):
            start(pool, pool_events)
            pool.memset(ones_inner[:], 1.0 / INNER).then_inc(inner_ready, 1)
            pool.memset(ones_row[:], 1.0).then_inc(row_ready, 1)
            pool.memset(pick_raw[:], 0.0).then_inc(pick_zeroed, 1)
            for i in range(3):
                pool.wait_ge(pick_zeroed if i == 0 else pick_made, max(i, 1))
                pool.affine_select(out=pick_raw[:], in_=pick_raw[:], compare_op=ALU.not_equal, fill=1.0,
                                   base=-32 * (i + 1), pattern=[[-1, 2 * STATES]], channel_multiplier=1
                                   ).then_inc(pick_made, 1)
            pool.wait_ge(pick_made, 3)
            pool.tensor_copy(pick[:], pick_raw[:]).then_inc(pick_ready, 1)
            pool.memset(eps[:], EPS).then_inc(eps_ready, 1)
            pool.memset(xpad[:, :, 0:1], 0.0).then_inc(zero_ready, 1)
            pool.memset(xpad[:, :, T + 1:T + 2], 0.0).then_inc(zero_ready, 1)
            for i in range(2):
                pool.memset(dA[i][:, :, 0:1], 0.0).then_inc(zero_ready, 1)
            run(pool, pre_gpsimd, scan_gpsimd, post_gpsimd)

        @block.tensor
        def _(pe):
            start(pe, pe_events)
            pe.wait_ge(weights_in, LOADED)
            for n in range(4):
                last = pe.transpose(pre[0][:, n * P:(n + 1) * P], in_rows[:, n, :], ident[:])
            last.then_inc(in_flipped, 1)
            NX = 1 + 2 * STATES
            for h in range(HALVES):
                last = pe.transpose(pre[1][:, h * P:h * P + NX], xp_rows[:, h * P:(h + 1) * P], ident[0:NX, 0:NX])
            last.then_inc(xp_flipped, 1)
            for h in range(HALVES):
                last = pe.transpose(post[0][:, h * P:(h + 1) * P], out_rows[:, h * P:(h + 1) * P], ident[:])
            last.then_inc(out_flipped, 1)
            pe.wait_ge(out_copied, 1)
            for h in range(HALVES):
                last = pe.matmul(post[1][:, 0:1], out_T[:, h, :], vec[:, 4, h:h + 1], start=(h == 0), stop=(h == 1))
            last.then_inc(bias_summed, 1)
            pe.wait_ge(in_copied, 1)
            pe.wait_ge(xp_copied, 1)
            pe.wait_ge(out_copied, 2)
            pe.wait_ge(bias_ready, 1)
            pe.wait_ge(inner_ready, 1)
            pe.wait_ge(row_ready, 1)
            pe.wait_ge(pick_ready, 1)
            run(pe, pre_tensor, scan_tensor, post_tensor)

        @block.scalar
        def _(act):
            start(act, act_events)
            act.wait_ge(weights_in, LOADED)
            act.wait_ge(a_capped_ready, 1)
            act.activation(a_exp[:], a_capped[:], ACT.Exp).then_inc(a_exp_ready, 1)
            act.wait_ge(in_flipped, 1)
            act.copy(in_T[:], pre[0][:].rearrange("p (n e) -> p n e", e=P)).then_inc(in_copied, 1)
            act.wait_ge(a_neg_ready, 1)
            act.wait_ge(zero_ready, 4)
            act.wait_ge(eps_ready, 1)
            run(act, pre_scalar, scan_scalar, post_scalar)

        @block.vector
        def _(dve):
            start(dve, dve_events)
            dve.wait_ge(weights_in, LOADED)
            dve.tensor_scalar(a_capped[:], a_raw[:], A_LOG_CAP, None, ALU.min).then_inc(a_capped_ready, 1)
            dve.wait_ge(a_exp_ready, 1)
            dve.tensor_scalar(a_neg[:], a_exp[:], -1.0, None, ALU.mult).then_inc(a_neg_ready, 1)
            dve.memset(xp_T[:], 0.0).then_inc(xp_zeroed, 1)
            dve.wait_ge(xp_zeroed, 1)
            dve.wait_ge(xp_flipped, 1)
            for h in range(HALVES):
                dve.tensor_copy(xp_T[:, h, 0:1], pre[1][:, h * P:h * P + 1])
                for g in range(1, 4):
                    last = dve.tensor_copy(xp_T[:, h, 32 * g:32 * (g + 1)], pre[1][:, h * P + 1:h * P + 1 + 2 * STATES])
            last.then_inc(xp_copied, 1)
            dve.wait_ge(out_flipped, 1)
            dve.tensor_copy(out_T[:], post[0][:, 0:HALVES * P].rearrange("p (h d) -> p h d", d=P)).then_inc(out_copied, 1)
            dve.wait_ge(out_copied, 1)
            for h in range(HALVES):
                last = dve.tensor_scalar(out_gT[:, h, :], out_T[:, h, :], vec[:, 3, h:h + 1], None, ALU.mult)
            last.then_inc(out_copied, 1)
            dve.wait_ge(bias_summed, 1)
            dve.tensor_copy(out_bias[:], post[1][:, 0:1]).then_inc(bias_ready, 1)
            dve.wait_ge(bias_ready, 1)
            dve.wait_ge(zero_ready, 4)
            run(dve, pre_vector, scan_vector, post_vector)


def experts(nc, hT, ident, x_hi, x_lo, comb, w1, b1, w2, b2, out):
    sems = []
    with ExitStack() as ctx:
        ctx.callback(clear, nc, sems)

        def sb(name, shape, dt=F32):
            return ctx.enter_context(nc.sbuf_tensor(name, shape, dt))

        def bank(name):
            return ctx.enter_context(nc.psum_tensor(name, [P, 512], F32))

        PAIR = 2
        COLS = HIDDEN + HALVES * DIM

        w_hi = sb("w_hi", [P, EXPERTS * COLS], F16)
        w_lo = sb("w_lo", [P, EXPERTS * COLS], F16)
        stage = [sb(f"stage{i}", [P, PAIR * COLS]) for i in range(2)]
        b1_rows = sb("b1_rows", [P, P])
        b1_T = sb("b1_T", [P, P])
        b2_in = sb("b2_in", [P, DIM])
        b2_hi, b2_lo = sb("b2_hi", [P, DIM], F16), sb("b2_lo", [P, DIM], F16)
        sel_raw = sb("sel_raw", [P, EXPERTS])
        sel = sb("sel", [P, EXPERTS], F16)
        g = [sb(f"g{i}", [P, HALVES, T]) for i in range(2)]
        m = [sb(f"m{i}", [P, HALVES, T]) for i in range(2)]
        m_hi = [sb(f"m_hi{i}", [P, HALVES, T], F16) for i in range(4)]
        m_lo = [sb(f"m_lo{i}", [P, HALVES, T], F16) for i in range(4)]
        o_T = sb("o_T", [P, T])
        o_rows = sb("o_rows", [P, 3, P])

        up_bank = [bank(f"up{i}") for i in range(HALVES)]
        cast = [bank(f"cast{i}") for i in range(2)]
        y = bank("y")
        turned = bank("turned")

        def sem(name):
            sems.append(ctx.enter_context(nc.semaphore(name)))
            return sems[-1]

        small_in = sem("small_in")
        stage_in = [sem(f"stage{i}_in") for i in range(2)]
        split_hi, split_lo = sem("split_hi"), sem("split_lo")
        sel_zeroed, sel_made, sel_ready = sem("sel_zeroed"), sem("sel_made"), sem("sel_ready")
        b1_flipped, b1_ready = sem("b1_flipped"), sem("b1_ready")
        b2_hi_ready, b2_ready = sem("b2_hi_ready"), sem("b2_ready")
        up_ready = [sem(f"up{h}_ready") for h in range(HALVES)]
        cast_ready, gelu_done, m_ready = sem("cast_ready"), sem("gelu_done"), sem("m_ready")
        hi_ready, down_done = sem("hi_ready"), sem("down_done")
        lo_ready = {"dve": sem("dve_lo_ready"), "pool": sem("pool_lo_ready")}
        y_summed, o_ready, o_flipped, rows_ready, stored = (
            sem("y_summed"), sem("o_ready"), sem("o_flipped"), sem("rows_ready"), sem("stored"))

        LAG = 2
        QUAD = 4
        QUADS = EXPERTS // QUAD
        PAIRS_PER_QUAD = QUAD // PAIR
        LO_ON = ["dve", "pool", "dve", "pool"]
        STORES = 2

        def weight(buf, layer, e, h):
            even, odd = e
            return buf[:, bass.ds(even * COLS + (PAIR * layer + odd) * HIDDEN + h * P, P)]

        def tokens(buf, b):
            return buf[:, bass.ds(b * T, T)]

        def wait_lo(eng, quad, j, back=0):
            who = LO_ON[j % QUAD]
            per = LO_ON.count(who)
            eng.wait_ge(lo_ready[who], done(per * (quad - back) + LO_ON[:j].count(who)))

        def up(pe, b, e, j):
            n = EXPERTS * b + e
            for h in range(HALVES):
                pe.wait_ge(gelu_done, done(2 * (n - 1) + h))
                w_h, w_l = (weight(w, 0, (e - j % PAIR, j % PAIR), h) for w in (w_hi, w_lo))
                pe.matmul(up_bank[h][:, 0:T], w_h, tokens(x_hi, b), start=True, stop=False)
                pe.matmul(up_bank[h][:, 0:T], w_h, tokens(x_lo, b), start=False, stop=False)
                pe.matmul(up_bank[h][:, 0:T], w_l, tokens(x_hi, b), start=False, stop=True).then_inc(up_ready[h], 1)
            pe.wait_ge(m_ready, done(n - 2))
            pe.matmul(cast[j % 2][:, 0:T], sel[:, bass.ds(e, 1)].broadcast_to([P, P]), tokens(comb, b),
                      start=True, stop=True).then_inc(cast_ready, 1)

        def down(pe, b, qd, j, last):
            n = EXPERTS * b + QUAD * qd + j
            pe.wait_ge(hi_ready, done(n))
            wait_lo(pe, QUADS * b + qd, j)
            for h in range(HALVES):
                w_h, w_l = (weight(w, 1, (QUAD * qd + j - j % PAIR, j % PAIR), h) for w in (w_hi, w_lo))
                pe.matmul(y[:, 0:T], w_h, m_hi[j][:, h, :], start=False, stop=False)
                pe.matmul(y[:, 0:T], w_h, m_lo[j][:, h, :], start=False, stop=False)
                mm = pe.matmul(y[:, 0:T], w_l, m_hi[j][:, h, :], start=False, stop=last and h == HALVES - 1)
            mm.then_inc(down_done, 1)
            if last:
                pe.wait_ge(down_done, done(n))
                pe.sem_inc(y_summed, 1)

        def tensor_quad(pe, b, qd, first, tail, end, between=None):
            for j in range(QUAD):
                ahead = j + LAG
                if ahead < QUAD or not tail:
                    if first:
                        pe.wait_ge(split_lo, PAIRS_PER_QUAD * qd + ahead // PAIR + 1)
                    up(pe, b, QUAD * qd + ahead, ahead)
                elif not end:
                    up(pe, b + 1, ahead - QUAD, ahead)
                down(pe, b, qd, j, tail and j == QUAD - 1)

        def tensor_start(pe, b):
            pe.wait_ge(o_ready, done(b - 1))
            pe.matmul(y[:, 0:T], b2_hi[:], tokens(comb, b), start=True, stop=False)
            pe.matmul(y[:, 0:T], b2_lo[:], tokens(comb, b), start=False, stop=False)

        def turn_back(pe, b):
            pe.wait_ge(o_ready, done(b))
            pe.wait_ge(rows_ready, done(b - 1))
            for i, (a, z) in enumerate(OUT_TILES):
                last = pe.transpose(turned[0:z, i * P:(i + 1) * P], o_T[:, a:a + z], ident[:])
            last.then_inc(o_flipped, 1)

        def gelu(act, b, e, j):
            n = EXPERTS * b + e
            act.wait_ge(m_ready, done(n - 2))
            for h in range(HALVES):
                act.wait_ge(up_ready[h], done(n))
                act.activation(g[j % 2][:, h, :], up_bank[h][:, 0:T], ACT.Gelu, scale=1 / (XSCALE * WSCALE),
                               bias=b1_T[:, bass.ds(HALVES * e + h, 1)]).then_inc(gelu_done, 1)

        def high(act, n, j):
            act.wait_ge(m_ready, done(n))
            act.wait_ge(down_done, done(n - QUAD))
            act.copy(m_hi[j][:], m[j % 2][:]).then_inc(hi_ready, 1)

        def split_low(dve, pair, i):
            dve.wait_ge(split_hi, pair + 1)
            cols = bass.ds(pair * PAIR * COLS, PAIR * COLS)
            dve.scalar_tensor_tensor(out=w_lo[:, cols], in0=stage[i][:], scalar=WSCALE,
                                     in1=w_hi[:, cols], op0=ALU.mult, op1=ALU.subtract).then_inc(split_lo, 1)

        def scalar_quad(act, b, qd, first, tail, end, between=None):
            for j in range(QUAD):
                n = EXPERTS * b + QUAD * qd + j
                gelu(act, b, QUAD * qd + j, j)
                if not (first and isinstance(qd, int) and qd == 0 and j == 0):
                    high(act, n - 1, (j - 1) % QUAD)
                if first and not tail and j % PAIR == 0:
                    i = j // PAIR
                    act.wait_ge(stage_in[i], 32 * (qd + 2))
                    split_high_cols(act, PAIRS_PER_QUAD * (qd + 1) + i, i)
                if between and j == 1:
                    between()
            if end:
                high(act, n, QUAD - 1)

        def split_high_cols(act, pair, i):
            act.activation(w_hi[:, bass.ds(pair * PAIR * COLS, PAIR * COLS)],
                           stage[i][:], ACT.Copy, scale=WSCALE).then_inc(split_hi, 1)

        def weigh(dve, b, qd, j):
            n = EXPERTS * b + QUAD * qd + j
            dve.wait_ge(gelu_done, done(2 * n + 1))
            dve.wait_ge(cast_ready, done(n))
            dve.wait_ge(hi_ready, done(n - 2))
            if j >= 2:
                wait_lo(dve, QUADS * b + qd, j - 2)
            else:
                wait_lo(dve, QUADS * b + qd, j + 2, back=1)
            dve.tensor_tensor(m[j % 2][:], g[j % 2][:],
                              cast[j % 2][:, 0:T].unsqueeze(1).broadcast_to([P, HALVES, T]), ALU.mult).then_inc(m_ready, 1)

        def low(eng, n, j):
            eng.wait_ge(hi_ready, done(n))
            eng.wait_ge(down_done, done(n - QUAD))
            eng.tensor_tensor(m_lo[j][:], m[j % 2][:], m_hi[j][:], ALU.subtract).then_inc(lo_ready[LO_ON[j]], 1)

        def vector_quad(dve, b, qd, first, tail, end, between=None):
            for j in range(QUAD):
                n = EXPERTS * b + QUAD * qd + j
                weigh(dve, b, qd, j)
                if LO_ON[(j - 1) % QUAD] == "dve" and not (first and isinstance(qd, int) and qd == 0 and j == 0):
                    low(dve, n - 1, (j - 1) % QUAD)
                if first and not tail and j % PAIR == 0:
                    split_low(dve, PAIRS_PER_QUAD * (qd + 1) + j // PAIR, j // PAIR)
                if between and j == 1:
                    between()
            if end and LO_ON[QUAD - 1] == "dve":
                low(dve, n, QUAD - 1)

        def gpsimd_quad(pool, b, qd, first, tail, end, between=None):
            for j in range(QUAD):
                if LO_ON[j] == "pool":
                    low(pool, EXPERTS * b + QUAD * qd + j, j)

        def sequence(eng, quad, b, first=False, end=False, between=None):
            quad(eng, b, 0, first, False, False, between)
            with eng.Fori(1, QUADS - 1) as qd:
                quad(eng, b, qd, first, False, False)
            quad(eng, b, QUADS - 1, first, True, end)

        def load_pair(sp, pair, i):
            ups = stage[i][:, 0:PAIR * HIDDEN].rearrange("p (e n) -> p e n", n=HIDDEN)
            downs = stage[i][:, PAIR * HIDDEN:PAIR * COLS].rearrange("p (c d) -> p c d", d=DIM)
            sp.dma_start(ups, w1.rearrange("e p n -> p e n")[:, bass.ds(pair * PAIR, PAIR), :]).then_inc(stage_in[i], 16)
            sp.dma_start(downs, w2.rearrange("e (h p) d -> p (e h) d", p=P)[:, bass.ds(pair * PAIR * HALVES, PAIR * HALVES), :]
                         ).then_inc(stage_in[i], 16)

        block = ctx.enter_context(nc.Block())

        @block.sync
        def _(sp):
            sp.sem_inc(stored, BIAS)
            for i in range(PAIRS_PER_QUAD):
                load_pair(sp, i, i)
            sp.dma_start(b1_rows[:], b1.rearrange("e (h p) -> (e h) p", p=P)).then_inc(small_in, 16)
            for i in range(2):
                sp.dma_start(b2_in[i * EXPERTS:(i + 1) * EXPERTS, :], b2).then_inc(small_in, 16)
            with sp.Fori(1, QUADS) as qd:
                for i in range(PAIRS_PER_QUAD):
                    sp.wait_ge(split_lo, PAIRS_PER_QUAD * (qd - 1) + i + 1)
                    load_pair(sp, PAIRS_PER_QUAD * qd + i, i)
            rows = out.rearrange("b t d -> (b t) d")
            with sp.Fori(0, SEQS) as b:
                sp.wait_ge(rows_ready, done(b))
                sp.dma_start(rows[bass.ds(b * T, 2 * P), :].rearrange("(n p) d -> p n d", p=P), o_rows[:, 0:2, :]
                             ).then_inc(stored, 16)
                sp.dma_start(rows[bass.ds(b * T + 2 * P, T - 2 * P), :], o_rows[0:T - 2 * P, 2, :]).then_inc(stored, 16)
            sp.wait_ge(stored, 16 * STORES * SEQS + BIAS)

        @block.gpsimd
        def _(pool):
            pool.sem_inc(lo_ready["pool"], BIAS)
            pool.memset(sel_raw[:], 0.0).then_inc(sel_zeroed, 1)
            for i in range(2):
                pool.wait_ge(sel_zeroed if i == 0 else sel_made, 1)
                pool.affine_select(out=sel_raw[:], in_=sel_raw[:], compare_op=ALU.not_equal, fill=SELSCALE,
                                   base=-(EXPERTS - 1) - EXPERTS * i, pattern=[[1, EXPERTS]], channel_multiplier=1
                                   ).then_inc(sel_made, 1)
            pool.wait_ge(sel_made, 2)
            pool.tensor_copy(sel[:], sel_raw[:]).then_inc(sel_ready, 1)
            sequence(pool, gpsimd_quad, 0, first=True)
            with pool.Fori(1, SEQS - 1) as b:
                sequence(pool, gpsimd_quad, b)
            sequence(pool, gpsimd_quad, SEQS - 1, end=True)

        @block.tensor
        def _(pe):
            for s in (*up_ready, cast_ready, down_done, y_summed, o_flipped):
                pe.sem_inc(s, BIAS)
            pe.wait_ge(small_in, 48)
            pe.transpose(turned[:, 0:P], b1_rows[:], ident[:]).then_inc(b1_flipped, 1)
            pe.wait_ge(sel_ready, 1)
            pe.wait_ge(b2_ready, 1)
            pe.wait_ge(split_lo, 1)
            for e in range(LAG):
                up(pe, 0, e, e)
            tensor_start(pe, 0)
            sequence(pe, tensor_quad, 0, first=True)
            with pe.Fori(1, SEQS - 1) as b:
                tensor_start(pe, b)
                turn_back(pe, b - 1)
                sequence(pe, tensor_quad, b)
            tensor_start(pe, SEQS - 1)
            turn_back(pe, SEQS - 2)
            sequence(pe, tensor_quad, SEQS - 1, end=True)
            turn_back(pe, SEQS - 1)

        @block.scalar
        def _(act):
            def copy_rows(b):
                act.wait_ge(o_flipped, done(b))
                act.wait_ge(stored, 16 * STORES * b + BIAS)
                act.copy(o_rows[:, 0:2, :], turned[:, 0:2 * P].rearrange("p (n d) -> p n d", d=P))
                act.copy(o_rows[0:T - 2 * P, 2, :], turned[0:T - 2 * P, 2 * P:3 * P]).then_inc(rows_ready, 1)

            for s in (gelu_done, hi_ready, rows_ready):
                act.sem_inc(s, BIAS)
            for i in range(PAIRS_PER_QUAD):
                act.wait_ge(stage_in[i], 32)
                split_high_cols(act, i, i)
            act.wait_ge(b1_flipped, 1)
            act.copy(b1_T[:], turned[:, 0:P]).then_inc(b1_ready, 1)
            act.wait_ge(small_in, 48)
            act.copy(b2_hi[:], b2_in[:]).then_inc(b2_hi_ready, 1)
            act.wait_ge(b1_ready, 1)
            sequence(act, scalar_quad, 0, first=True)
            with act.Fori(1, SEQS - 1) as b:
                sequence(act, scalar_quad, b, between=lambda: copy_rows(b - 1))
            sequence(act, scalar_quad, SEQS - 1, end=True, between=lambda: copy_rows(SEQS - 2))
            copy_rows(SEQS - 1)

        @block.vector
        def _(dve):
            def add_up(b):
                dve.wait_ge(y_summed, done(b))
                dve.wait_ge(o_flipped, done(b - 1))
                dve.scalar_tensor_tensor(out=o_T[:], in0=y[:, 0:T], scalar=1 / CSCALE, in1=tokens(hT, b),
                                         op0=ALU.mult, op1=ALU.add).then_inc(o_ready, 1)

            for s in (m_ready, lo_ready["dve"], o_ready):
                dve.sem_inc(s, BIAS)
            for i in range(PAIRS_PER_QUAD):
                split_low(dve, i, i)
            dve.wait_ge(b2_hi_ready, 1)
            dve.tensor_tensor(b2_lo[:], b2_in[:], b2_hi[:], ALU.subtract).then_inc(b2_ready, 1)
            sequence(dve, vector_quad, 0, first=True)
            with dve.Fori(1, SEQS - 1) as b:
                sequence(dve, vector_quad, b, between=lambda: add_up(b - 1))
            sequence(dve, vector_quad, SEQS - 1, end=True, between=lambda: add_up(SEQS - 2))
            add_up(SEQS - 1)


_INS = ["x", "L0_tok_W", "L0_tok_b", "L0_tok_gamma", "L0_tok_beta", "L0_attn_in_proj_w", "L0_attn_x_proj_w",
        "L0_attn_dt_w", "L0_attn_dt_b", "L0_attn_conv_w", "L0_attn_conv_b", "L0_attn_A_log", "L0_attn_D_param",
        "L0_attn_out_w", "L0_attn_ln_g", "L0_attn_ln_b", "L0_ffn_w1", "L0_ffn_b1", "L0_ffn_w2", "L0_ffn_b2",
        "L0_ffn_router_w", "L0_ffn_router_b"]

_COLUMNS = ["L0_tok_b", "L0_tok_gamma", "L0_tok_beta", "L0_attn_dt_b", "L0_attn_conv_b", "L0_attn_D_param",
            "L0_attn_ln_g", "L0_attn_ln_b"]


def kernel(**inputs):
    import concourse.bacc as _bacc
    from concourse.bass_utils import run_bass_kernel_spmd as _run

    nc = _bacc.Bacc("TRN2", target_bir_lowering=False, num_devices=1)
    arrays, args = {}, []
    for name in _INS:
        a = np.ascontiguousarray(inputs[name])
        if name in ("L0_ffn_router_w", "L0_ffn_router_b", "L0_ffn_b2"):
            axis = 0 if name == "L0_ffn_b2" else a.ndim - 1
            a = np.ascontiguousarray(np.flip(a, axis=axis))
        if name in _COLUMNS:
            a = np.ascontiguousarray(a.reshape(-1, P).T)
        if name == "L0_attn_dt_w":
            a = a.reshape(1, -1)
        arrays[f"in_{name}_dram"] = a
        args.append(nc.dram_tensor(f"in_{name}_dram", a.shape, mybir.dt.from_np(a.dtype), kind="ExternalInput").ap())
    result = nc.dram_tensor("out_0_dram", (SEQS, T, DIM), F32, kind="ExternalOutput").ap()
    build(nc, *args, result)
    r = _run(nc, [arrays], core_ids=[0])
    return r.results[0]["out_0_dram"]
```

```python
from contextlib import ExitStack

import numpy as np

import concourse.bass as bass
from concourse import mybir

F32 = mybir.dt.float32
F16 = mybir.dt.float16
BF16 = mybir.dt.bfloat16
ALU = mybir.AluOpType
ACT = mybir.ActivationFunctionType
AX = mybir.AxisListType

P = 128
SEQS, FRAMES, DIM = 8, 375, 128
TAPS = 5
T = FRAMES - TAPS + 1
TOKENS = SEQS * T
INNER, HALVES = 256, 2
STATES = 16
EXPERTS, HIDDEN, TOPK = 64, 256, 42
EPS = 1e-5
BIAS = 4
A_LOG_CAP = 84.0

ROWS = SEQS * FRAMES
ROW_TILES = -(-ROWS // P)
LAST_ROWS = ROWS - (ROW_TILES - 1) * P

ROUTE_AT = [0, P, T - P]
OUT_TILES = [(0, P), (P, P), (2 * P, T - 2 * P)]
ROUNDS = -(-(EXPERTS - TOPK) // 8)
SENTINELS = 8 * ROUNDS - (EXPERTS - TOPK)
QCOLS = EXPERTS + SENTINELS

XSCALE, WSCALE = 16.0, 16.0
CSCALE = 1024.0
SELSCALE = 1.0 / 16.0
MSCALE = CSCALE * SELSCALE

def _series():
    f = lambda v: 2 * np.arctanh(np.sqrt(v + 1e-30)) / np.sqrt(v + 1e-30)
    c = np.polynomial.chebyshev.Chebyshev.interpolate(f, 4, domain=[0, 1 / 9])
    return [float(a) for a in c.convert(kind=np.polynomial.Polynomial).coef]


SERIES = _series()


def done(turn):
    return turn + 1 + BIAS


def build(nc, x, tok_w, tok_b, gamma, beta, in_w, xproj_w, dt_w, dt_b, conv_w, conv_b, a_log, d_par,
          out_w, ln_g, ln_b, w1, b1, w2, b2, router_w, router_b, out):
    with ExitStack() as kept:
        def keep(name, shape, dt=F32):
            return kept.enter_context(nc.sbuf_tensor(name, shape, dt))

        hT = keep("hT", [P, TOKENS])
        ident = keep("ident", [P, P])
        ones_ln = keep("ones_ln", [P, P])
        x_hi = keep("x_hi", [P, TOKENS], F16)
        x_lo = keep("x_lo", [P, TOKENS], F16)
        comb = keep("comb", [P, TOKENS], F16)
        front(nc, kept, hT, ident, ones_ln, x, tok_w, tok_b, gamma, beta)
        tower(nc, hT, ident, ones_ln, x_hi, x_lo, comb, in_w, xproj_w, dt_w, dt_b, conv_w, conv_b,
              a_log, d_par, out_w, ln_g, ln_b, router_w, router_b)
        experts(nc, hT, ident, x_hi, x_lo, comb, w1, b1, w2, b2, out)


def clear(nc, sems):
    nums = sorted(s.num for s in sems)
    first = nums[0]
    for at, num in enumerate(nums):
        if at + 1 == len(nums) or nums[at + 1] != num + 1:
            nc.gpsimd.sem_clear(range(first, num + 1))
            first = nums[min(at + 1, len(nums) - 1)]
    nc.all_engine_barrier()


def front(nc, kept, hT, ident, ones_ln, x, tok_w, tok_b, gamma, beta):
    sems = []
    with ExitStack() as ctx:
        ctx.callback(clear, nc, sems)

        def sb(name, shape, dt=F32):
            return ctx.enter_context(nc.sbuf_tensor(name, shape, dt))

        def sem(name):
            sems.append(ctx.enter_context(nc.semaphore(name)))
            return sems[-1]

        rows = sb("rows", [P, ROW_TILES, DIM])
        wrow = sb("wrow", [P, TAPS * DIM])
        xT = sb("xT", [P, ROW_TILES * P])
        wT = sb("wT", [P, TAPS, P])
        vecs = sb("vecs", [P, 3])
        stats = sb("stats", [P, SEQS, 6])
        mv = sb("mv", [P, 2])
        rstd = sb("rstd", [P, 1])
        gain = sb("gain", [P, 1])
        veps, lnv, r0, r0sq, newton = (sb(n, [P, 1]) for n in ("veps", "lnv", "r0", "r0sq", "newton"))
        flip = [ctx.enter_context(nc.psum_tensor(f"flip{i}", [P, 4, P], F32)) for i in range(2)]
        conv = [ctx.enter_context(nc.psum_tensor(f"conv{i}", [P, 512], F32)) for i in range(4)]

        x_in = [sem(f"x_in{i}") for i in range(4)]
        w_in, vecs_in = sem("w_in"), sem("vecs_in")
        zeroed, ident_ready, ones_ready = sem("zeroed"), sem("ident_ready"), sem("ones_ready")
        flipped, flip_copied = sem("flipped"), sem("flip_copied")
        conv_ready, y_ready, stats_ready = sem("conv_ready"), sem("y_ready"), sem("stats_ready")
        moments_ready, rstd_ready, gain_ready = sem("moments_ready"), sem("rstd_ready"), sem("gain_ready")
        veps_ready, ln_taken, r0_ready, r0_squared, newton_ready = (
            sem(n) for n in ("veps_ready", "ln_taken", "r0_ready", "r0_squared", "newton_ready"))
        scaled, normed = sem("scaled"), sem("normed")

        x_rows = x.rearrange("b t d -> (b t) d")
        GROUPS = -(-ROW_TILES // 4)
        WGROUPS = -(-TAPS // 4)
        load_tiles = [(0, 4), (4, 12), (12, ROW_TILES - 1)]

        block = ctx.enter_context(nc.Block())

        @block.sync
        def _(sp):
            sp.dma_start(wrow[:], tok_w).then_inc(w_in, 16)
            for i, (a, z) in enumerate(load_tiles):
                sp.dma_start(rows[:, a:z, :], x_rows[a * P:z * P, :].rearrange("(n p) d -> p n d", p=P)
                             ).then_inc(x_in[i], 16)
            sp.dma_start(rows[0:LAST_ROWS, ROW_TILES - 1, :], x_rows[(ROW_TILES - 1) * P:ROWS, :]).then_inc(x_in[3], 16)
            for i, v in enumerate((tok_b, gamma, beta)):
                sp.dma_start(vecs[:, i:i + 1], v).then_inc(vecs_in, 16)

        @block.gpsimd
        def _(pool):
            pool.memset(ident[:], 0.0).then_inc(zeroed, 1)
            pool.wait_ge(zeroed, 1)
            pool.affine_select(out=ident[:], in_=ident[:], compare_op=ALU.not_equal, fill=1.0, base=0,
                               pattern=[[-1, P]], channel_multiplier=1).then_inc(ident_ready, 1)
            pool.memset(ones_ln[:], 1.0 / DIM).then_inc(ones_ready, 1)

        @block.tensor
        def _(pe):
            pe.wait_ge(ident_ready, 1)
            pe.wait_ge(w_in, 16)
            for g in range(WGROUPS):
                for k in range(4 * g, min(4 * g + 4, TAPS)):
                    last = pe.transpose(flip[g % 2][:, k % 4, :], wrow[:, k * DIM:(k + 1) * DIM], ident[:])
                last.then_inc(flipped, 1)
            for g in range(GROUPS):
                pe.wait_ge(flip_copied, g + WGROUPS - 1)
                for n in range(4 * g, min(4 * g + 4, ROW_TILES)):
                    for i, (a, _z) in enumerate(load_tiles):
                        if n == a:
                            pe.wait_ge(x_in[i], 16)
                    if n < ROW_TILES - 1:
                        last = pe.transpose(flip[(g + WGROUPS) % 2][:, n % 4, :], rows[:, n, :], ident[:])
                    else:
                        pe.wait_ge(x_in[3], 16)
                        last = pe.transpose(flip[(g + WGROUPS) % 2][:, n % 4, 0:LAST_ROWS],
                                            rows[0:LAST_ROWS, n, :], ident[0:LAST_ROWS, 0:LAST_ROWS])
                last.then_inc(flipped, 1)
            for b in range(SEQS):
                need = -(-((b + 1) * FRAMES) // (4 * P))
                pe.wait_ge(flip_copied, WGROUPS + need)
                if b >= 4:
                    pe.wait_ge(y_ready, b - 3)
                for k in range(TAPS):
                    last = pe.matmul(conv[b % 4][:, 0:T], wT[:, k, :], xT[:, b * FRAMES + k:b * FRAMES + k + T],
                                     start=(k == 0), stop=(k == TAPS - 1))
                last.then_inc(conv_ready, 1)

        @block.scalar
        def _(act):
            for g in range(WGROUPS):
                n = min(4, TAPS - 4 * g)
                act.wait_ge(flipped, g + 1)
                act.copy(wT[:, 4 * g:4 * g + n, :], flip[g % 2][:, 0:n, :]).then_inc(flip_copied, 1)
            for g in range(GROUPS):
                act.wait_ge(flipped, g + 1 + WGROUPS)
                z = min(4 * P, ROWS - 4 * P * g)
                act.copy(xT[:, 4 * P * g:4 * P * g + z],
                         flip[(g + WGROUPS) % 2][:].rearrange("p a b -> p (a b)")[:, 0:z]).then_inc(flip_copied, 1)
            act.wait_ge(vecs_in, 48)
            for b in range(SEQS):
                act.wait_ge(conv_ready, b + 1)
                act.activation(hT[:, b * T:(b + 1) * T], conv[b % 4][:, 0:T], ACT.Identity,
                               bias=vecs[:, 0:1]).then_inc(y_ready, 1)
            act.wait_ge(veps_ready, 1)
            act.activation(lnv[:], veps[:], ACT.Ln).then_inc(ln_taken, 1)
            act.wait_ge(ln_taken, 1)
            act.activation(r0[:], lnv[:], ACT.Exp, scale=-0.5).then_inc(r0_ready, 1)
            act.wait_ge(r0_ready, 1)
            act.activation(r0sq[:], r0[:], ACT.Square).then_inc(r0_squared, 1)
            for b in range(SEQS):
                act.wait_ge(scaled, b + 1)
                act.activation(hT[:, b * T:(b + 1) * T], hT[:, b * T:(b + 1) * T], ACT.Relu,
                               bias=vecs[:, 2:3]).then_inc(normed, 1)

        @block.vector
        def _(dve):
            for b in range(SEQS):
                dve.wait_ge(y_ready, b + 1)
                dve.bn_stats(stats[:, b, :], hT[:, b * T:(b + 1) * T]).then_inc(stats_ready, 1)
            dve.wait_ge(stats_ready, SEQS)
            dve.bn_aggr(mv[:], stats[:].rearrange("p b s -> p (b s)")).then_inc(moments_ready, 1)
            dve.wait_ge(moments_ready, 1)
            dve.tensor_scalar(veps[:], mv[:, 1:2], EPS, None, ALU.add).then_inc(veps_ready, 1)
            dve.wait_ge(r0_squared, 1)
            dve.wait_ge(veps_ready, 1)
            dve.tensor_tensor(newton[:], r0sq[:], veps[:], ALU.mult).then_inc(newton_ready, 1)
            dve.wait_ge(newton_ready, 1)
            dve.tensor_scalar(newton[:], newton[:], -0.5, 1.5, ALU.mult, ALU.add).then_inc(newton_ready, 1)
            dve.wait_ge(newton_ready, 2)
            dve.tensor_tensor(rstd[:], newton[:], r0[:], ALU.mult).then_inc(rstd_ready, 1)
            dve.wait_ge(rstd_ready, 1)
            dve.wait_ge(vecs_in, 48)
            dve.tensor_tensor(gain[:], rstd[:], vecs[:, 1:2], ALU.mult).then_inc(gain_ready, 1)
            dve.wait_ge(gain_ready, 1)
            for b in range(SEQS):
                s = hT[:, b * T:(b + 1) * T]
                dve.tensor_scalar(s, s, mv[:, 0:1], gain[:, 0:1], ALU.subtract, ALU.mult).then_inc(scaled, 1)


def tower(nc, hT, ident, ones_ln, x_hi, x_lo, comb, in_w, xproj_w, dt_w, dt_b, conv_w, conv_b,
          a_log, d_par, out_w, ln_g, ln_b, router_w, router_b):
    sems = []
    with ExitStack() as ctx:
        ctx.callback(clear, nc, sems)

        def sb(name, shape, dt=F32):
            return ctx.enter_context(nc.sbuf_tensor(name, shape, dt))

        def bank(name, shape=(P, 512)):
            return ctx.enter_context(nc.psum_tensor(name, list(shape), F32))

        in_rows = sb("in_rows", [P, 4, DIM])
        xp_rows = sb("xp_rows", [1 + 2 * STATES, INNER])
        out_rows = sb("out_rows", [P, INNER])
        tap_rows = sb("tap_rows", [P, 3, HALVES, DIM])
        in_T = sb("in_T", [P, 3, HALVES, P])
        z_T = sb("z_T", [P, HALVES, P])
        xp_T = sb("xp_T", [P, HALVES, P])
        out_T = sb("out_T", [P, HALVES, P])
        out_gT = sb("out_gT", [P, HALVES, P])
        out_bias = sb("out_bias", [P, 1])
        a_raw = sb("a_raw", [P, HALVES, STATES])
        a_capped = sb("a_capped", [P, HALVES, STATES])
        a_exp = sb("a_exp", [P, HALVES, STATES])
        a_neg = sb("a_neg", [P, HALVES, STATES])
        taps = sb("taps", [P, HALVES, 3])
        vec = sb("vec", [P, 5, HALVES])
        dt_row = sb("dt_row", [1, INNER])
        rw = sb("rw", [P, EXPERTS])
        rb = sb("rb", [1, EXPERTS])
        ones_row = sb("ones_row", [1, P])
        ones_inner = sb("ones_inner", [P, P])
        pick_raw = sb("pick_raw", [P, 2 * STATES])
        pick = sb("pick", [P, 2 * STATES], BF16)

        cen1, sq1, rs1 = (sb(n, [P, T]) for n in ("cen1", "sq1", "rs1"))
        xn1 = sb("xn1", [P, T + 2])
        d_row = sb("d_row", [1, T])
        rest = sb("rest", [P, T])
        dt_pos, dt_abs, dt_exp, dt_ln, dt_rec, dt_s, dt_s2, dt_poly = (
            sb(n, [P, HALVES, T])
            for n in ("dt_pos", "dt_abs", "dt_exp", "dt_ln", "dt_rec", "dt_s", "dt_s2", "dt_poly"))
        xc = [sb(f"xc{i}", [P, HALVES, T]) for i in range(2)]
        zg = [sb(f"zg{i}", [P, HALVES, T]) for i in range(2)]
        bc = [sb(f"bc{i}", [P, T], BF16) for i in range(2)]
        delta = [sb(f"delta{i}", [P, HALVES, T]) for i in range(2)]
        dx = [sb(f"dx{i}", [P, HALVES, T]) for i in range(2)]
        DEEP, AHEAD, LAG = 4, 2, 2
        dA = [sb(f"dA{i}", [P, HALVES, T]) for i in range(DEEP)]
        bx = [sb(f"bx{i}", [P, HALVES, T]) for i in range(2)]
        hs = [sb(f"hs{i}", [P, HALVES, T]) for i in range(DEEP)]
        cs = [sb(f"cs{i}", [P, T]) for i in range(DEEP)]
        hc = [sb(f"hc{i}", [P, HALVES, T]) for i in range(DEEP)]
        yb, yz, cen2, sq2, yn = (sb(n, [P, HALVES, T]) for n in ("yb", "yz", "cen2", "sq2", "yn"))
        rs2, cen3, sq3, rs3, xn3 = (sb(n, [P, T]) for n in ("rs2", "cen3", "sq3", "rs3", "xn3"))
        eps, two = sb("eps", [P, 1]), sb("two", [P, 1])
        lnv, r0, r0sq, newton = ([sb(f"{n}{i}", [P, T]) for i in range(4)] for n in ("lnv", "r0_", "r0sq", "newton"))
        top, ssum, srec, wsum, wrec = (sb(n, [P, 3]) for n in ("top", "ssum", "srec", "wsum", "wrec"))
        lg, ex, ew, wm = (sb(n, [P, 3, EXPERTS]) for n in ("lg", "ex", "ew", "wm"))
        qn = sb("qn", [P, 3, QCOLS])
        low8 = sb("low8", [P, 3, 8])
        cw = sb("cw", [P, 3, 2, EXPERTS])

        bank_b, bank_c = bank("bank_b"), bank("bank_c")
        ysum = [bank(f"ysum{i}") for i in range(HALVES)]
        pre = [bank(f"pre{i}") for i in range(2)]
        post = [bank(f"post{i}") for i in range(2)]

        def sem(name):
            sems.append(ctx.enter_context(nc.semaphore(name)))
            return sems[-1]

        weights_in = sem("weights_in")
        xp_zeroed, inner_ready, row_ready, pick_zeroed, pick_made, pick_ready = (
            sem(n) for n in ("xp_zeroed", "inner_ready", "row_ready", "pick_zeroed", "pick_made", "pick_ready"))
        tap_rows_ready = sem("tap_rows_ready")
        eps_ready, waited = sem("eps_ready"), sem("waited")
        zero_ready, a_capped_ready, a_exp_ready, a_neg_ready = (
            sem(n) for n in ("zero_ready", "a_capped_ready", "a_exp_ready", "a_neg_ready"))
        in_flipped, xp_flipped, out_flipped = sem("in_flipped"), sem("xp_flipped"), sem("out_flipped")
        in_copied, xp_copied, out_copied = sem("in_copied"), sem("xp_copied"), sem("out_copied")
        bias_summed, bias_ready = sem("bias_summed"), sem("bias_ready")
        pe_events = {n: sem(n) for n in (
            "mean1", "var1", "xin_ready", "z_ready", "dbc_ready", "dt_ready", "b_cast", "c_cast",
            "summed", "ysum_ready", "mean2", "var2", "proj_ready", "mean3", "var3", "logits_ready",
            "comb_flipped")}
        act_events = {n: sem(n) for n in (
            "sq1_ready", "xc_ready", "zg_ready", "drow_ready", "dtabs_ready", "dtexp_ready", "dtln_ready",
            "dtrec_ready", "dts2_ready", "dA_ready", "c_copied", "sq2_ready", "sq3_ready", "xhi_ready", "ex_ready",
            "ew_ready", "comb_hi_ready", "bc_hi_ready", "bc_mid_ready",
            *(f"{n}{i}" for n in ("ln_taken", "r0_ready", "r0_squared") for i in (1, 2, 3)))}
        dve_events = {n: sem(n) for n in (
            "cen1_ready", "rs1_ready", "xn1_ready", "rest_ready", "poly_done", "delta_ready", "bx_ready", "scan_done",
            "y_ready2", "cen2_ready", "rs2_ready", "h_ready", "cen3_ready", "rs3_ready", "xn3_ready",
            "xlo_ready", "top_ready", "lg_ready", "ssum_ready", "srec_ready", "nsrec_ready", "qn_ready",
            "low_found", "low_dropped", "wm_ready", "wsum_ready", "wrec_ready", "bc_ready", "cw_ready", "comb_ready",
            *(f"vr_ready{i}" for i in (1, 2, 3)))}
        pool_events = {n: sem(n) for n in (
            "dts_ready", "dx_ready", "hc_ready",
            "gated", "yn_ready")}
        ev = {**pe_events, **act_events, **dve_events, **pool_events}

        def tokens(buf, b, at=0, n=T, parts=slice(0, P)):
            return buf[parts, bass.ds(b * T + at, n)]

        def over_halves(ap):
            return ap.unsqueeze(1).broadcast_to([P, HALVES, T])

        def over_experts(ap):
            return ap.unsqueeze(2).broadcast_to([P, 3, EXPERTS])

        NS = STATES

        def wait_apart(eng, event, value):
            eng.wait_ge(ev[event], value)
            eng.sem_inc(waited, 1)

        def rsqrt_scalar(act, i, b, var):
            act.wait_ge(ev[f"var{i}"], done(b))
            act.wait_ge(ev[f"rs{i}_ready"], done(b - 1))
            act.activation(lnv[i][:], var, ACT.Ln, bias=eps[:]).then_inc(ev[f"ln_taken{i}"], 1)
            act.wait_ge(ev[f"ln_taken{i}"], done(b))
            act.activation(r0[i][:], lnv[i][:], ACT.Exp, scale=-0.5).then_inc(ev[f"r0_ready{i}"], 1)
            act.wait_ge(ev[f"r0_ready{i}"], done(b))
            act.activation(r0sq[i][:], r0[i][:], ACT.Square).then_inc(ev[f"r0_squared{i}"], 1)

        def rsqrt_vector(dve, i, b, var, rs):
            dve.wait_ge(ev[f"r0_squared{i}"], done(b))
            dve.scalar_tensor_tensor(out=newton[i][:], in0=var, scalar=EPS, in1=r0sq[i][:],
                                     op0=ALU.add, op1=ALU.mult).then_inc(ev[f"vr_ready{i}"], 1)
            dve.wait_ge(ev[f"vr_ready{i}"], done(b))
            dve.scalar_tensor_tensor(out=rs[:], in0=newton[i][:], scalar=-3.0, in1=r0[i][:],
                                     op0=ALU.add, op1=ALU.mult).then_inc(ev[f"rs{i}_ready"], 1)

        def pre_tensor(pe, b, k):
            q = parity(b)
            b = turn(b)
            if k == 0:
                pe.wait_ge(ev["dtabs_ready"], done(b - 1))
                pe.matmul(pre[0][:, 0:T], ones_ln[:], tokens(hT, b), start=True, stop=True).then_inc(ev["mean1"], 1)
            if k == 2:
                pe.wait_ge(ev["sq1_ready"], done(b))
                pe.matmul(pre[1][:, 0:T], ones_ln[:], sq1[:], start=True, stop=True).then_inc(ev["var1"], 1)
            if k == 4:
                pe.wait_ge(ev["xn1_ready"], done(b))
                for h in range(HALVES):
                    for i in range(3):
                        last = pe.matmul(pre[h][:, 0:T], in_T[:, i, h, :], xn1[:, i:i + T], start=(i == 0), stop=(i == 2))
                last.then_inc(ev["xin_ready"], 1)
            if k == 5:
                pe.wait_ge(ev["xc_ready"], done(b))
                for h in range(HALVES):
                    last = pe.matmul(pre[h][:, 0:T], z_T[:, h, :], xn1[:, 1:T + 1], start=True, stop=True)
                last.then_inc(ev["z_ready"], 1)
            if k == 6:
                pe.wait_ge(ev["zg_ready"], done(b))
                for h in range(HALVES):
                    last = pe.matmul(pre[0][:, 0:T], xp_T[:, h, :], xc[q][:, h, :], start=(h == 0), stop=(h == 1))
                last.then_inc(ev["dbc_ready"], 1)
            if k == 7:
                pe.wait_ge(ev["drow_ready"], done(b))
                pe.wait_ge(ev["rest_ready"], done(b))
                for h in range(HALVES):
                    last = pe.matmul(pre[h][:, 0:T], dt_row[0:1, h * P:(h + 1) * P], d_row[0:1, :], start=True, stop=True)
                last.then_inc(ev["dt_ready"], 1)

        def pre_scalar(act, b, k):
            q = parity(b)
            b = turn(b)
            if k == 1:
                act.wait_ge(ev["cen1_ready"], done(b))
                act.activation(sq1[:], cen1[:], ACT.Square).then_inc(ev["sq1_ready"], 1)
            if k == 2:
                rsqrt_scalar(act, 1, b, pre[1][:, 0:T])
            if k == 5:
                act.preload_act_table_set("silu_and_others")
                act.wait_ge(ev["xin_ready"], done(b))
                act.wait_ge(ev["ysum_ready"], done(b - 2))
                act.wait_ge(ev["y_ready2"], done(b - 2))
                for h in range(HALVES):
                    last = act.activation(xc[q][:, h, :], pre[h][:, 0:T], ACT.Silu, bias=vec[:, 0, h:h + 1])
                last.then_inc(ev["xc_ready"], 1)
                act.wait_ge(ev["z_ready"], done(b))
                act.wait_ge(ev["gated"], done(b - 2))
                for h in range(HALVES):
                    last = act.activation(zg[q][:, h, :], pre[h][:, 0:T], ACT.Silu)
                last.then_inc(ev["zg_ready"], 1)
                act.preload_act_table_set("natural_log_exp_and_others")
            if k == 6:
                act.wait_ge(ev["dbc_ready"], done(b))
                act.copy(d_row[0:1, :], pre[0][0:1, 0:T]).then_inc(ev["drow_ready"], 1)
                act.wait_ge(ev["ysum_ready"], done(b - 2))
                act.copy(bc[q][:], pre[0][:, 0:T]).then_inc(ev["bc_hi_ready"], 1)
            if k == 7:
                act.wait_ge(ev["rest_ready"], done(b))
                act.copy(bc[q][64:128, :], rest[64:128, :]).then_inc(ev["bc_mid_ready"], 1)
            if k == 8:
                act.wait_ge(ev["dt_ready"], done(b))
                act.wait_ge(ev["delta_ready"], done(b - 1))
                for h in range(HALVES):
                    act.activation(dt_pos[:, h, :], pre[h][:, 0:T], ACT.Relu, bias=vec[:, 1, h:h + 1])
                    last = act.activation(dt_abs[:, h, :], pre[h][:, 0:T], ACT.Abs, bias=vec[:, 1, h:h + 1])
                last.then_inc(ev["dtabs_ready"], 1)
                act.wait_ge(ev["dtabs_ready"], done(b))
                act.activation(dt_exp[:], dt_abs[:], ACT.Exp, scale=-1.0).then_inc(ev["dtexp_ready"], 1)
            if k == 9:
                act.wait_ge(ev["dtexp_ready"], done(b))
                act.activation(dt_ln[:], dt_exp[:], ACT.Ln, bias=two[:]).then_inc(ev["dtln_ready"], 1)
                act.wait_ge(ev["dtln_ready"], done(b))
                act.activation(dt_rec[:], dt_ln[:], ACT.Exp, scale=-1.0).then_inc(ev["dtrec_ready"], 1)
            if k == 10:
                act.wait_ge(ev["dts_ready"], done(b))
                act.activation(dt_s2[:], dt_s[:], ACT.Square).then_inc(ev["dts2_ready"], 1)

        def pre_vector(dve, b, k):
            q = parity(b)
            b = turn(b)
            if k == 0:
                dve.wait_ge(ev["mean1"], done(b))
                dve.tensor_tensor(cen1[:], tokens(hT, b), pre[0][:, 0:T], ALU.subtract).then_inc(ev["cen1_ready"], 1)
            if k == 3:
                rsqrt_vector(dve, 1, b, pre[1][:, 0:T], rs1)
                dve.wait_ge(ev["rs1_ready"], done(b))
                dve.scalar_tensor_tensor(out=xn1[:, 1:T + 1], in0=cen1[:], scalar=-0.5, in1=rs1[:],
                                         op0=ALU.mult, op1=ALU.mult).then_inc(ev["xn1_ready"], 1)
            if k == 6:
                dve.wait_ge(ev["bc_hi_ready"], done(b))
                dve.tensor_tensor(rest[:], pre[0][:, 0:T], bc[q][:], ALU.subtract).then_inc(ev["rest_ready"], 1)
            if k == 8:
                dve.wait_ge(ev["bc_mid_ready"], done(b))
                dve.tensor_tensor(bc[q][96:128, :], rest[96:128, :], bc[q][96:128, :], ALU.subtract
                                  ).then_inc(ev["bc_ready"], 1)
            if k == 10:
                dve.wait_ge(ev["dts2_ready"], done(b))
                dve.tensor_scalar(dt_poly[:], dt_s2[:], SERIES[4], None, ALU.mult).then_inc(ev["poly_done"], 1)
                dve.wait_ge(ev["poly_done"], done(5 * b))
                dve.scalar_tensor_tensor(out=dt_poly[:], in0=dt_poly[:], scalar=SERIES[3], in1=dt_s2[:],
                                         op0=ALU.add, op1=ALU.mult).then_inc(ev["poly_done"], 1)
            if k == 11:
                dve.wait_ge(ev["poly_done"], done(5 * b + 1))
                dve.scalar_tensor_tensor(out=dt_poly[:], in0=dt_poly[:], scalar=SERIES[2], in1=dt_s2[:],
                                         op0=ALU.add, op1=ALU.mult).then_inc(ev["poly_done"], 1)
                dve.wait_ge(ev["poly_done"], done(5 * b + 2))
                dve.scalar_tensor_tensor(out=dt_poly[:], in0=dt_poly[:], scalar=SERIES[1], in1=dt_s2[:],
                                         op0=ALU.add, op1=ALU.mult).then_inc(ev["poly_done"], 1)
            if k == 12:
                dve.wait_ge(ev["poly_done"], done(5 * b + 3))
                dve.scalar_tensor_tensor(out=dt_poly[:], in0=dt_poly[:], scalar=SERIES[0], in1=dt_s[:],
                                         op0=ALU.add, op1=ALU.mult).then_inc(ev["poly_done"], 1)
                dve.wait_ge(ev["poly_done"], done(5 * b + 4))
                dve.wait_ge(ev["ysum_ready"], done(b - 2))
                dve.tensor_tensor(delta[q][:], dt_poly[:], dt_pos[:], ALU.add).then_inc(ev["delta_ready"], 1)

        def pre_gpsimd(pool, b, k):
            q = parity(b)
            b = turn(b)
            if k == 9:
                pool.wait_ge(ev["dtrec_ready"], done(b))
                pool.tensor_tensor(dt_s[:], dt_exp[:], dt_rec[:], ALU.mult).then_inc(ev["dts_ready"], 1)
            if k == 12:
                pool.wait_ge(ev["delta_ready"], done(b))
                pool.tensor_tensor(dx[q][:], delta[q][:], xc[q][:], ALU.mult).then_inc(ev["dx_ready"], 1)

        def cast_states(pe, b, s):
            q, n = parity(b), NS * turn(b) + s
            if s == 0:
                pe.wait_ge(ev["bc_ready"], done(turn(b)))
            pe.wait_ge(ev["bx_ready"], done(n - 1))
            pe.matmul(bank_b[:, 0:T], pick[:, s:s + 1].broadcast_to([P, P]), bc[q][:], start=True, stop=True
                      ).then_inc(ev["b_cast"], 1)
            pe.wait_ge(ev["c_copied"], done(n - 1))
            pe.matmul(bank_c[:, 0:T], pick[:, NS + s:NS + s + 1].broadcast_to([P, P]), bc[q][:], start=True, stop=True
                      ).then_inc(ev["c_cast"], 1)

        def sum_states(pe, b, s):
            n = NS * turn(b) + s
            if s == 0:
                pe.wait_ge(ev["y_ready2"], done(turn(b) - 1))
            pe.wait_ge(ev["hc_ready"], done(n))
            for h in range(HALVES):
                last = pe.matmul(ysum[h][:, 0:T], ident[:], hc[s % DEEP][:, h, :], start=(s == 0), stop=(s == NS - 1))
            last.then_inc(ev["summed"], 1)
            if s == NS - 1:
                pe.wait_ge(ev["summed"], done(n))
                pe.sem_inc(ev["ysum_ready"], 1)

        def scan_tensor(pe, b, s, following, previous, post, pre):
            if s + 1 < NS:
                cast_states(pe, b, s + 1)
            elif following:
                cast_states(pe, following, 0)
            if s >= LAG:
                sum_states(pe, b, s - LAG)
            elif previous:
                sum_states(pe, previous, s - LAG + NS)
            post()
            pre()

        def decays(act, b, s):
            q, n = parity(b), NS * turn(b) + s
            if s == 0:
                act.wait_ge(ev["delta_ready"], done(turn(b)))
            act.wait_ge(ev["scan_done"], done(n - DEEP))
            for h in range(HALVES):
                last = act.activation(dA[s % DEEP][:, h, 1:T], delta[q][:, h, 1:T], ACT.Exp, scale=a_neg[:, h, s:s + 1])
            last.then_inc(ev["dA_ready"], 1)

        def scan_scalar(act, b, s, following, previous, post, pre):
            n = NS * turn(b) + s
            act.wait_ge(ev["c_cast"], done(n))
            act.wait_ge(ev["hc_ready"], done(n - DEEP))
            act.copy(cs[s % DEEP][:], bank_c[:, 0:T]).then_inc(ev["c_copied"], 1)
            if s + AHEAD < NS:
                decays(act, b, s + AHEAD)
            elif following:
                decays(act, following, s + AHEAD - NS)
            post()
            pre()

        def scan_vector(dve, b, s, following, previous, post, pre):
            q, n = parity(b), NS * turn(b) + s
            if s == 0:
                dve.wait_ge(ev["dx_ready"], done(turn(b)))
            dve.wait_ge(ev["b_cast"], done(n))
            dve.tensor_tensor(bx[s % 2][:], dx[q][:], over_halves(bank_b[:, 0:T]), ALU.mult).then_inc(ev["bx_ready"], 1)
            dve.wait_ge(ev["bx_ready"], done(n))
            dve.wait_ge(ev["dA_ready"], done(n))
            dve.wait_ge(ev["hc_ready"], done(n - DEEP))
            dve.tensor_tensor_scan(hs[s % DEEP][:].rearrange("p h t -> p (h t)"),
                                   dA[s % DEEP][:].rearrange("p h t -> p (h t)"),
                                   bx[s % 2][:].rearrange("p h t -> p (h t)"), 0.0, ALU.mult, ALU.add
                                   ).then_inc(ev["scan_done"], 1)
            post()
            pre()

        def scan_gpsimd(pool, b, s, following, previous, post, pre):
            n = NS * turn(b) + s
            pool.wait_ge(ev["scan_done"], done(n))
            pool.wait_ge(ev["c_copied"], done(n))
            pool.wait_ge(ev["summed"], done(n - DEEP))
            pool.tensor_tensor(hc[s % DEEP][:], hs[s % DEEP][:], over_halves(cs[s % DEEP][:]), ALU.mult
                               ).then_inc(ev["hc_ready"], 1)
            post()
            pre()

        def post_tensor(pe, b, k):
            b = turn(b)
            if k == 3:
                pe.wait_ge(ev["gated"], done(b))
                pe.wait_ge(ev["comb_ready"], done(b - 1))
                for h in range(HALVES):
                    last = pe.matmul(post[0][:, 0:T], ones_inner[:], yz[:, h, :], start=(h == 0), stop=(h == 1))
                last.then_inc(ev["mean2"], 1)
            if k == 5:
                pe.wait_ge(ev["sq2_ready"], done(b))
                for h in range(HALVES):
                    last = pe.matmul(post[1][:, 0:T], ones_inner[:], sq2[:, h, :], start=(h == 0), stop=(h == 1))
                last.then_inc(ev["var2"], 1)
            if k == 8:
                pe.wait_ge(ev["yn_ready"], done(b))
                for h in range(HALVES):
                    last = pe.matmul(post[0][:, 0:T], out_gT[:, h, :], yn[:, h, :], start=(h == 0), stop=(h == 1))
                last.then_inc(ev["proj_ready"], 1)
            if k == 9:
                pe.wait_ge(ev["h_ready"], done(b))
                pe.matmul(post[1][:, 0:T], ones_ln[:], tokens(hT, b), start=True, stop=True).then_inc(ev["mean3"], 1)
            if k == 10:
                pe.wait_ge(ev["sq3_ready"], done(b))
                pe.matmul(post[0][:, 0:T], ones_ln[:], sq3[:], start=True, stop=True).then_inc(ev["var3"], 1)
            if k == 12:
                pe.wait_ge(ev["xn3_ready"], done(b))
                for i, at in enumerate(ROUTE_AT):
                    pe.matmul(post[1][:, i * EXPERTS:(i + 1) * EXPERTS], xn3[:, at:at + P], rw[:], start=True, stop=False)
                    last = pe.matmul(post[1][:, i * EXPERTS:(i + 1) * EXPERTS], ones_row[:], rb[:], start=False, stop=True)
                last.then_inc(ev["logits_ready"], 1)
            if k == 15:
                pe.wait_ge(ev["cw_ready"], done(b))
                for i, at in enumerate(ROUTE_AT):
                    last = pe.transpose(post[0][:, at:at + P], cw[:, i, :, :].rearrange("p a e -> p (a e)"), ident[:])
                last.then_inc(ev["comb_flipped"], 1)

        def post_scalar(act, b, k):
            b = turn(b)
            if k == 4:
                act.wait_ge(ev["cen2_ready"], done(b))
                act.activation(sq2[:], cen2[:], ACT.Square).then_inc(ev["sq2_ready"], 1)
            if k == 6:
                rsqrt_scalar(act, 2, b, post[1][:, 0:T])
            if k == 9:
                act.wait_ge(ev["cen3_ready"], done(b))
                act.activation(sq3[:], cen3[:], ACT.Square).then_inc(ev["sq3_ready"], 1)
            if k == 10:
                rsqrt_scalar(act, 3, b, post[0][:, 0:T])
            if k == 12:
                act.wait_ge(ev["xn3_ready"], done(b))
                act.activation(tokens(x_hi, b), xn3[:], ACT.Copy, scale=XSCALE).then_inc(ev["xhi_ready"], 1)
                act.wait_ge(ev["lg_ready"], done(b))
                act.activation(ex[:], lg[:], ACT.Exp).then_inc(ev["ex_ready"], 1)
            if k == 13:
                act.wait_ge(ev["qn_ready"], done(b))
                for i in range(3):
                    last = act.activation(ew[:, i, :], qn[:, i, 0:EXPERTS], ACT.Exp, scale=-1.0, bias=srec[:, i:i + 1])
                last.then_inc(ev["ew_ready"], 1)
            if k == 15:
                act.wait_ge(ev["comb_flipped"], done(b))
                act.activation(tokens(comb, b), post[0][:, 0:T], ACT.Copy, scale=CSCALE).then_inc(ev["comb_hi_ready"], 1)

        def post_vector(dve, b, k):
            q = parity(b)
            b = turn(b)
            if k == 1:
                dve.wait_ge(ev["ysum_ready"], done(b))
                for h in range(HALVES):
                    last = dve.scalar_tensor_tensor(out=yb[:, h, :], in0=xc[q][:, h, :], scalar=vec[:, 2, h:h + 1],
                                                    in1=ysum[h][:, 0:T], op0=ALU.mult, op1=ALU.add)
                last.then_inc(ev["y_ready2"], 1)
            if k == 3:
                dve.wait_ge(ev["mean2"], done(b))
                dve.tensor_tensor(cen2[:], yz[:], over_halves(post[0][:, 0:T]), ALU.subtract).then_inc(ev["cen2_ready"], 1)
            if k == 6:
                dve.wait_ge(ev["yn_ready"], done(b - 1))
                rsqrt_vector(dve, 2, b, post[1][:, 0:T], rs2)
            if k == 8:
                dve.wait_ge(ev["proj_ready"], done(b))
                dve.scalar_tensor_tensor(out=tokens(hT, b), in0=post[0][:, 0:T], scalar=out_bias[:, 0:1],
                                         in1=tokens(hT, b), op0=ALU.add, op1=ALU.add).then_inc(ev["h_ready"], 1)
            if k == 9:
                dve.wait_ge(ev["mean3"], done(b))
                dve.tensor_tensor(cen3[:], tokens(hT, b), post[1][:, 0:T], ALU.subtract).then_inc(ev["cen3_ready"], 1)
            if k == 11:
                rsqrt_vector(dve, 3, b, post[0][:, 0:T], rs3)
                dve.wait_ge(ev["rs3_ready"], done(b))
                dve.wait_ge(ev["logits_ready"], done(b - 1))
                dve.scalar_tensor_tensor(out=xn3[:], in0=cen3[:], scalar=-0.5, in1=rs3[:],
                                         op0=ALU.mult, op1=ALU.mult).then_inc(ev["xn3_ready"], 1)
            if k == 12:
                dve.wait_ge(ev["logits_ready"], done(b))
                logits = post[1][:, 0:3 * EXPERTS].rearrange("p (i e) -> p i e", e=EXPERTS)
                dve.tensor_reduce(top[:], logits, AX.X, ALU.max).then_inc(ev["top_ready"], 1)
                dve.wait_ge(ev["top_ready"], done(b))
                dve.tensor_tensor(lg[:], logits, over_experts(top[:]), ALU.subtract).then_inc(ev["lg_ready"], 1)
            if k == 13:
                dve.wait_ge(ev["ex_ready"], done(b))
                dve.tensor_reduce(ssum[:], ex[:], AX.X, ALU.add).then_inc(ev["ssum_ready"], 1)
                dve.wait_ge(ev["ssum_ready"], done(b))
                dve.wait_ge(ev["ew_ready"], done(b - 1))
                dve.reciprocal(wrec[:], ssum[:]).then_inc(ev["srec_ready"], 1)
                dve.wait_ge(ev["srec_ready"], done(b))
                dve.tensor_scalar(srec[:], wrec[:], -1.0, None, ALU.mult).then_inc(ev["nsrec_ready"], 1)
                dve.wait_ge(ev["nsrec_ready"], done(b))
                dve.tensor_tensor(qn[:, :, 0:EXPERTS], ex[:], over_experts(srec[:]), ALU.mult)
                dve.memset(qn[:, :, EXPERTS:QCOLS], 1.0).then_inc(ev["qn_ready"], 1)
                dve.wait_ge(ev["xhi_ready"], done(b))
                dve.scalar_tensor_tensor(out=tokens(x_lo, b), in0=xn3[:], scalar=XSCALE, in1=tokens(x_hi, b),
                                         op0=ALU.mult, op1=ALU.subtract).then_inc(ev["xlo_ready"], 1)
            if k == 14:
                for r in range(ROUNDS):
                    if r == 0:
                        wait_apart(dve, "ew_ready", done(b))
                    else:
                        wait_apart(dve, "low_dropped", done(ROUNDS * b + r - 1))
                    for i in range(3):
                        last = dve.max(low8[:, i, :], qn[:, i, :])
                    last.then_inc(ev["low_found"], 1)
                    wait_apart(dve, "low_found", done(ROUNDS * b + r))
                    for i in range(3):
                        last = dve.match_replace(qn[:, i, :], low8[:, i, :], qn[:, i, :], -5.0)
                    last.then_inc(ev["low_dropped"], 1)
                dve.wait_ge(ev["low_dropped"], done(ROUNDS * b + ROUNDS - 1))
                dve.scalar_tensor_tensor(out=wm[:], in0=qn[:, :, 0:EXPERTS], scalar=-2.0, in1=ew[:],
                                         op0=ALU.is_gt, op1=ALU.mult).then_inc(ev["wm_ready"], 1)
                dve.wait_ge(ev["wm_ready"], done(b))
                dve.tensor_reduce(wsum[:], wm[:], AX.X, ALU.add).then_inc(ev["wsum_ready"], 1)
                dve.wait_ge(ev["wsum_ready"], done(b))
                dve.reciprocal(wrec[:], wsum[:]).then_inc(ev["wrec_ready"], 1)
                dve.wait_ge(ev["wrec_ready"], done(b))
                dve.wait_ge(ev["comb_flipped"], done(b - 1))
                for a in range(2):
                    last = dve.tensor_tensor(cw[:, :, a, :], wm[:], over_experts(wrec[:]), ALU.mult)
                last.then_inc(ev["cw_ready"], 1)
            if k == 15:
                dve.wait_ge(ev["comb_hi_ready"], done(b))
                low = tokens(comb, b, parts=slice(EXPERTS, P))
                dve.scalar_tensor_tensor(out=low, in0=post[0][EXPERTS:P, 0:T], scalar=CSCALE, in1=low,
                                         op0=ALU.mult, op1=ALU.subtract).then_inc(ev["comb_ready"], 1)

        def post_gpsimd(pool, b, k):
            q = parity(b)
            b = turn(b)
            if k == 2:
                pool.wait_ge(ev["y_ready2"], done(b))
                pool.tensor_tensor(yz[:], yb[:], zg[q][:], ALU.mult).then_inc(ev["gated"], 1)
            if k == 7:
                pool.wait_ge(ev["rs2_ready"], done(b))
                pool.tensor_tensor(yn[:], cen2[:], over_halves(rs2[:]), ALU.mult).then_inc(ev["yn_ready"], 1)

        def turn(b):
            return b[0]

        def parity(b):
            return b[1]

        def steps(eng, pre_stage, scan_stage, post_stage, b, with_pre=True, with_post=True):
            t, q = b
            following = (t + 1, 1 - q) if with_pre else None
            previous = (t - 1, 1 - q) if with_post else None
            for k in range(NS):
                scan_stage(eng, b, k, following, previous,
                           lambda: post_stage(eng, previous, k) if previous else None,
                           lambda: pre_stage(eng, following, k) if following else None)

        def alone(eng, stage, b):
            for k in range(NS):
                stage(eng, b, k)

        def run(eng, pre_stage, scan_stage, post_stage):
            alone(eng, pre_stage, (0, 0))
            if scan_stage is scan_tensor:
                cast_states(eng, (0, 0), 0)
            if scan_stage is scan_scalar:
                for s in range(AHEAD):
                    decays(eng, (0, 0), s)
            steps(eng, pre_stage, scan_stage, post_stage, (0, 0), with_post=False)
            with eng.Fori(0, SEQS // 2 - 1) as i:
                steps(eng, pre_stage, scan_stage, post_stage, (2 * i + 1, 1))
                steps(eng, pre_stage, scan_stage, post_stage, (2 * i + 2, 0))
            steps(eng, pre_stage, scan_stage, post_stage, (SEQS - 1, 1), with_pre=False)
            if scan_stage is scan_tensor:
                for s in range(NS - LAG, NS):
                    sum_states(eng, (SEQS - 1, 1), s)
            alone(eng, post_stage, (SEQS - 1, 1))

        def start(eng, events):
            for name in events:
                eng.sem_inc(ev[name], BIAS)

        block = ctx.enter_context(nc.Block())
        N_WEIGHTS = 13

        @block.sync
        def _(sp):
            loads = [
                (in_rows[:], in_w.rearrange("(n p) d -> p n d", p=P)),
                (xp_rows[:], xproj_w),
                (out_rows[:], out_w),
                (a_raw[:], a_log.rearrange("(h p) s -> p h s", p=P)),
                (taps[:], conv_w.rearrange("(h p) a k -> p h (a k)", p=P)),
                (vec[:, 0, :], conv_b),
                (vec[:, 1, :], dt_b),
                (vec[:, 2, :], d_par),
                (vec[:, 3, :], ln_g),
                (vec[:, 4, :], ln_b),
                (dt_row[:], dt_w),
                (rw[:], router_w),
                (rb[:], router_b.rearrange("(a e) -> a e", a=1)),
            ]
            assert len(loads) == N_WEIGHTS
            for dst, src in loads:
                sp.dma_start(dst, src).then_inc(weights_in, 16)

        LOADED = 16 * N_WEIGHTS

        @block.gpsimd
        def _(pool):
            start(pool, pool_events)
            pool.memset(ones_inner[:], 1.0 / INNER).then_inc(inner_ready, 1)
            pool.memset(ones_row[:], 1.0).then_inc(row_ready, 1)
            pool.memset(pick_raw[:], 0.0).then_inc(pick_zeroed, 1)
            for i in range(3):
                pool.wait_ge(pick_zeroed if i == 0 else pick_made, max(i, 1))
                pool.affine_select(out=pick_raw[:], in_=pick_raw[:], compare_op=ALU.not_equal, fill=1.0,
                                   base=-32 * (i + 1), pattern=[[-1, 2 * STATES]], channel_multiplier=1
                                   ).then_inc(pick_made, 1)
            pool.wait_ge(pick_made, 3)
            pool.tensor_copy(pick[:], pick_raw[:]).then_inc(pick_ready, 1)
            pool.memset(eps[:], EPS).then_inc(eps_ready, 1)
            pool.memset(two[:], 2.0).then_inc(eps_ready, 1)
            pool.memset(xn1[:, 0:1], 0.0).then_inc(zero_ready, 1)
            pool.memset(xn1[:, T + 1:T + 2], 0.0).then_inc(zero_ready, 1)
            for i in range(DEEP):
                pool.memset(dA[i][:, :, 0:1], 0.0).then_inc(zero_ready, 1)
            run(pool, pre_gpsimd, scan_gpsimd, post_gpsimd)

        @block.tensor
        def _(pe):
            start(pe, pe_events)
            pe.wait_ge(weights_in, LOADED)
            pe.wait_ge(tap_rows_ready, 1)
            for i in range(3):
                into = (ysum[0], ysum[1], pre[0])[i]
                for h in range(HALVES):
                    last = pe.transpose(into[:, h * P:(h + 1) * P], tap_rows[:, i, h, :], ident[:])
            for h in range(HALVES):
                last = pe.transpose(pre[0][:, (HALVES + h) * P:(HALVES + h + 1) * P], in_rows[:, HALVES + h, :], ident[:])
            last.then_inc(in_flipped, 1)
            NX = 1 + 2 * STATES
            for h in range(HALVES):
                last = pe.transpose(pre[1][:, h * P:h * P + NX], xp_rows[:, h * P:(h + 1) * P], ident[0:NX, 0:NX])
            last.then_inc(xp_flipped, 1)
            for h in range(HALVES):
                last = pe.transpose(post[0][:, h * P:(h + 1) * P], out_rows[:, h * P:(h + 1) * P], ident[:])
            last.then_inc(out_flipped, 1)
            pe.wait_ge(out_copied, 1)
            for h in range(HALVES):
                last = pe.matmul(post[1][:, 0:1], out_T[:, h, :], vec[:, 4, h:h + 1], start=(h == 0), stop=(h == 1))
            last.then_inc(bias_summed, 1)
            pe.wait_ge(in_copied, 1)
            pe.wait_ge(xp_copied, 1)
            pe.wait_ge(out_copied, 2)
            pe.wait_ge(bias_ready, 1)
            pe.wait_ge(inner_ready, 1)
            pe.wait_ge(row_ready, 1)
            pe.wait_ge(pick_ready, 1)
            run(pe, pre_tensor, scan_tensor, post_tensor)

        @block.scalar
        def _(act):
            start(act, act_events)
            act.wait_ge(weights_in, LOADED)
            act.wait_ge(a_capped_ready, 1)
            act.activation(a_exp[:], a_capped[:], ACT.Exp).then_inc(a_exp_ready, 1)
            act.wait_ge(in_flipped, 1)
            for i in range(3):
                bank_i = (ysum[0], ysum[1], pre[0])[i]
                act.copy(in_T[:, i, :, :], bank_i[:, 0:HALVES * P].rearrange("p (n e) -> p n e", e=P))
            act.copy(z_T[:], pre[0][:, HALVES * P:2 * HALVES * P].rearrange("p (n e) -> p n e", e=P)).then_inc(in_copied, 1)
            act.preload_act_table_set("natural_log_exp_and_others")
            act.wait_ge(a_neg_ready, 1)
            act.wait_ge(zero_ready, 2 + DEEP)
            act.wait_ge(eps_ready, 2)
            run(act, pre_scalar, scan_scalar, post_scalar)

        @block.vector
        def _(dve):
            start(dve, dve_events)
            dve.wait_ge(weights_in, LOADED)
            for i in range(3):
                for h in range(HALVES):
                    last = dve.tensor_scalar(tap_rows[:, i, h, :], in_rows[:, h, :], taps[:, h, i:i + 1], None, ALU.mult)
            last.then_inc(tap_rows_ready, 1)
            dve.tensor_scalar(a_capped[:], a_raw[:], A_LOG_CAP, None, ALU.min).then_inc(a_capped_ready, 1)
            dve.wait_ge(a_exp_ready, 1)
            dve.tensor_scalar(a_neg[:], a_exp[:], -1.0, None, ALU.mult).then_inc(a_neg_ready, 1)
            dve.memset(xp_T[:], 0.0).then_inc(xp_zeroed, 1)
            dve.wait_ge(xp_zeroed, 1)
            dve.wait_ge(xp_flipped, 1)
            for h in range(HALVES):
                dve.tensor_copy(xp_T[:, h, 0:1], pre[1][:, h * P:h * P + 1])
                for g in range(1, 4):
                    last = dve.tensor_copy(xp_T[:, h, 32 * g:32 * (g + 1)], pre[1][:, h * P + 1:h * P + 1 + 2 * STATES])
            last.then_inc(xp_copied, 1)
            dve.wait_ge(out_flipped, 1)
            dve.tensor_copy(out_T[:], post[0][:, 0:HALVES * P].rearrange("p (h d) -> p h d", d=P)).then_inc(out_copied, 1)
            dve.wait_ge(out_copied, 1)
            for h in range(HALVES):
                last = dve.tensor_scalar(out_gT[:, h, :], out_T[:, h, :], vec[:, 3, h:h + 1], -0.5, ALU.mult, ALU.mult)
            last.then_inc(out_copied, 1)
            dve.wait_ge(bias_summed, 1)
            dve.tensor_copy(out_bias[:], post[1][:, 0:1]).then_inc(bias_ready, 1)
            dve.wait_ge(bias_ready, 1)
            dve.wait_ge(zero_ready, 2 + DEEP)
            run(dve, pre_vector, scan_vector, post_vector)


def experts(nc, hT, ident, x_hi, x_lo, comb, w1, b1, w2, b2, out):
    sems = []
    with ExitStack() as ctx:
        ctx.callback(clear, nc, sems)

        def sb(name, shape, dt=F32):
            return ctx.enter_context(nc.sbuf_tensor(name, shape, dt))

        def bank(name):
            return ctx.enter_context(nc.psum_tensor(name, [P, 512], F32))

        PAIR = 2
        COLS = HIDDEN + HALVES * DIM

        w_hi = sb("w_hi", [P, EXPERTS * COLS], F16)
        w_lo = sb("w_lo", [P, EXPERTS * COLS], F16)
        stage = [sb(f"stage{i}", [P, PAIR * COLS]) for i in range(2)]
        b1_rows = sb("b1_rows", [P, P])
        b1_T = sb("b1_T", [P, P])
        b2_in = sb("b2_in", [P, DIM])
        b2_hi, b2_lo = sb("b2_hi", [P, DIM], F16), sb("b2_lo", [P, DIM], F16)
        sel_raw = sb("sel_raw", [P, EXPERTS])
        sel = sb("sel", [P, EXPERTS], F16)
        g = [sb(f"g{i}", [P, HALVES, T]) for i in range(2)]
        m = [sb(f"m{i}", [P, HALVES, T]) for i in range(2)]
        m_hi = [sb(f"m_hi{i}", [P, HALVES, T], F16) for i in range(4)]
        m_lo = [sb(f"m_lo{i}", [P, HALVES, T], F16) for i in range(4)]
        o_T = sb("o_T", [P, T])
        o_rows = sb("o_rows", [P, 3, P])

        up_bank = [bank(f"up{i}") for i in range(HALVES)]
        cast = [bank(f"cast{i}") for i in range(2)]
        y = bank("y")
        turned = bank("turned")

        def sem(name):
            sems.append(ctx.enter_context(nc.semaphore(name)))
            return sems[-1]

        small_in = sem("small_in")
        stage_in = [sem(f"stage{i}_in") for i in range(2)]
        split_hi, split_lo = sem("split_hi"), sem("split_lo")
        sel_zeroed, sel_made, sel_ready = sem("sel_zeroed"), sem("sel_made"), sem("sel_ready")
        b1_flipped, b1_ready = sem("b1_flipped"), sem("b1_ready")
        b2_hi_ready, b2_ready = sem("b2_hi_ready"), sem("b2_ready")
        up_ready = [sem(f"up{h}_ready") for h in range(HALVES)]
        cast_ready, gelu_done, m_ready = sem("cast_ready"), sem("gelu_done"), sem("m_ready")
        hi_ready, down_done = sem("hi_ready"), sem("down_done")
        lo_ready = {"dve": sem("dve_lo_ready"), "pool": sem("pool_lo_ready")}
        y_summed, o_ready, o_flipped, rows_ready, stored = (
            sem("y_summed"), sem("o_ready"), sem("o_flipped"), sem("rows_ready"), sem("stored"))

        LAG = 3
        QUAD = 4
        QUADS = EXPERTS // QUAD
        PAIRS_PER_QUAD = QUAD // PAIR
        LO_ON = ["dve", "pool", "dve", "pool"]
        STORES = 2

        def weight(buf, layer, e, h):
            even, odd = e
            return buf[:, bass.ds(even * COLS + (PAIR * layer + odd) * HIDDEN + h * P, P)]

        def tokens(buf, b):
            return buf[:, bass.ds(b * T, T)]

        def wait_lo(eng, quad, j, back=0):
            who = LO_ON[j % QUAD]
            per = LO_ON.count(who)
            eng.wait_ge(lo_ready[who], done(per * (quad - back) + LO_ON[:j].count(who)))

        def up(pe, b, e, j):
            n = EXPERTS * b + e
            for h in range(HALVES):
                pe.wait_ge(gelu_done, done(2 * (n - 1) + h))
                w_h, w_l = (weight(w, 0, (e - j % PAIR, j % PAIR), h) for w in (w_hi, w_lo))
                pe.matmul(up_bank[h][:, 0:T], w_h, tokens(x_hi, b), start=True, stop=False)
                pe.matmul(up_bank[h][:, 0:T], w_h, tokens(x_lo, b), start=False, stop=False)
                pe.matmul(up_bank[h][:, 0:T], w_l, tokens(x_hi, b), start=False, stop=True).then_inc(up_ready[h], 1)
            pe.wait_ge(m_ready, done(n - 2))
            pe.matmul(cast[j % 2][:, 0:T], sel[:, bass.ds(e, 1)].broadcast_to([P, P]), tokens(comb, b),
                      start=True, stop=True).then_inc(cast_ready, 1)

        def down(pe, b, qd, j, last):
            n = EXPERTS * b + QUAD * qd + j
            pe.wait_ge(hi_ready, done(n))
            wait_lo(pe, QUADS * b + qd, j)
            for h in range(HALVES):
                w_h, w_l = (weight(w, 1, (QUAD * qd + j - j % PAIR, j % PAIR), h) for w in (w_hi, w_lo))
                pe.matmul(y[:, 0:T], w_h, m_hi[j][:, h, :], start=False, stop=False)
                pe.matmul(y[:, 0:T], w_h, m_lo[j][:, h, :], start=False, stop=False)
                mm = pe.matmul(y[:, 0:T], w_l, m_hi[j][:, h, :], start=False, stop=last and h == HALVES - 1)
            mm.then_inc(down_done, 1)
            if last:
                pe.wait_ge(down_done, done(n))
                pe.sem_inc(y_summed, 1)

        def tensor_quad(pe, b, qd, first, tail, end, between=None):
            for j in range(QUAD):
                ahead = j + LAG
                if ahead < QUAD or not tail:
                    if first:
                        pe.wait_ge(split_lo, PAIRS_PER_QUAD * qd + ahead // PAIR + 1)
                    up(pe, b, QUAD * qd + ahead, ahead)
                elif not end:
                    up(pe, b + 1, ahead - QUAD, ahead)
                down(pe, b, qd, j, tail and j == QUAD - 1)

        def tensor_start(pe, b):
            pe.wait_ge(o_ready, done(b - 1))
            pe.matmul(y[:, 0:T], b2_hi[:], tokens(comb, b), start=True, stop=False)
            pe.matmul(y[:, 0:T], b2_lo[:], tokens(comb, b), start=False, stop=False)

        def turn_back(pe, b):
            pe.wait_ge(o_ready, done(b))
            pe.wait_ge(rows_ready, done(b - 1))
            for i, (a, z) in enumerate(OUT_TILES):
                last = pe.transpose(turned[0:z, i * P:(i + 1) * P], o_T[:, a:a + z], ident[:])
            last.then_inc(o_flipped, 1)

        def gelu(act, b, e, j):
            n = EXPERTS * b + e
            act.wait_ge(m_ready, done(n - 2))
            for h in range(HALVES):
                act.wait_ge(up_ready[h], done(n))
                act.activation(g[j % 2][:, h, :], up_bank[h][:, 0:T], ACT.Gelu, scale=1 / (XSCALE * WSCALE),
                               bias=b1_T[:, bass.ds(HALVES * e + h, 1)]).then_inc(gelu_done, 1)

        def high(act, n, j):
            act.wait_ge(m_ready, done(n))
            act.wait_ge(down_done, done(n - QUAD))
            act.copy(m_hi[j][:], m[j % 2][:]).then_inc(hi_ready, 1)

        def split_low(dve, pair, i):
            dve.wait_ge(split_hi, pair + 1)
            cols = bass.ds(pair * PAIR * COLS, PAIR * COLS)
            dve.scalar_tensor_tensor(out=w_lo[:, cols], in0=stage[i][:], scalar=WSCALE,
                                     in1=w_hi[:, cols], op0=ALU.mult, op1=ALU.subtract).then_inc(split_lo, 1)

        def scalar_quad(act, b, qd, first, tail, end, between=None):
            for j in range(QUAD):
                n = EXPERTS * b + QUAD * qd + j
                gelu(act, b, QUAD * qd + j, j)
                if not (first and isinstance(qd, int) and qd == 0 and j == 0):
                    high(act, n - 1, (j - 1) % QUAD)
                if first and not tail and j % PAIR == 0:
                    i = j // PAIR
                    act.wait_ge(stage_in[i], 32 * (qd + 2))
                    split_high_cols(act, PAIRS_PER_QUAD * (qd + 1) + i, i)
                if between and j == 1:
                    between()
            if end:
                high(act, n, QUAD - 1)

        def split_high_cols(act, pair, i):
            act.activation(w_hi[:, bass.ds(pair * PAIR * COLS, PAIR * COLS)],
                           stage[i][:], ACT.Copy, scale=WSCALE).then_inc(split_hi, 1)

        def weigh(dve, b, qd, j):
            n = EXPERTS * b + QUAD * qd + j
            dve.wait_ge(gelu_done, done(2 * n + 1))
            dve.wait_ge(cast_ready, done(n))
            dve.wait_ge(hi_ready, done(n - 2))
            if j >= 2:
                wait_lo(dve, QUADS * b + qd, j - 2)
            else:
                wait_lo(dve, QUADS * b + qd, j + 2, back=1)
            dve.tensor_tensor(m[j % 2][:], g[j % 2][:],
                              cast[j % 2][:, 0:T].unsqueeze(1).broadcast_to([P, HALVES, T]), ALU.mult).then_inc(m_ready, 1)

        def low(eng, n, j):
            eng.wait_ge(hi_ready, done(n))
            eng.wait_ge(down_done, done(n - QUAD))
            eng.tensor_tensor(m_lo[j][:], m[j % 2][:], m_hi[j][:], ALU.subtract).then_inc(lo_ready[LO_ON[j]], 1)

        def vector_quad(dve, b, qd, first, tail, end, between=None):
            for j in range(QUAD):
                n = EXPERTS * b + QUAD * qd + j
                weigh(dve, b, qd, j)
                if LO_ON[(j - 1) % QUAD] == "dve" and not (first and isinstance(qd, int) and qd == 0 and j == 0):
                    low(dve, n - 1, (j - 1) % QUAD)
                if first and not tail and j % PAIR == 0:
                    split_low(dve, PAIRS_PER_QUAD * (qd + 1) + j // PAIR, j // PAIR)
                if between and j == 1:
                    between()
            if end and LO_ON[QUAD - 1] == "dve":
                low(dve, n, QUAD - 1)

        def gpsimd_quad(pool, b, qd, first, tail, end, between=None):
            for j in range(QUAD):
                if LO_ON[j] == "pool":
                    low(pool, EXPERTS * b + QUAD * qd + j, j)

        def sequence(eng, quad, b, first=False, end=False, between=None):
            quad(eng, b, 0, first, False, False, between)
            with eng.Fori(1, QUADS - 1) as qd:
                quad(eng, b, qd, first, False, False)
            quad(eng, b, QUADS - 1, first, True, end)

        def load_pair(sp, pair, i):
            ups = stage[i][:, 0:PAIR * HIDDEN].rearrange("p (e n) -> p e n", n=HIDDEN)
            downs = stage[i][:, PAIR * HIDDEN:PAIR * COLS].rearrange("p (c d) -> p c d", d=DIM)
            sp.dma_start(ups, w1.rearrange("e p n -> p e n")[:, bass.ds(pair * PAIR, PAIR), :]).then_inc(stage_in[i], 16)
            sp.dma_start(downs, w2.rearrange("e (h p) d -> p (e h) d", p=P)[:, bass.ds(pair * PAIR * HALVES, PAIR * HALVES), :]
                         ).then_inc(stage_in[i], 16)

        block = ctx.enter_context(nc.Block())

        @block.sync
        def _(sp):
            sp.sem_inc(stored, BIAS)
            for i in range(PAIRS_PER_QUAD):
                load_pair(sp, i, i)
            sp.dma_start(b1_rows[:], b1.rearrange("e (h p) -> (e h) p", p=P)).then_inc(small_in, 16)
            for i in range(2):
                sp.dma_start(b2_in[i * EXPERTS:(i + 1) * EXPERTS, :], b2).then_inc(small_in, 16)
            with sp.Fori(1, QUADS) as qd:
                for i in range(PAIRS_PER_QUAD):
                    sp.wait_ge(split_lo, PAIRS_PER_QUAD * (qd - 1) + i + 1)
                    load_pair(sp, PAIRS_PER_QUAD * qd + i, i)
            rows = out.rearrange("b t d -> (b t) d")
            with sp.Fori(0, SEQS) as b:
                sp.wait_ge(rows_ready, done(b))
                sp.dma_start(rows[bass.ds(b * T, 2 * P), :].rearrange("(n p) d -> p n d", p=P), o_rows[:, 0:2, :]
                             ).then_inc(stored, 16)
                sp.dma_start(rows[bass.ds(b * T + 2 * P, T - 2 * P), :], o_rows[0:T - 2 * P, 2, :]).then_inc(stored, 16)
            sp.wait_ge(stored, 16 * STORES * SEQS + BIAS)

        @block.gpsimd
        def _(pool):
            pool.sem_inc(lo_ready["pool"], BIAS)
            pool.memset(sel_raw[:], 0.0).then_inc(sel_zeroed, 1)
            for i in range(2):
                pool.wait_ge(sel_zeroed if i == 0 else sel_made, 1)
                pool.affine_select(out=sel_raw[:], in_=sel_raw[:], compare_op=ALU.not_equal, fill=SELSCALE,
                                   base=-(EXPERTS - 1) - EXPERTS * i, pattern=[[1, EXPERTS]], channel_multiplier=1
                                   ).then_inc(sel_made, 1)
            pool.wait_ge(sel_made, 2)
            pool.tensor_copy(sel[:], sel_raw[:]).then_inc(sel_ready, 1)
            sequence(pool, gpsimd_quad, 0, first=True)
            with pool.Fori(1, SEQS - 1) as b:
                sequence(pool, gpsimd_quad, b)
            sequence(pool, gpsimd_quad, SEQS - 1, end=True)

        @block.tensor
        def _(pe):
            for s in (*up_ready, cast_ready, down_done, y_summed, o_flipped):
                pe.sem_inc(s, BIAS)
            pe.wait_ge(small_in, 48)
            pe.transpose(turned[:, 0:P], b1_rows[:], ident[:]).then_inc(b1_flipped, 1)
            pe.wait_ge(sel_ready, 1)
            pe.wait_ge(b2_ready, 1)
            pe.wait_ge(split_lo, 1)
            for e in range(LAG):
                up(pe, 0, e, e)
            tensor_start(pe, 0)
            sequence(pe, tensor_quad, 0, first=True)
            with pe.Fori(1, SEQS - 1) as b:
                tensor_start(pe, b)
                turn_back(pe, b - 1)
                sequence(pe, tensor_quad, b)
            tensor_start(pe, SEQS - 1)
            turn_back(pe, SEQS - 2)
            sequence(pe, tensor_quad, SEQS - 1, end=True)
            turn_back(pe, SEQS - 1)

        @block.scalar
        def _(act):
            def copy_rows(b):
                act.wait_ge(o_flipped, done(b))
                act.wait_ge(stored, 16 * STORES * b + BIAS)
                act.copy(o_rows[:, 0:2, :], turned[:, 0:2 * P].rearrange("p (n d) -> p n d", d=P))
                act.copy(o_rows[0:T - 2 * P, 2, :], turned[0:T - 2 * P, 2 * P:3 * P]).then_inc(rows_ready, 1)

            for s in (gelu_done, hi_ready, rows_ready):
                act.sem_inc(s, BIAS)
            for i in range(PAIRS_PER_QUAD):
                act.wait_ge(stage_in[i], 32)
                split_high_cols(act, i, i)
            act.wait_ge(b1_flipped, 1)
            act.copy(b1_T[:], turned[:, 0:P]).then_inc(b1_ready, 1)
            act.wait_ge(small_in, 48)
            act.copy(b2_hi[:], b2_in[:]).then_inc(b2_hi_ready, 1)
            act.wait_ge(b1_ready, 1)
            sequence(act, scalar_quad, 0, first=True)
            with act.Fori(1, SEQS - 1) as b:
                sequence(act, scalar_quad, b, between=lambda: copy_rows(b - 1))
            sequence(act, scalar_quad, SEQS - 1, end=True, between=lambda: copy_rows(SEQS - 2))
            copy_rows(SEQS - 1)

        @block.vector
        def _(dve):
            def add_up(b):
                dve.wait_ge(y_summed, done(b))
                dve.wait_ge(o_flipped, done(b - 1))
                dve.scalar_tensor_tensor(out=o_T[:], in0=y[:, 0:T], scalar=1 / CSCALE, in1=tokens(hT, b),
                                         op0=ALU.mult, op1=ALU.add).then_inc(o_ready, 1)

            for s in (m_ready, lo_ready["dve"], o_ready):
                dve.sem_inc(s, BIAS)
            for i in range(PAIRS_PER_QUAD):
                split_low(dve, i, i)
            dve.wait_ge(b2_hi_ready, 1)
            dve.tensor_tensor(b2_lo[:], b2_in[:], b2_hi[:], ALU.subtract).then_inc(b2_ready, 1)
            sequence(dve, vector_quad, 0, first=True)
            with dve.Fori(1, SEQS - 1) as b:
                sequence(dve, vector_quad, b, between=lambda: add_up(b - 1))
            sequence(dve, vector_quad, SEQS - 1, end=True, between=lambda: add_up(SEQS - 2))
            add_up(SEQS - 1)


_INS = ["x", "L0_tok_W", "L0_tok_b", "L0_tok_gamma", "L0_tok_beta", "L0_attn_in_proj_w", "L0_attn_x_proj_w",
        "L0_attn_dt_w", "L0_attn_dt_b", "L0_attn_conv_w", "L0_attn_conv_b", "L0_attn_A_log", "L0_attn_D_param",
        "L0_attn_out_w", "L0_attn_ln_g", "L0_attn_ln_b", "L0_ffn_w1", "L0_ffn_b1", "L0_ffn_w2", "L0_ffn_b2",
        "L0_ffn_router_w", "L0_ffn_router_b"]

_COLUMNS = ["L0_tok_b", "L0_tok_gamma", "L0_tok_beta", "L0_attn_dt_b", "L0_attn_conv_b", "L0_attn_D_param",
            "L0_attn_ln_g", "L0_attn_ln_b"]


def kernel(**inputs):
    import concourse.bacc as _bacc
    from concourse.bass_utils import run_bass_kernel_spmd as _run

    nc = _bacc.Bacc("TRN2", target_bir_lowering=False, num_devices=1)
    arrays, args = {}, []
    for name in _INS:
        a = np.ascontiguousarray(inputs[name])
        if name in ("L0_ffn_router_w", "L0_ffn_router_b", "L0_ffn_b2"):
            axis = 0 if name == "L0_ffn_b2" else a.ndim - 1
            a = np.ascontiguousarray(np.flip(a, axis=axis))
        if name in _COLUMNS:
            a = np.ascontiguousarray(a.reshape(-1, P).T)
        if name == "L0_attn_dt_w":
            a = a.reshape(1, -1)
        arrays[f"in_{name}_dram"] = a
        args.append(nc.dram_tensor(f"in_{name}_dram", a.shape, mybir.dt.from_np(a.dtype), kind="ExternalInput").ap())
    result = nc.dram_tensor("out_0_dram", (SEQS, T, DIM), F32, kind="ExternalOutput").ap()
    build(nc, *args, result)
    r = _run(nc, [arrays], core_ids=[0])
    return r.results[0]["out_0_dram"]
```

```python
from contextlib import ExitStack

import numpy as np

import concourse.bass as bass
from concourse import mybir

F32 = mybir.dt.float32
F16 = mybir.dt.float16
BF16 = mybir.dt.bfloat16
ALU = mybir.AluOpType
ACT = mybir.ActivationFunctionType
AX = mybir.AxisListType

P = 128
SEQS, FRAMES, DIM = 8, 375, 128
TAPS = 5
T = FRAMES - TAPS + 1
TOKENS = SEQS * T
INNER, HALVES = 256, 2
STATES = 16
EXPERTS, HIDDEN, TOPK = 64, 256, 42
EPS = 1e-5
BIAS = 32
A_LOG_CAP = 84.0

ROWS = SEQS * FRAMES
ROW_TILES = -(-ROWS // P)
LAST_ROWS = ROWS - (ROW_TILES - 1) * P

ROUTE_AT = [0, P, T - P]
OUT_TILES = [(0, P), (P, P), (2 * P, T - 2 * P)]
ROUNDS = -(-(EXPERTS - TOPK) // 8)
SENTINELS = 8 * ROUNDS - (EXPERTS - TOPK)
QCOLS = EXPERTS + SENTINELS

GROUP = 8
GROUPS = EXPERTS // GROUP
BLOCKS = GROUP * HIDDEN // P
GROUP_COLS = GROUP * HIDDEN
STAGE_COLS = GROUP_COLS // 2

TOWER_IN = 16 * 13
FIRST_IN = 16 * 5

XSCALE, WSCALE = 16.0, 16.0
CSCALE = 1024.0
SELSCALE = 1.0 / 16.0

def _series():
    f = lambda v: 2 * np.arctanh(np.sqrt(v + 1e-30)) / np.sqrt(v + 1e-30)
    c = np.polynomial.chebyshev.Chebyshev.interpolate(f, 4, domain=[0, 1 / 9]).convert(kind=np.polynomial.Polynomial)
    pairs = [(-float(r.real), float(r.imag) ** 2) for r in c.roots() if r.imag > 0]
    return float(c.coef[4]), pairs


LEADING, FACTORS = _series()


def done(turn):
    return turn + 1 + BIAS


def build(nc, x, tok_w, tok_b, gamma, beta, in_w, xproj_w, dt_w, dt_b, conv_w, conv_b, a_log, d_par,
          out_w, ln_g, ln_b, w1, b1, w2, b2, router_w, router_b, out):
    with ExitStack() as kept:
        def keep(name, shape, dt=F32):
            return kept.enter_context(nc.sbuf_tensor(name, shape, dt))

        hT = keep("hT", [P, TOKENS])
        ident = keep("ident", [P, P])
        ones_ln = keep("ones_ln", [P, P])
        x_hi = keep("x_hi", [P, TOKENS], F16)
        x_lo = keep("x_lo", [P, TOKENS], F16)
        comb = keep("comb", [P, TOKENS], F16)
        tower_in = kept.enter_context(nc.semaphore("tower_in"))
        experts_in = kept.enter_context(nc.semaphore("experts_in"))
        kept.callback(clear, nc, [tower_in, experts_in])
        stage = [keep(f"stage{i}", [P, STAGE_COLS]) for i in range(2)]
        b1_T = keep("b1_T", [P, EXPERTS * HIDDEN // P])
        b2_in = keep("b2_in", [P, DIM])
        expert_loads = [
            *(weight_load(stage, w1, w2, 0, 0, i) for i in range(2)),
            (b1_T[:].rearrange("p (q k) -> p q k", k=BLOCKS),
             b1.rearrange("(q i) (r k) -> (i r) q k", i=GROUP, k=BLOCKS)),
            *((b2_in[i * EXPERTS:(i + 1) * EXPERTS, :], b2) for i in range(2)),
        ]
        assert len(expert_loads) * 16 == FIRST_IN
        with ExitStack() as for_tower:
            def keep_for_tower(name, shape):
                return for_tower.enter_context(nc.sbuf_tensor(name, shape, F32))

            weights = {
                "in_rows": keep_for_tower("in_rows", [P, 4, DIM]),
                "xp_rows": keep_for_tower("xp_rows", [1 + 2 * STATES, INNER]),
                "out_rows": keep_for_tower("out_rows", [P, INNER]),
                "a_raw": keep_for_tower("a_raw", [P, HALVES, STATES]),
                "taps": keep_for_tower("taps", [P, HALVES, 3]),
                "vec": keep_for_tower("vec", [P, 5, HALVES]),
                "dt_row": keep_for_tower("dt_row", [1, INNER]),
                "rw": keep_for_tower("rw", [P, EXPERTS]),
                "rb": keep_for_tower("rb", [1, EXPERTS]),
            }
            tower_loads = [
                (weights["in_rows"][:], in_w.rearrange("(n p) d -> p n d", p=P)),
                (weights["xp_rows"][:], xproj_w),
                (weights["out_rows"][:], out_w),
                (weights["a_raw"][:], a_log.rearrange("(h p) s -> p h s", p=P)),
                (weights["taps"][:], conv_w.rearrange("(h p) a k -> p h (a k)", p=P)),
                *((weights["vec"][:, i, :], v) for i, v in enumerate((conv_b, dt_b, d_par, ln_g, ln_b))),
                (weights["dt_row"][:], dt_w),
                (weights["rw"][:], router_w),
                (weights["rb"][:], router_b.rearrange("(a e) -> a e", a=1)),
            ]
            assert len(tower_loads) * 16 == TOWER_IN
            front(nc, kept, hT, ident, ones_ln, x, tok_w, tok_b, gamma, beta,
                  [(dst, src, tower_in) for dst, src in tower_loads] + [(dst, src, experts_in) for dst, src in expert_loads])
            tower(nc, hT, ident, ones_ln, x_hi, x_lo, comb, weights, tower_in)
        experts(nc, hT, ident, x_hi, x_lo, comb, (stage, b1_T, b2_in), experts_in, w1, w2, out)


def weight_load(stage, w1, w2, g, layer, i):
    if layer == 0:
        half = GROUP // 2
        return (stage[i][:].rearrange("p (e n) -> p e n", n=HIDDEN),
                w1.rearrange("e p n -> p e n")[:, bass.ds(GROUP * g + half * i, half), :])
    return (stage[i][:],
            w2.rearrange("(q i) (r k) d -> (i r) q (k d)", i=GROUP, k=BLOCKS)
            [:, bass.ds(g, 1), i * STAGE_COLS:(i + 1) * STAGE_COLS].rearrange("p a n -> p (a n)"))


def clear(nc, sems):
    nums = sorted(s.num for s in sems)
    first = nums[0]
    for at, num in enumerate(nums):
        if at + 1 == len(nums) or nums[at + 1] != num + 1:
            nc.gpsimd.sem_clear(range(first, num + 1))
            first = nums[min(at + 1, len(nums) - 1)]
    nc.all_engine_barrier()


def front(nc, kept, hT, ident, ones_ln, x, tok_w, tok_b, gamma, beta, later_loads):
    sems = []
    with ExitStack() as ctx:
        ctx.callback(clear, nc, sems)

        def sb(name, shape, dt=F32):
            return ctx.enter_context(nc.sbuf_tensor(name, shape, dt))

        def sem(name):
            sems.append(ctx.enter_context(nc.semaphore(name)))
            return sems[-1]

        rows = sb("rows", [P, ROW_TILES, DIM])
        wrow = sb("wrow", [P, TAPS * DIM])
        xT = sb("xT", [P, ROW_TILES * P])
        wT = sb("wT", [P, TAPS, P])
        vecs = sb("vecs", [P, 3])
        stats = sb("stats", [P, SEQS, 6])
        mv = sb("mv", [P, 2])
        rstd = sb("rstd", [P, 1])
        gain = sb("gain", [P, 1])
        veps, lnv, r0, r0sq, newton = (sb(n, [P, 1]) for n in ("veps", "lnv", "r0", "r0sq", "newton"))
        flip = [ctx.enter_context(nc.psum_tensor(f"flip{i}", [P, 4, P], F32)) for i in range(2)]
        conv = [ctx.enter_context(nc.psum_tensor(f"conv{i}", [P, 512], F32)) for i in range(4)]

        x_in = [sem(f"x_in{i}") for i in range(4)]
        w_in, vecs_in = sem("w_in"), sem("vecs_in")
        zeroed, ident_ready, ones_ready = sem("zeroed"), sem("ident_ready"), sem("ones_ready")
        flipped, flip_copied = sem("flipped"), sem("flip_copied")
        conv_ready, y_ready, stats_ready = sem("conv_ready"), sem("y_ready"), sem("stats_ready")
        moments_ready, rstd_ready, gain_ready = sem("moments_ready"), sem("rstd_ready"), sem("gain_ready")
        veps_ready, ln_taken, r0_ready, r0_squared, newton_ready = (
            sem(n) for n in ("veps_ready", "ln_taken", "r0_ready", "r0_squared", "newton_ready"))
        scaled, normed = sem("scaled"), sem("normed")

        x_rows = x.rearrange("b t d -> (b t) d")
        GROUPS = -(-ROW_TILES // 4)
        WGROUPS = -(-TAPS // 4)
        load_tiles = [(0, 4), (4, 12), (12, ROW_TILES - 1)]

        block = ctx.enter_context(nc.Block())

        @block.sync
        def _(sp):
            sp.dma_start(wrow[:], tok_w).then_inc(w_in, 16)
            for i, (a, z) in enumerate(load_tiles):
                sp.dma_start(rows[:, a:z, :], x_rows[a * P:z * P, :].rearrange("(n p) d -> p n d", p=P)
                             ).then_inc(x_in[i], 16)
            sp.dma_start(rows[0:LAST_ROWS, ROW_TILES - 1, :], x_rows[(ROW_TILES - 1) * P:ROWS, :]).then_inc(x_in[3], 16)
            for i, v in enumerate((tok_b, gamma, beta)):
                sp.dma_start(vecs[:, i:i + 1], v).then_inc(vecs_in, 16)
            for dst, src, into in later_loads:
                sp.dma_start(dst, src).then_inc(into, 16)

        @block.gpsimd
        def _(pool):
            pool.memset(ident[:], 0.0).then_inc(zeroed, 1)
            pool.wait_ge(zeroed, 1)
            pool.affine_select(out=ident[:], in_=ident[:], compare_op=ALU.not_equal, fill=1.0, base=0,
                               pattern=[[-1, P]], channel_multiplier=1).then_inc(ident_ready, 1)
            pool.memset(ones_ln[:], 1.0 / DIM).then_inc(ones_ready, 1)

        @block.tensor
        def _(pe):
            pe.wait_ge(ident_ready, 1)
            pe.wait_ge(w_in, 16)
            for g in range(WGROUPS):
                for k in range(4 * g, min(4 * g + 4, TAPS)):
                    last = pe.transpose(flip[g % 2][:, k % 4, :], wrow[:, k * DIM:(k + 1) * DIM], ident[:])
                last.then_inc(flipped, 1)
            for g in range(GROUPS):
                pe.wait_ge(flip_copied, g + WGROUPS - 1)
                for n in range(4 * g, min(4 * g + 4, ROW_TILES)):
                    for i, (a, _z) in enumerate(load_tiles):
                        if n == a:
                            pe.wait_ge(x_in[i], 16)
                    if n < ROW_TILES - 1:
                        last = pe.transpose(flip[(g + WGROUPS) % 2][:, n % 4, :], rows[:, n, :], ident[:])
                    else:
                        pe.wait_ge(x_in[3], 16)
                        last = pe.transpose(flip[(g + WGROUPS) % 2][:, n % 4, 0:LAST_ROWS],
                                            rows[0:LAST_ROWS, n, :], ident[0:LAST_ROWS, 0:LAST_ROWS])
                last.then_inc(flipped, 1)
            for b in range(SEQS):
                need = -(-((b + 1) * FRAMES) // (4 * P))
                pe.wait_ge(flip_copied, WGROUPS + need)
                if b >= 4:
                    pe.wait_ge(y_ready, b - 3)
                for k in range(TAPS):
                    last = pe.matmul(conv[b % 4][:, 0:T], wT[:, k, :], xT[:, b * FRAMES + k:b * FRAMES + k + T],
                                     start=(k == 0), stop=(k == TAPS - 1))
                last.then_inc(conv_ready, 1)

        @block.scalar
        def _(act):
            act.preload_act_table_set("natural_log_exp_and_others")
            for g in range(WGROUPS):
                n = min(4, TAPS - 4 * g)
                act.wait_ge(flipped, g + 1)
                act.copy(wT[:, 4 * g:4 * g + n, :], flip[g % 2][:, 0:n, :]).then_inc(flip_copied, 1)
            for g in range(GROUPS):
                act.wait_ge(flipped, g + 1 + WGROUPS)
                z = min(4 * P, ROWS - 4 * P * g)
                act.copy(xT[:, 4 * P * g:4 * P * g + z],
                         flip[(g + WGROUPS) % 2][:].rearrange("p a b -> p (a b)")[:, 0:z]).then_inc(flip_copied, 1)
            act.wait_ge(vecs_in, 48)
            for b in range(SEQS):
                act.wait_ge(conv_ready, b + 1)
                act.activation(hT[:, b * T:(b + 1) * T], conv[b % 4][:, 0:T], ACT.Identity,
                               bias=vecs[:, 0:1]).then_inc(y_ready, 1)
            act.wait_ge(veps_ready, 1)
            act.activation(lnv[:], veps[:], ACT.Ln).then_inc(ln_taken, 1)
            act.wait_ge(ln_taken, 1)
            act.activation(r0[:], lnv[:], ACT.Exp, scale=-0.5).then_inc(r0_ready, 1)
            act.wait_ge(r0_ready, 1)
            act.activation(r0sq[:], r0[:], ACT.Square).then_inc(r0_squared, 1)
            for b in range(SEQS):
                act.wait_ge(scaled, b + 1)
                act.activation(hT[:, b * T:(b + 1) * T], hT[:, b * T:(b + 1) * T], ACT.Relu,
                               bias=vecs[:, 2:3]).then_inc(normed, 1)

        @block.vector
        def _(dve):
            for b in range(SEQS):
                dve.wait_ge(y_ready, b + 1)
                dve.bn_stats(stats[:, b, :], hT[:, b * T:(b + 1) * T]).then_inc(stats_ready, 1)
            dve.wait_ge(stats_ready, SEQS)
            dve.bn_aggr(mv[:], stats[:].rearrange("p b s -> p (b s)")).then_inc(moments_ready, 1)
            dve.wait_ge(moments_ready, 1)
            dve.tensor_scalar(veps[:], mv[:, 1:2], EPS, None, ALU.add).then_inc(veps_ready, 1)
            dve.wait_ge(r0_squared, 1)
            dve.wait_ge(veps_ready, 1)
            dve.tensor_tensor(newton[:], r0sq[:], veps[:], ALU.mult).then_inc(newton_ready, 1)
            dve.wait_ge(newton_ready, 1)
            dve.tensor_scalar(newton[:], newton[:], -0.5, 1.5, ALU.mult, ALU.add).then_inc(newton_ready, 1)
            dve.wait_ge(newton_ready, 2)
            dve.tensor_tensor(rstd[:], newton[:], r0[:], ALU.mult).then_inc(rstd_ready, 1)
            dve.wait_ge(rstd_ready, 1)
            dve.wait_ge(vecs_in, 48)
            dve.tensor_tensor(gain[:], rstd[:], vecs[:, 1:2], ALU.mult).then_inc(gain_ready, 1)
            dve.wait_ge(gain_ready, 1)
            for b in range(SEQS):
                s = hT[:, b * T:(b + 1) * T]
                dve.tensor_scalar(s, s, mv[:, 0:1], gain[:, 0:1], ALU.subtract, ALU.mult).then_inc(scaled, 1)


def tower(nc, hT, ident, ones_ln, x_hi, x_lo, comb, weights, tower_in):
    sems = []
    with ExitStack() as ctx:
        ctx.callback(clear, nc, sems)

        def sb(name, shape, dt=F32):
            return ctx.enter_context(nc.sbuf_tensor(name, shape, dt))

        def bank(name, shape=(P, 512)):
            return ctx.enter_context(nc.psum_tensor(name, list(shape), F32))

        in_rows, xp_rows, out_rows, a_raw, taps, vec, dt_row, rw, rb = (
            weights[n] for n in ("in_rows", "xp_rows", "out_rows", "a_raw", "taps", "vec", "dt_row", "rw", "rb"))
        tap_rows = sb("tap_rows", [P, 3, HALVES, DIM])
        in_T = sb("in_T", [P, 3, HALVES, P])
        z_T = sb("z_T", [P, HALVES, P])
        xp_T = sb("xp_T", [P, HALVES, P])
        out_T = sb("out_T", [P, HALVES, P])
        out_gT = sb("out_gT", [P, HALVES, P])
        out_bias = sb("out_bias", [P, 1])
        a_capped = sb("a_capped", [P, HALVES, STATES])
        a_exp = sb("a_exp", [P, HALVES, STATES])
        a_neg = sb("a_neg", [P, HALVES, STATES])
        ones_row = sb("ones_row", [1, P])
        rw_half = sb("rw_half", [P, EXPERTS])
        ones_inner = sb("ones_inner", [P, P])
        pick_raw = sb("pick_raw", [P, 2 * STATES])
        pick = sb("pick", [P, 2 * STATES], BF16)

        cen1, sq1, rs1 = (sb(n, [P, T]) for n in ("cen1", "sq1", "rs1"))
        xn1 = sb("xn1", [P, T + 2])
        d_row = sb("d_row", [1, T])
        rest = sb("rest", [P, T])
        dt_pos, dt_abs, dt_exp, dt_rec, dt_s, dt_s2 = (
            sb(n, [P, HALVES, T]) for n in ("dt_pos", "dt_abs", "dt_exp", "dt_rec", "dt_s", "dt_s2"))
        dt_quad = [sb(f"dt_quad{i}", [P, HALVES, T]) for i in range(2)]
        xc = [sb(f"xc{i}", [P, HALVES, T]) for i in range(2)]
        zg = [sb(f"zg{i}", [P, HALVES, T]) for i in range(2)]
        bc = [sb(f"bc{i}", [P, T], BF16) for i in range(2)]
        delta = [sb(f"delta{i}", [P, HALVES, T]) for i in range(2)]
        dx = [sb(f"dx{i}", [P, HALVES, T]) for i in range(2)]
        DEEP, CAST_AHEAD, AHEAD, LAG = 4, 2, 2, 2
        dA = [sb(f"dA{i}", [P, HALVES, T]) for i in range(DEEP)]
        bx = [sb(f"bx{i}", [P, HALVES, T]) for i in range(2)]
        hs = [sb(f"hs{i}", [P, HALVES, T]) for i in range(DEEP)]
        cs = [sb(f"cs{i}", [P, T]) for i in range(DEEP)]
        hc = [sb(f"hc{i}", [P, HALVES, T]) for i in range(DEEP)]
        yb, yz, cen2, sq2, yn = (sb(n, [P, HALVES, T]) for n in ("yb", "yz", "cen2", "sq2", "yn"))
        rs2, cen3, sq3, rs3, xn3 = (sb(n, [P, T]) for n in ("rs2", "cen3", "sq3", "rs3", "xn3"))
        eps, two = sb("eps", [P, 1]), sb("two", [P, 1])
        shift = [sb(f"shift{i}", [P, 1]) for i in range(2)]
        lnv, r0, r0sq, newton = (
            {i: sb(f"{n}{i}", [P, T]) for i in (1, 2, 3)} for n in ("lnv", "r0_", "r0sq", "newton"))
        top, ssum, srec, wsum, wrec = (sb(n, [P, 3]) for n in ("top", "ssum", "srec", "wsum", "wrec"))
        lg, ex, ew, wm = (sb(n, [P, 3, EXPERTS]) for n in ("lg", "ex", "ew", "wm"))
        qn = sb("qn", [P, 3, QCOLS])
        low8 = sb("low8", [P, 3, 8])
        cw = sb("cw", [P, 3, 2, EXPERTS])

        bank_b = [bank(f"bank_b{i}") for i in range(2)]
        bank_c = bank("bank_c")
        ysum = [bank(f"ysum{i}") for i in range(HALVES)]
        pre = [bank(f"pre{i}") for i in range(2)]
        post = bank("post")

        def sem(name):
            sems.append(ctx.enter_context(nc.semaphore(name)))
            return sems[-1]

        xp_zeroed, inner_ready, row_ready, pick_zeroed, pick_made, pick_ready = (
            sem(n) for n in ("xp_zeroed", "inner_ready", "row_ready", "pick_zeroed", "pick_made", "pick_ready"))
        tap_rows_ready, rw_ready = sem("tap_rows_ready"), sem("rw_ready")
        eps_ready, waited = sem("eps_ready"), sem("waited")
        zero_ready, a_capped_ready, a_exp_ready, a_neg_ready = (
            sem(n) for n in ("zero_ready", "a_capped_ready", "a_exp_ready", "a_neg_ready"))
        in_flipped, xp_flipped, out_flipped = sem("in_flipped"), sem("xp_flipped"), sem("out_flipped")
        in_copied, xp_copied, out_copied = sem("in_copied"), sem("xp_copied"), sem("out_copied")
        bias_summed, bias_ready = sem("bias_summed"), sem("bias_ready")
        pe_events = {n: sem(n) for n in (
            "mean1", "var1", "xin_ready", "z_ready", "dbc_ready", "dt_ready", "b_cast", "c_cast",
            "summed", "ysum_ready", "mean2", "var2", "proj_ready", "mean3", "var3", "logits_ready",
            "comb_flipped")}
        act_events = {n: sem(n) for n in (
            "sq1_ready", "xc_ready", "zg_ready", "drow_ready", "dtabs_ready", "dtexp_ready", "dtln_ready",
            "dtrec_ready", "dts2_ready", "dtquad_ready", "dA_ready", "c_copied", "sq2_ready", "sq3_ready", "xhi_ready", "ex_ready",
            "ew_ready", "comb_hi_ready", "bc_hi_ready", "bc_mid_ready",
            *(f"{n}{i}" for n in ("ln_taken", "r0_ready", "r0_squared") for i in (1, 2, 3)))}
        dve_events = {n: sem(n) for n in (
            "cen1_ready", "rs1_ready", "xn1_ready", "rest_ready", "series_done", "delta_ready", "bx_ready", "scan_done",
            "y_ready2", "cen2_ready", "rs2_ready", "h_ready", "cen3_ready", "rs3_ready", "xn3_ready",
            "xlo_ready", "top_ready", "lg_ready", "ssum_ready", "srec_ready", "nsrec_ready", "qn_ready",
            "low_found", "low_dropped", "wm_ready", "wsum_ready", "wrec_ready", "bc_ready", "cw_ready", "comb_ready",
            *(f"vr_ready{i}" for i in (1, 2, 3)))}
        pool_events = {n: sem(n) for n in (
            "dts_ready", "dx_ready", "hc_ready",
            "gated", "yn_ready")}
        ev = {**pe_events, **act_events, **dve_events, **pool_events}

        def tokens(buf, b, at=0, n=T, parts=slice(0, P)):
            return buf[parts, bass.ds(b * T + at, n)]

        def over_halves(ap):
            return ap.unsqueeze(1).broadcast_to([P, HALVES, T])

        def over_experts(ap):
            return ap.unsqueeze(2).broadcast_to([P, 3, EXPERTS])

        NS = STATES

        def wait_apart(eng, event, value):
            eng.wait_ge(ev[event], value)
            eng.sem_inc(waited, 1)

        def rsqrt_scalar(act, i, b, var):
            act.wait_ge(ev[f"var{i}"], done(b))
            act.wait_ge(ev[f"rs{i}_ready"], done(b - 1))
            act.activation(lnv[i][:], var, ACT.Ln, bias=eps[:]).then_inc(ev[f"ln_taken{i}"], 1)
            act.wait_ge(ev[f"ln_taken{i}"], done(b))
            act.activation(r0[i][:], lnv[i][:], ACT.Exp, scale=-0.5).then_inc(ev[f"r0_ready{i}"], 1)
            act.wait_ge(ev[f"r0_ready{i}"], done(b))
            act.activation(r0sq[i][:], r0[i][:], ACT.Square).then_inc(ev[f"r0_squared{i}"], 1)

        def rsqrt_vector(dve, i, b, var, rs):
            dve.wait_ge(ev[f"r0_squared{i}"], done(b))
            dve.scalar_tensor_tensor(out=newton[i][:], in0=var, scalar=EPS, in1=r0sq[i][:],
                                     op0=ALU.add, op1=ALU.mult).then_inc(ev[f"vr_ready{i}"], 1)
            dve.wait_ge(ev[f"vr_ready{i}"], done(b))
            dve.scalar_tensor_tensor(out=rs[:], in0=newton[i][:], scalar=-3.0, in1=r0[i][:],
                                     op0=ALU.add, op1=ALU.mult).then_inc(ev[f"rs{i}_ready"], 1)

        WHEN = {
            "mean1": 0, "center1": 2, "sq1": 5, "var1": 4, "rsqrt1_scalar": 7, "rsqrt1_vector": 9,
            "norm1": 8, "x_in": 10, "silu": 12, "z_in": 11, "dbc": 15, "b_c_high": 16, "b_c_rest": 20,
            "dt": 18, "b_c_mid": 21, "b_c_low": 29, "dt_abs": 20, "dt_exp": 20, "dt_rec": 20, "dt_s": 22,
            "dt_squares": 22, "series1": 27, "series2": 28, "delta": 29, "dx": 27,
            "sum_up": 4, "gate": 3, "mean2": 6, "center2": 8, "sq2": 9, "var2": 9, "rsqrt2_scalar": 10,
            "rsqrt2_vector": 10, "norm2": 10, "out_proj": 11, "residual": 14, "mean3": 12, "center3": 15,
            "sq3": 13, "var3": 13, "rsqrt3_scalar": 14, "rsqrt3_vector": 19, "norm3": 17, "logits": 17,
            "x_high": 23, "x_low": 30, "top": 21, "exp": 18, "probs": 22, "exp_again": 20, "drop1": 24,
            "drop2": 24, "drop3": 25, "weights": 26, "comb_flip": 23, "comb_high": 28, "comb_low": 31,
        }

        def pre_tensor(pe, b, at):
            q = parity(b)
            b = turn(b)
            if at == WHEN["mean1"]:
                pe.wait_ge(ev["dtabs_ready"], done(b - 1))
                pe.matmul(pre[0][:, 0:T], ones_ln[:], tokens(hT, b), start=True, stop=True).then_inc(ev["mean1"], 1)
            if at == WHEN["var1"]:
                pe.wait_ge(ev["sq1_ready"], done(b))
                pe.matmul(pre[1][:, 0:T], ones_ln[:], sq1[:], start=True, stop=True).then_inc(ev["var1"], 1)
            if at == WHEN["x_in"]:
                pe.wait_ge(ev["xn1_ready"], done(b))
                for h in range(HALVES):
                    for i in range(3):
                        last = pe.matmul(pre[h][:, 0:T], in_T[:, i, h, :], xn1[:, i:i + T], start=(i == 0), stop=(i == 2))
                    last.then_inc(ev["xin_ready"], 1)
            if at == WHEN["z_in"]:
                for h in range(HALVES):
                    pe.wait_ge(ev["xc_ready"], done(2 * b + h))
                    pe.matmul(pre[h][:, 0:T], z_T[:, h, :], xn1[:, 1:T + 1], start=True, stop=True
                              ).then_inc(ev["z_ready"], 1)
            if at == WHEN["dbc"]:
                pe.wait_ge(ev["zg_ready"], done(b))
                for h in range(HALVES):
                    last = pe.matmul(pre[0][:, 0:T], xp_T[:, h, :], xc[q][:, h, :], start=(h == 0), stop=(h == 1))
                last.then_inc(ev["dbc_ready"], 1)
            if at == WHEN["dt"]:
                pe.wait_ge(ev["drow_ready"], done(b))
                pe.wait_ge(ev["rest_ready"], done(b))
                for h in range(HALVES):
                    last = pe.matmul(pre[h][:, 0:T], dt_row[0:1, h * P:(h + 1) * P], d_row[0:1, :], start=True, stop=True)
                last.then_inc(ev["dt_ready"], 1)

        def pre_scalar(act, b, at):
            q = parity(b)
            b = turn(b)
            if at == WHEN["sq1"]:
                act.wait_ge(ev["cen1_ready"], done(b))
                act.activation(sq1[:], cen1[:], ACT.Square).then_inc(ev["sq1_ready"], 1)
            if at == WHEN["rsqrt1_scalar"]:
                rsqrt_scalar(act, 1, b, pre[1][:, 0:T])
            if at == WHEN["silu"]:
                act.preload_act_table_set("silu_and_others")
                act.wait_ge(ev["y_ready2"], done(b - 2))
                for h in range(HALVES):
                    act.wait_ge(ev["xin_ready"], done(2 * b + h))
                    act.activation(xc[q][:, h, :], pre[h][:, 0:T], ACT.Silu, bias=vec[:, 0, h:h + 1]
                                   ).then_inc(ev["xc_ready"], 1)
                act.wait_ge(ev["gated"], done(b - 2))
                for h in range(HALVES):
                    act.wait_ge(ev["z_ready"], done(2 * b + h))
                    last = act.activation(zg[q][:, h, :], pre[h][:, 0:T], ACT.Silu)
                last.then_inc(ev["zg_ready"], 1)
                act.preload_act_table_set("natural_log_exp_and_others")
            if at == WHEN["b_c_high"]:
                act.wait_ge(ev["dbc_ready"], done(b))
                act.copy(d_row[0:1, :], pre[0][0:1, 0:T]).then_inc(ev["drow_ready"], 1)
                act.wait_ge(ev["c_cast"], done(NS * (b - 1) - 1))
                act.copy(bc[q][:], pre[0][:, 0:T]).then_inc(ev["bc_hi_ready"], 1)
            if at == WHEN["b_c_mid"]:
                act.wait_ge(ev["rest_ready"], done(b))
                act.copy(bc[q][64:128, :], rest[64:128, :]).then_inc(ev["bc_mid_ready"], 1)
            if at == WHEN["dt_abs"]:
                act.wait_ge(ev["dt_ready"], done(b))
                act.wait_ge(ev["delta_ready"], done(b - 1))
                for h in range(HALVES):
                    act.activation(dt_pos[:, h, :], pre[h][:, 0:T], ACT.Relu, bias=vec[:, 1, h:h + 1])
                    last = act.activation(dt_abs[:, h, :], pre[h][:, 0:T], ACT.Abs, bias=vec[:, 1, h:h + 1])
                last.then_inc(ev["dtabs_ready"], 1)
            if at == WHEN["dt_exp"]:
                act.wait_ge(ev["dtabs_ready"], done(b))
                act.activation(dt_exp[:], dt_abs[:], ACT.Exp, scale=-1.0).then_inc(ev["dtexp_ready"], 1)
            if at == WHEN["dt_rec"]:
                act.wait_ge(ev["dtexp_ready"], done(b))
                act.activation(dt_rec[:], dt_exp[:], ACT.Ln, bias=two[:]).then_inc(ev["dtln_ready"], 1)
                act.wait_ge(ev["dtln_ready"], done(b))
                act.activation(dt_rec[:], dt_rec[:], ACT.Exp, scale=-1.0).then_inc(ev["dtrec_ready"], 1)
            if at == WHEN["dt_squares"]:
                act.wait_ge(ev["dts_ready"], done(b))
                act.activation(dt_s2[:], dt_s[:], ACT.Square).then_inc(ev["dts2_ready"], 1)
                act.wait_ge(ev["dts2_ready"], done(b))
                for i in range(2):
                    last = act.activation(dt_quad[i][:], dt_s2[:], ACT.Square, bias=shift[i][:])
                last.then_inc(ev["dtquad_ready"], 1)

        def pre_vector(dve, b, at):
            q = parity(b)
            b = turn(b)
            if at == WHEN["center1"]:
                dve.wait_ge(ev["mean1"], done(b))
                dve.wait_ge(ev["xn1_ready"], done(b - 1))
                dve.tensor_tensor(cen1[:], tokens(hT, b), pre[0][:, 0:T], ALU.subtract).then_inc(ev["cen1_ready"], 1)
            if at == WHEN["rsqrt1_vector"]:
                dve.wait_ge(ev["xn1_ready"], done(b - 1))
                rsqrt_vector(dve, 1, b, pre[1][:, 0:T], rs1)
            if at == WHEN["b_c_rest"]:
                dve.wait_ge(ev["bc_hi_ready"], done(b))
                dve.tensor_tensor(rest[:], pre[0][:, 0:T], bc[q][:], ALU.subtract).then_inc(ev["rest_ready"], 1)
            if at == WHEN["b_c_low"]:
                dve.wait_ge(ev["bc_mid_ready"], done(b))
                dve.tensor_tensor(bc[q][96:128, :], rest[96:128, :], bc[q][96:128, :], ALU.subtract
                                  ).then_inc(ev["bc_ready"], 1)
            for i, before in enumerate((dt_s, dt_quad[0])):
                if at == WHEN[f"series{i + 1}"]:
                    if i == 0:
                        dve.wait_ge(ev["dtquad_ready"], done(b))
                    else:
                        dve.wait_ge(ev["series_done"], done(2 * b))
                    dve.scalar_tensor_tensor(out=dt_quad[i][:], in0=dt_quad[i][:], scalar=FACTORS[i][1], in1=before[:],
                                             op0=ALU.add, op1=ALU.mult).then_inc(ev["series_done"], 1)
            if at == WHEN["delta"]:
                dve.wait_ge(ev["series_done"], done(2 * b + 1))
                dve.wait_ge(ev["dA_ready"], done(NS * (b - 1) - 1))
                dve.wait_ge(ev["dx_ready"], done(b - 2))
                dve.scalar_tensor_tensor(out=delta[q][:], in0=dt_quad[1][:], scalar=LEADING, in1=dt_pos[:],
                                         op0=ALU.mult, op1=ALU.add).then_inc(ev["delta_ready"], 1)

        def make_norm1(eng, b):
            b = turn(b)
            eng.wait_ge(ev["rs1_ready"], done(b))
            eng.wait_ge(ev["z_ready"], done(2 * b - 1))
            eng.tensor_tensor(xn1[:, 1:T + 1], cen1[:], rs1[:], ALU.mult).then_inc(ev["xn1_ready"], 1)

        def make_norm3(eng, b):
            b = turn(b)
            eng.wait_ge(ev["rs3_ready"], done(b))
            eng.wait_ge(ev["logits_ready"], done(b - 1))
            eng.wait_ge(ev["xlo_ready"], done(b - 1))
            eng.tensor_tensor(xn3[:], cen3[:], rs3[:], ALU.mult).then_inc(ev["xn3_ready"], 1)

        def make_dt_s(eng, b):
            b = turn(b)
            eng.wait_ge(ev["dtrec_ready"], done(b))
            eng.tensor_tensor(dt_s[:], dt_exp[:], dt_rec[:], ALU.mult).then_inc(ev["dts_ready"], 1)

        def make_dx(eng, b):
            q = parity(b)
            b = turn(b)
            eng.wait_ge(ev["delta_ready"], done(b))
            eng.wait_ge(ev["bx_ready"], done(NS * (b - 1) - 1))
            eng.tensor_tensor(dx[q][:], delta[q][:], xc[q][:], ALU.mult).then_inc(ev["dx_ready"], 1)

        def make_gate(eng, b):
            q = parity(b)
            b = turn(b)
            eng.wait_ge(ev["y_ready2"], done(b))
            eng.tensor_tensor(yz[:], yb[:], zg[q][:], ALU.mult).then_inc(ev["gated"], 1)

        def make_norm2(eng, b):
            b = turn(b)
            eng.wait_ge(ev["rs2_ready"], done(b))
            eng.tensor_tensor(yn[:], cen2[:], over_halves(rs2[:]), ALU.mult).then_inc(ev["yn_ready"], 1)

        def pre_gpsimd(pool, b, at):
            if at == WHEN["norm1"]:
                make_norm1(pool, b)
            if at == WHEN["dt_s"]:
                make_dt_s(pool, b)
            if at == WHEN["dx"]:
                make_dx(pool, b)

        def pre_vector_alone(dve, b, at):
            if at == WHEN["series1"]:
                make_dt_s(dve, b)
            pre_vector(dve, b, at)
            if at == WHEN["rsqrt1_vector"]:
                make_norm1(dve, b)
            if at == WHEN["delta"]:
                make_dx(dve, b)

        def post_vector_alone(dve, b, at):
            post_vector(dve, b, at)
            if at == WHEN["sum_up"]:
                make_gate(dve, b)
            if at == WHEN["rsqrt2_vector"]:
                make_norm2(dve, b)
            if at == WHEN["rsqrt3_vector"]:
                make_norm3(dve, b)

        def cast_states(pe, b, s):
            q, n = parity(b), NS * turn(b) + s
            if s == 0:
                pe.wait_ge(ev["bc_ready"], done(turn(b)))
            pe.wait_ge(ev["bx_ready"], done(n - 2))
            pe.matmul(bank_b[s % 2][:, 0:T], pick[:, s:s + 1].broadcast_to([P, P]), bc[q][:], start=True, stop=True
                      ).then_inc(ev["b_cast"], 1)
            pe.wait_ge(ev["c_copied"], done(n - 1))
            pe.matmul(bank_c[:, 0:T], pick[:, NS + s:NS + s + 1].broadcast_to([P, P]), bc[q][:], start=True, stop=True
                      ).then_inc(ev["c_cast"], 1)

        def sum_states(pe, b, s):
            n = NS * turn(b) + s
            if s == 0:
                pe.wait_ge(ev["y_ready2"], done(turn(b) - 1))
            pe.wait_ge(ev["hc_ready"], done(n))
            for h in range(HALVES):
                last = pe.matmul(ysum[h][:, 0:T], ident[:], hc[s % DEEP][:, h, :], start=(s == 0), stop=(s == NS - 1))
            last.then_inc(ev["summed"], 1)
            if s == NS - 1:
                pe.wait_ge(ev["summed"], done(n))
                pe.sem_inc(ev["ysum_ready"], 1)

        def scan_tensor(pe, b, s, following, previous, beside):
            if s + CAST_AHEAD < NS:
                cast_states(pe, b, s + CAST_AHEAD)
            elif following:
                cast_states(pe, following, s + CAST_AHEAD - NS)
            beside(0)
            if s >= LAG:
                sum_states(pe, b, s - LAG)
            elif previous:
                sum_states(pe, previous, s - LAG + NS)
            beside(1)

        def decays(act, b, s):
            q, n = parity(b), NS * turn(b) + s
            if s == 0:
                act.wait_ge(ev["delta_ready"], done(turn(b)))
            act.wait_ge(ev["scan_done"], done(n - DEEP))
            for h in range(HALVES):
                last = act.activation(dA[s % DEEP][:, h, 1:T], delta[q][:, h, 1:T], ACT.Exp, scale=a_neg[:, h, s:s + 1])
            last.then_inc(ev["dA_ready"], 1)

        def copy_c(act, b, s):
            n = NS * turn(b) + s
            act.wait_ge(ev["c_cast"], done(n))
            act.wait_ge(ev["hc_ready"], done(n - DEEP))
            act.copy(cs[s % DEEP][:], bank_c[:, 0:T]).then_inc(ev["c_copied"], 1)

        def scan_scalar(act, b, s, following, previous, beside):
            if s + 1 < NS:
                copy_c(act, b, s + 1)
            elif following:
                copy_c(act, following, 0)
            if s + AHEAD < NS:
                decays(act, b, s + AHEAD)
            elif following:
                decays(act, following, s + AHEAD - NS)
            beside(0)
            beside(1)

        def scan_vector(dve, b, s, following, previous, beside):
            q, n = parity(b), NS * turn(b) + s
            if s == 0:
                dve.wait_ge(ev["dx_ready"], done(turn(b)))
            dve.wait_ge(ev["b_cast"], done(n))
            dve.tensor_tensor(bx[s % 2][:], dx[q][:], over_halves(bank_b[s % 2][:, 0:T]), ALU.mult).then_inc(ev["bx_ready"], 1)
            beside(0)
            dve.wait_ge(ev["bx_ready"], done(n))
            dve.wait_ge(ev["dA_ready"], done(n))
            dve.wait_ge(ev["hc_ready"], done(n - DEEP))
            dve.tensor_tensor_scan(hs[s % DEEP][:].rearrange("p h t -> p (h t)"),
                                   dA[s % DEEP][:].rearrange("p h t -> p (h t)"),
                                   bx[s % 2][:].rearrange("p h t -> p (h t)"), 0.0, ALU.mult, ALU.add
                                   ).then_inc(ev["scan_done"], 1)
            beside(1)

        def scan_gpsimd(pool, b, s, following, previous, beside):
            n = NS * turn(b) + s
            beside(0)
            pool.wait_ge(ev["scan_done"], done(n))
            pool.wait_ge(ev["c_copied"], done(n))
            pool.wait_ge(ev["summed"], done(n - DEEP))
            pool.tensor_tensor(hc[s % DEEP][:], hs[s % DEEP][:], over_halves(cs[s % DEEP][:]), ALU.mult
                               ).then_inc(ev["hc_ready"], 1)
            beside(1)

        def post_tensor(pe, b, at):
            b = turn(b)
            if at == WHEN["mean2"]:
                pe.wait_ge(ev["gated"], done(b))
                pe.wait_ge(ev["comb_ready"], done(b - 1))
                for h in range(HALVES):
                    last = pe.matmul(post[:, 0:T], ones_inner[:], yz[:, h, :], start=(h == 0), stop=(h == 1))
                last.then_inc(ev["mean2"], 1)
            if at == WHEN["var2"]:
                pe.wait_ge(ev["sq2_ready"], done(b))
                for h in range(HALVES):
                    last = pe.matmul(post[:, 0:T], ones_inner[:], sq2[:, h, :], start=(h == 0), stop=(h == 1))
                last.then_inc(ev["var2"], 1)
            if at == WHEN["out_proj"]:
                pe.wait_ge(ev["yn_ready"], done(b))
                for h in range(HALVES):
                    last = pe.matmul(post[:, 0:T], out_gT[:, h, :], yn[:, h, :], start=(h == 0), stop=(h == 1))
                last.then_inc(ev["proj_ready"], 1)
            if at == WHEN["mean3"]:
                pe.wait_ge(ev["h_ready"], done(b))
                pe.matmul(post[:, 0:T], ones_ln[:], tokens(hT, b), start=True, stop=True).then_inc(ev["mean3"], 1)
            if at == WHEN["var3"]:
                pe.wait_ge(ev["sq3_ready"], done(b))
                pe.matmul(post[:, 0:T], ones_ln[:], sq3[:], start=True, stop=True).then_inc(ev["var3"], 1)
            if at == WHEN["logits"]:
                pe.wait_ge(ev["xn3_ready"], done(b))
                for i, at in enumerate(ROUTE_AT):
                    pe.matmul(post[:, i * EXPERTS:(i + 1) * EXPERTS], xn3[:, at:at + P], rw_half[:], start=True, stop=False)
                    last = pe.matmul(post[:, i * EXPERTS:(i + 1) * EXPERTS], ones_row[:], rb[:], start=False, stop=True)
                last.then_inc(ev["logits_ready"], 1)
            if at == WHEN["comb_flip"]:
                pe.wait_ge(ev["cw_ready"], done(b))
                for i, at in enumerate(ROUTE_AT):
                    last = pe.transpose(post[:, at:at + P], cw[:, i, :, :].rearrange("p a e -> p (a e)"), ident[:])
                last.then_inc(ev["comb_flipped"], 1)

        def post_scalar(act, b, at):
            b = turn(b)
            if at == WHEN["sq2"]:
                act.wait_ge(ev["cen2_ready"], done(b))
                act.activation(sq2[:], cen2[:], ACT.Square).then_inc(ev["sq2_ready"], 1)
            if at == WHEN["rsqrt2_scalar"]:
                rsqrt_scalar(act, 2, b, post[:, 0:T])
            if at == WHEN["sq3"]:
                act.wait_ge(ev["cen3_ready"], done(b))
                act.activation(sq3[:], cen3[:], ACT.Square).then_inc(ev["sq3_ready"], 1)
            if at == WHEN["rsqrt3_scalar"]:
                rsqrt_scalar(act, 3, b, post[:, 0:T])
            if at == WHEN["x_high"]:
                act.wait_ge(ev["xn3_ready"], done(b))
                act.activation(tokens(x_hi, b), xn3[:], ACT.Copy, scale=-0.5 * XSCALE).then_inc(ev["xhi_ready"], 1)
            if at == WHEN["exp"]:
                act.wait_ge(ev["lg_ready"], done(b))
                act.activation(ex[:], lg[:], ACT.Exp).then_inc(ev["ex_ready"], 1)
            if at == WHEN["exp_again"]:
                act.wait_ge(ev["qn_ready"], done(b))
                for i in range(3):
                    last = act.activation(ew[:, i, :], qn[:, i, 0:EXPERTS], ACT.Exp, scale=-1.0, bias=srec[:, i:i + 1])
                last.then_inc(ev["ew_ready"], 1)
            if at == WHEN["comb_high"]:
                act.wait_ge(ev["comb_flipped"], done(b))
                act.activation(tokens(comb, b), post[:, 0:T], ACT.Copy, scale=CSCALE).then_inc(ev["comb_hi_ready"], 1)

        def post_vector(dve, b, at):
            q = parity(b)
            b = turn(b)
            if at == WHEN["sum_up"]:
                dve.wait_ge(ev["ysum_ready"], done(b))
                for h in range(HALVES):
                    last = dve.scalar_tensor_tensor(out=yb[:, h, :], in0=xc[q][:, h, :], scalar=vec[:, 2, h:h + 1],
                                                    in1=ysum[h][:, 0:T], op0=ALU.mult, op1=ALU.add)
                last.then_inc(ev["y_ready2"], 1)
            if at == WHEN["center2"]:
                dve.wait_ge(ev["mean2"], done(b))
                dve.tensor_tensor(cen2[:], yz[:], over_halves(post[:, 0:T]), ALU.subtract).then_inc(ev["cen2_ready"], 1)
            if at == WHEN["rsqrt2_vector"]:
                dve.wait_ge(ev["yn_ready"], done(b - 1))
                rsqrt_vector(dve, 2, b, post[:, 0:T], rs2)
            if at == WHEN["residual"]:
                dve.wait_ge(ev["proj_ready"], done(b))
                dve.scalar_tensor_tensor(out=tokens(hT, b), in0=post[:, 0:T], scalar=out_bias[:, 0:1],
                                         in1=tokens(hT, b), op0=ALU.add, op1=ALU.add).then_inc(ev["h_ready"], 1)
            if at == WHEN["center3"]:
                dve.wait_ge(ev["mean3"], done(b))
                dve.wait_ge(ev["xn3_ready"], done(b - 1))
                dve.tensor_tensor(cen3[:], tokens(hT, b), post[:, 0:T], ALU.subtract).then_inc(ev["cen3_ready"], 1)
            if at == WHEN["rsqrt3_vector"]:
                dve.wait_ge(ev["xn3_ready"], done(b - 1))
                rsqrt_vector(dve, 3, b, post[:, 0:T], rs3)
            if at == WHEN["x_low"]:
                dve.wait_ge(ev["xhi_ready"], done(b))
                dve.scalar_tensor_tensor(out=tokens(x_lo, b), in0=xn3[:], scalar=-0.5 * XSCALE, in1=tokens(x_hi, b),
                                         op0=ALU.mult, op1=ALU.subtract).then_inc(ev["xlo_ready"], 1)
            if at == WHEN["top"]:
                dve.wait_ge(ev["logits_ready"], done(b))
                logits = post[:, 0:3 * EXPERTS].rearrange("p (i e) -> p i e", e=EXPERTS)
                dve.tensor_reduce(top[:], logits, AX.X, ALU.max).then_inc(ev["top_ready"], 1)
                dve.wait_ge(ev["top_ready"], done(b))
                dve.tensor_tensor(lg[:], logits, over_experts(top[:]), ALU.subtract).then_inc(ev["lg_ready"], 1)
            if at == WHEN["probs"]:
                dve.wait_ge(ev["ex_ready"], done(b))
                dve.tensor_reduce(ssum[:], ex[:], AX.X, ALU.add).then_inc(ev["ssum_ready"], 1)
                dve.wait_ge(ev["ssum_ready"], done(b))
                dve.wait_ge(ev["ew_ready"], done(b - 1))
                dve.reciprocal(wrec[:], ssum[:]).then_inc(ev["srec_ready"], 1)
                dve.wait_ge(ev["srec_ready"], done(b))
                dve.tensor_scalar(srec[:], wrec[:], -1.0, None, ALU.mult).then_inc(ev["nsrec_ready"], 1)
                dve.wait_ge(ev["nsrec_ready"], done(b))
                dve.tensor_tensor(qn[:, :, 0:EXPERTS], ex[:], over_experts(srec[:]), ALU.mult)
                dve.memset(qn[:, :, EXPERTS:QCOLS], 1.0).then_inc(ev["qn_ready"], 1)
            for r in range(ROUNDS):
                if at == WHEN[f"drop{r + 1}"]:
                    if r == 0:
                        wait_apart(dve, "ew_ready", done(b))
                    else:
                        wait_apart(dve, "low_dropped", done(ROUNDS * b + r - 1))
                    for i in range(3):
                        last = dve.max(low8[:, i, :], qn[:, i, :])
                    last.then_inc(ev["low_found"], 1)
                    wait_apart(dve, "low_found", done(ROUNDS * b + r))
                    for i in range(3):
                        last = dve.match_replace(qn[:, i, :], low8[:, i, :], qn[:, i, :], -5.0)
                    last.then_inc(ev["low_dropped"], 1)
            if at == WHEN["weights"]:
                dve.wait_ge(ev["low_dropped"], done(ROUNDS * b + ROUNDS - 1))
                dve.scalar_tensor_tensor(out=wm[:], in0=qn[:, :, 0:EXPERTS], scalar=-2.0, in1=ew[:],
                                         op0=ALU.is_gt, op1=ALU.mult).then_inc(ev["wm_ready"], 1)
                dve.wait_ge(ev["wm_ready"], done(b))
                dve.tensor_reduce(wsum[:], wm[:], AX.X, ALU.add).then_inc(ev["wsum_ready"], 1)
                dve.wait_ge(ev["wsum_ready"], done(b))
                dve.reciprocal(wrec[:], wsum[:]).then_inc(ev["wrec_ready"], 1)
                dve.wait_ge(ev["wrec_ready"], done(b))
                dve.wait_ge(ev["comb_flipped"], done(b - 1))
                for a in range(2):
                    last = dve.tensor_tensor(cw[:, :, a, :], wm[:], over_experts(wrec[:]), ALU.mult)
                last.then_inc(ev["cw_ready"], 1)
            if at == WHEN["comb_low"]:
                dve.wait_ge(ev["comb_hi_ready"], done(b))
                low = tokens(comb, b, parts=slice(EXPERTS, P))
                dve.scalar_tensor_tensor(out=low, in0=post[EXPERTS:P, 0:T], scalar=CSCALE, in1=low,
                                         op0=ALU.mult, op1=ALU.subtract).then_inc(ev["comb_ready"], 1)

        def post_gpsimd(pool, b, at):
            if at == WHEN["gate"]:
                make_gate(pool, b)
            if at == WHEN["norm2"]:
                make_norm2(pool, b)
            if at == WHEN["norm3"]:
                make_norm3(pool, b)

        def turn(b):
            return b[0]

        def parity(b):
            return b[1]

        def steps(eng, pre_stage, scan_stage, post_stage, b, with_pre=True, with_post=True):
            t, q = b
            following = (t + 1, 1 - q) if with_pre else None
            previous = (t - 1, 1 - q) if with_post else None
            for s in range(NS):
                def beside(half):
                    if previous:
                        post_stage(eng, previous, 2 * s + half)
                    if following:
                        pre_stage(eng, following, 2 * s + half)
                scan_stage(eng, b, s, following, previous, beside)

        def alone(eng, stage, b, first=0, last=2 * STATES - 1):
            for at in range(first, last + 1):
                stage(eng, b, at)

        def run(eng, pre_stage, scan_stage, post_stage, first=0):
            pre_alone, post_alone = {
                scan_vector: (pre_vector_alone, post_vector_alone), scan_gpsimd: (None, None),
            }.get(scan_stage, (pre_stage, post_stage))
            if pre_alone:
                alone(eng, pre_alone, (0, 0), first=first)
            if scan_stage is scan_tensor:
                for s in range(CAST_AHEAD):
                    cast_states(eng, (0, 0), s)
            if scan_stage is scan_scalar:
                copy_c(eng, (0, 0), 0)
                for s in range(AHEAD):
                    decays(eng, (0, 0), s)
            steps(eng, pre_stage, scan_stage, post_stage, (0, 0), with_post=False)
            with eng.Fori(0, SEQS // 2 - 1) as i:
                steps(eng, pre_stage, scan_stage, post_stage, (2 * i + 1, 1))
                steps(eng, pre_stage, scan_stage, post_stage, (2 * i + 2, 0))
            steps(eng, pre_stage, scan_stage, post_stage, (SEQS - 1, 1), with_pre=False)
            if scan_stage is scan_tensor:
                for s in range(NS - LAG, NS):
                    sum_states(eng, (SEQS - 1, 1), s)
            if post_alone:
                alone(eng, post_alone, (SEQS - 1, 1))

        def start(eng, events):
            for name in events:
                eng.sem_inc(ev[name], BIAS)

        tap_banks = [ysum[0], ysum[1], bank_c]

        block = ctx.enter_context(nc.Block())

        @block.gpsimd
        def _(pool):
            start(pool, pool_events)
            pool.memset(ones_inner[:], 1.0 / INNER).then_inc(inner_ready, 1)
            pool.memset(ones_row[:], 1.0).then_inc(row_ready, 1)
            pool.memset(pick_raw[:], 0.0).then_inc(pick_zeroed, 1)
            for i in range(3):
                pool.wait_ge(pick_zeroed if i == 0 else pick_made, max(i, 1))
                pool.affine_select(out=pick_raw[:], in_=pick_raw[:], compare_op=ALU.not_equal, fill=1.0,
                                   base=-32 * (i + 1), pattern=[[-1, 2 * STATES]], channel_multiplier=1
                                   ).then_inc(pick_made, 1)
            pool.wait_ge(pick_made, 3)
            pool.tensor_copy(pick[:], pick_raw[:]).then_inc(pick_ready, 1)
            pool.memset(eps[:], EPS).then_inc(eps_ready, 1)
            pool.memset(two[:], 2.0).then_inc(eps_ready, 1)
            for i in range(2):
                pool.memset(shift[i][:], FACTORS[i][0]).then_inc(eps_ready, 1)
            pool.memset(xn1[:, 0:1], 0.0).then_inc(zero_ready, 1)
            pool.memset(xn1[:, T + 1:T + 2], 0.0).then_inc(zero_ready, 1)
            for i in range(DEEP):
                pool.memset(dA[i][:, :, 0:1], 0.0).then_inc(zero_ready, 1)
            run(pool, pre_gpsimd, scan_gpsimd, post_gpsimd)

        @block.tensor
        def _(pe):
            start(pe, pe_events)
            pe.wait_ge(tower_in, TOWER_IN)
            alone(pe, pre_tensor, (0, 0), last=WHEN["mean1"])
            pe.wait_ge(tap_rows_ready, 1)
            for i in range(3):
                for h in range(HALVES):
                    pe.transpose(tap_banks[i][:, h * P:(h + 1) * P], tap_rows[:, i, h, :], ident[:])
            for h in range(HALVES):
                last = pe.transpose(bank_b[0][:, h * P:(h + 1) * P], in_rows[:, HALVES + h, :], ident[:])
            last.then_inc(in_flipped, 1)
            NX = 1 + 2 * STATES
            for h in range(HALVES):
                last = pe.transpose(bank_b[1][:, h * P:h * P + NX], xp_rows[:, h * P:(h + 1) * P], ident[0:NX, 0:NX])
            last.then_inc(xp_flipped, 1)
            for h in range(HALVES):
                last = pe.transpose(post[:, h * P:(h + 1) * P], out_rows[:, h * P:(h + 1) * P], ident[:])
            last.then_inc(out_flipped, 1)
            alone(pe, pre_tensor, (0, 0), first=WHEN["mean1"] + 1, last=WHEN["var1"])
            pe.wait_ge(out_copied, 1)
            for h in range(HALVES):
                last = pe.matmul(post[:, 2 * P:2 * P + 1], out_T[:, h, :], vec[:, 4, h:h + 1], start=(h == 0), stop=(h == 1))
            last.then_inc(bias_summed, 1)
            pe.wait_ge(in_copied, 1)
            pe.wait_ge(rw_ready, 1)
            pe.wait_ge(xp_copied, 1)
            pe.wait_ge(out_copied, 2)
            pe.wait_ge(bias_ready, 1)
            pe.wait_ge(inner_ready, 1)
            pe.wait_ge(row_ready, 1)
            pe.wait_ge(pick_ready, 1)
            run(pe, pre_tensor, scan_tensor, post_tensor, first=WHEN["var1"] + 1)

        @block.scalar
        def _(act):
            start(act, act_events)
            act.wait_ge(tower_in, TOWER_IN)
            act.wait_ge(a_capped_ready, 1)
            act.activation(a_exp[:], a_capped[:], ACT.Exp).then_inc(a_exp_ready, 1)
            alone(act, pre_scalar, (0, 0), last=WHEN["sq1"])
            act.wait_ge(in_flipped, 1)
            for i in range(3):
                act.activation(in_T[:, i, :, :], tap_banks[i][:, 0:HALVES * P].rearrange("p (n e) -> p n e", e=P),
                               ACT.Copy, scale=-0.5)
            act.activation(z_T[:], bank_b[0][:, 0:HALVES * P].rearrange("p (n e) -> p n e", e=P),
                           ACT.Copy, scale=-0.5).then_inc(in_copied, 1)
            act.wait_ge(a_neg_ready, 1)
            act.wait_ge(zero_ready, 2 + DEEP)
            act.wait_ge(eps_ready, 4)
            run(act, pre_scalar, scan_scalar, post_scalar, first=WHEN["sq1"] + 1)

        @block.vector
        def _(dve):
            start(dve, dve_events)
            dve.wait_ge(tower_in, TOWER_IN)
            for i in range(3):
                for h in range(HALVES):
                    last = dve.tensor_scalar(tap_rows[:, i, h, :], in_rows[:, h, :], taps[:, h, i:i + 1], None, ALU.mult)
            last.then_inc(tap_rows_ready, 1)
            dve.tensor_scalar(a_capped[:], a_raw[:], A_LOG_CAP, None, ALU.min).then_inc(a_capped_ready, 1)
            alone(dve, pre_vector, (0, 0), last=WHEN["center1"])
            dve.wait_ge(a_exp_ready, 1)
            dve.tensor_scalar(a_neg[:], a_exp[:], -1.0, None, ALU.mult).then_inc(a_neg_ready, 1)
            dve.tensor_scalar(rw_half[:], rw[:], -0.5, None, ALU.mult).then_inc(rw_ready, 1)
            dve.memset(xp_T[:], 0.0).then_inc(xp_zeroed, 1)
            dve.wait_ge(xp_zeroed, 1)
            dve.wait_ge(xp_flipped, 1)
            for h in range(HALVES):
                dve.tensor_copy(xp_T[:, h, 0:1], bank_b[1][:, h * P:h * P + 1])
                for g in range(1, 4):
                    last = dve.tensor_copy(xp_T[:, h, 32 * g:32 * (g + 1)], bank_b[1][:, h * P + 1:h * P + 1 + 2 * STATES])
            last.then_inc(xp_copied, 1)
            dve.wait_ge(out_flipped, 1)
            dve.tensor_copy(out_T[:], post[:, 0:HALVES * P].rearrange("p (h d) -> p h d", d=P)).then_inc(out_copied, 1)
            dve.wait_ge(out_copied, 1)
            for h in range(HALVES):
                last = dve.tensor_scalar(out_gT[:, h, :], out_T[:, h, :], vec[:, 3, h:h + 1], -0.5, ALU.mult, ALU.mult)
            last.then_inc(out_copied, 1)
            dve.wait_ge(bias_summed, 1)
            dve.tensor_copy(out_bias[:], post[:, 2 * P:2 * P + 1]).then_inc(bias_ready, 1)
            dve.wait_ge(bias_ready, 1)
            dve.wait_ge(zero_ready, 2 + DEEP)
            run(dve, pre_vector, scan_vector, post_vector, first=WHEN["center1"] + 1)


def experts(nc, hT, ident, x_hi, x_lo, comb, early, first_in, w1, w2, out):
    sems = []
    with ExitStack() as ctx:
        ctx.callback(clear, nc, sems)

        def sb(name, shape, dt=F32):
            return ctx.enter_context(nc.sbuf_tensor(name, shape, dt))

        def bank(name):
            return ctx.enter_context(nc.psum_tensor(name, [P, 512], F32))

        BUFS = 4
        w_hi = sb("w_hi", [P, GROUPS * 2 * GROUP_COLS], F16)
        w_lo = sb("w_lo", [P, GROUPS * 2 * GROUP_COLS], F16)
        stage, b1_T, b2_in = early
        b2_hi, b2_lo = sb("b2_hi", [P, DIM], F16), sb("b2_lo", [P, DIM], F16)
        sel_raw = sb("sel_raw", [P, EXPERTS])
        sel = sb("sel", [P, GROUPS * P], F16)
        g = [sb(f"g{i}", [P, HALVES, T]) for i in range(2)]
        m = [sb(f"m{i}", [P, HALVES, T]) for i in range(BUFS)]
        m_hi = [sb(f"m_hi{i}", [P, HALVES, T], F16) for i in range(BUFS)]
        m_lo = [sb(f"m_lo{i}", [P, HALVES, T], F16) for i in range(BUFS)]
        o_T = sb("o_T", [P, T])
        o_rows = sb("o_rows", [P, 3, P])

        up_bank = [[bank(f"up{j}_{h}") for h in range(HALVES)] for j in range(2)]
        cast = [bank(f"cast{i}") for i in range(2)]
        y = bank("y")
        turned = bank("turned")

        def sem(name):
            sems.append(ctx.enter_context(nc.semaphore(name)))
            return sems[-1]

        stage_in = [sem(f"stage{i}_in") for i in range(2)]
        split_hi, split_lo = [sem(f"split{i}_hi") for i in range(2)], sem("split_lo")
        sel_zeroed, sel_made, sel_ready = sem("sel_zeroed"), sem("sel_made"), sem("sel_ready")
        b2_hi_ready, b2_ready = sem("b2_hi_ready"), sem("b2_ready")
        up_ready = [sem(f"up{h}_ready") for h in range(HALVES)]
        cast_ready, gelu_done, m_ready = sem("cast_ready"), sem("gelu_done"), sem("m_ready")
        hi_ready, down_done = sem("hi_ready"), sem("down_done")
        lo_ready = {"dve": sem("dve_lo_ready"), "pool": sem("pool_lo_ready")}
        o_ready, o_flipped, rows_ready, stored = (
            sem("o_ready"), sem("o_flipped"), sem("rows_ready"), sem("stored"))

        LAG = 3
        LO_ON = ["dve", "pool", "pool", "pool"] * 2
        STORES = 2
        LAYERS = 2
        SPLITS = 2 * LAYERS

        def weight(buf, layer, grp, j, h):
            return buf[:, bass.ds((LAYERS * grp + layer) * GROUP_COLS + (HALVES * j + h) * P, P)]

        def tokens(buf, b):
            return buf[:, bass.ds(b * T, T)]

        def wait_lo(eng, group, j):
            who = LO_ON[j % GROUP]
            per = LO_ON.count(who)
            eng.wait_ge(lo_ready[who], done(per * group + LO_ON[:j].count(who)))

        def spread(pe, b, grp, u):
            n = EXPERTS * b + GROUP * grp
            pe.wait_ge(m_ready, done(n - GROUP - 1))
            pe.matmul(cast[u][:, 0:T], sel[:, bass.ds(P * grp, P)], tokens(comb, b), start=True, stop=True).then_inc(cast_ready, 1)

        def up(pe, b, grp, j):
            n = EXPERTS * b + GROUP * grp + j
            for h in range(HALVES):
                pe.wait_ge(gelu_done, done(2 * (n - 2) + h))
                w_h, w_l = (weight(w, 0, grp, j, h) for w in (w_hi, w_lo))
                pe.matmul(up_bank[j % 2][h][:, 0:T], w_h, tokens(x_hi, b), start=True, stop=False)
                pe.matmul(up_bank[j % 2][h][:, 0:T], w_h, tokens(x_lo, b), start=False, stop=False)
                pe.matmul(up_bank[j % 2][h][:, 0:T], w_l, tokens(x_hi, b), start=False, stop=True).then_inc(up_ready[h], 1)

        def down(pe, b, grp, j, last):
            n = EXPERTS * b + GROUP * grp + j
            pe.wait_ge(hi_ready, done(n))
            wait_lo(pe, GROUPS * b + grp, j)
            for h in range(HALVES):
                w_h, w_l = (weight(w, 1, grp, j, h) for w in (w_hi, w_lo))
                pe.matmul(y[:, 0:T], w_h, m_hi[j % BUFS][:, h, :], start=False, stop=False)
                pe.matmul(y[:, 0:T], w_h, m_lo[j % BUFS][:, h, :], start=False, stop=False)
                mm = pe.matmul(y[:, 0:T], w_l, m_hi[j % BUFS][:, h, :], start=False, stop=last and h == HALVES - 1)
            mm.then_inc(down_done, 1)

        def tensor_start(pe, b):
            pe.wait_ge(o_ready, done(b - 1))
            pe.matmul(y[:, 0:T], b2_hi[:], tokens(comb, b), start=True, stop=False)
            pe.matmul(y[:, 0:T], b2_lo[:], tokens(comb, b), start=False, stop=False)

        def turn_back(pe, b):
            pe.wait_ge(o_ready, done(b))
            pe.wait_ge(rows_ready, done(b - 1))
            for i, (a, z) in enumerate(OUT_TILES):
                last = pe.transpose(turned[0:z, i * P:(i + 1) * P], o_T[:, a:a + z], ident[:])
            last.then_inc(o_flipped, 1)

        def tensor_group(pe, b, grp, u, first, tail, end, between=None):
            for j in range(GROUP):
                ahead = j + LAG
                if not (tail and end and ahead >= GROUP):
                    to_b, to_grp, to_j = b, grp, ahead
                    if ahead >= GROUP:
                        to_b, to_grp, to_j = (b + 1, 0, ahead - GROUP) if tail else (b, grp + 1, ahead - GROUP)
                    if first and not (tail and ahead >= GROUP) and to_j == 0:
                        pe.wait_ge(split_lo, SPLITS * to_grp + 2)
                    if to_j == 0:
                        if first:
                            pe.wait_ge(sel_ready, 2)
                        spread(pe, to_b, to_grp, 1 - u)
                    up(pe, to_b, to_grp, to_j)
                if j == 0 and isinstance(grp, int) and grp == 0:
                    tensor_start(pe, b)
                if first and j % (GROUP // 2) == 0:
                    pe.wait_ge(split_lo, SPLITS * grp + 3 + j // (GROUP // 2))
                down(pe, b, grp, j, tail and j == GROUP - 1)
                if between and u == 0 and j == 2:
                    between()

        def gelu(act, b, grp, j):
            n = EXPERTS * b + GROUP * grp + j
            act.wait_ge(m_ready, done(n - 2))
            for h in range(HALVES):
                act.wait_ge(up_ready[h], done(n))
                act.activation(g[j % 2][:, h, :], up_bank[j % 2][h][:, 0:T], ACT.Gelu, scale=1 / (XSCALE * WSCALE),
                               bias=b1_T[:, bass.ds(BLOCKS * grp + HALVES * j + h, 1)]).then_inc(gelu_done, 1)

        def high(act, n, j):
            act.wait_ge(m_ready, done(n))
            act.wait_ge(down_done, done(n - BUFS))
            act.copy(m_hi[j % BUFS][:], m[j % BUFS][:]).then_inc(hi_ready, 1)

        def scalar_group(act, b, grp, u, first, tail, end, between=None):
            for j in range(GROUP):
                n = EXPERTS * b + GROUP * grp + j
                gelu(act, b, grp, j)
                if first and not tail and j in (2, 4):
                    split_high(act, grp + 1, 0, j // 2 - 1)
                if not (first and isinstance(grp, int) and grp == 0 and j == 0):
                    high(act, n - 1, (j - 1) % GROUP)
                if between and u == 1 and j == 1:
                    between()
            if end and tail:
                high(act, n, GROUP - 1)

        def staged(layer, i):
            return stage[i][:].rearrange("p (c k) -> p k c", k=BLOCKS) if layer == 0 else stage[i][:]

        def split_part(buf, grp, layer, i):
            if layer == 0:
                return buf[:, bass.ds(LAYERS * grp * GROUP_COLS, GROUP_COLS)].rearrange(
                    "p (k c) -> p k c", k=BLOCKS)[:, :, i * P // 2:(i + 1) * P // 2]
            return buf[:, bass.ds((LAYERS * grp + 1) * GROUP_COLS + i * STAGE_COLS, STAGE_COLS)]

        def split_high(eng, grp, layer, i):
            if not (isinstance(grp, int) and grp == 0 and layer == 0):
                eng.wait_ge(stage_in[i], 16 * (LAYERS * grp + layer))
            if layer == 0:
                eng.activation(split_part(w_hi, grp, 0, i), staged(0, i), ACT.Copy, scale=WSCALE).then_inc(split_hi[0], 1)
            else:
                eng.tensor_scalar(split_part(w_hi, grp, 1, i), staged(1, i), WSCALE, None, ALU.mult
                                  ).then_inc(split_hi[1], 1)

        def split_low(dve, grp, layer, i):
            dve.wait_ge(split_hi[layer], 2 * grp + i + 1)
            dve.scalar_tensor_tensor(out=split_part(w_lo, grp, layer, i), in0=staged(layer, i), scalar=WSCALE,
                                     in1=split_part(w_hi, grp, layer, i), op0=ALU.mult, op1=ALU.subtract
                                     ).then_inc(split_lo, 1)

        def weigh(dve, b, grp, u, j):
            n = EXPERTS * b + GROUP * grp + j
            dve.wait_ge(gelu_done, done(2 * n + 1))
            if j == 0:
                dve.wait_ge(cast_ready, done(GROUPS * b + grp))
            dve.wait_ge(hi_ready, done(n - BUFS))
            if j >= BUFS:
                wait_lo(dve, GROUPS * b + grp, j - BUFS)
            else:
                wait_lo(dve, GROUPS * b + grp - 1, j - BUFS + GROUP)
            dve.tensor_tensor(m[j % BUFS][:], g[j % 2][:],
                              cast[u][:, 0:T].unsqueeze(1).broadcast_to([P, HALVES, T]), ALU.mult).then_inc(m_ready, 1)

        def low(eng, n, j):
            eng.wait_ge(hi_ready, done(n))
            eng.wait_ge(down_done, done(n - BUFS))
            eng.tensor_tensor(m_lo[j % BUFS][:], m[j % BUFS][:], m_hi[j % BUFS][:], ALU.subtract).then_inc(lo_ready[LO_ON[j]], 1)

        def vector_group(dve, b, grp, u, first, tail, end, between=None):
            for j in range(GROUP):
                n = EXPERTS * b + GROUP * grp + j
                weigh(dve, b, grp, u, j)
                if LO_ON[(j - 1) % GROUP] == "dve" and not (first and isinstance(grp, int) and grp == 0 and j == 0):
                    low(dve, n - 1, (j - 1) % GROUP)
                if first and isinstance(grp, int) and grp == 0 and j < 2:
                    split_high(dve, 0, 1, j)
                    split_low(dve, 0, 1, j)
                if first and not (isinstance(grp, int) and grp == 0) and j == 0:
                    split_low(dve, grp, 1, 1)
                if first and not tail:
                    if j in (2, 4):
                        split_low(dve, grp + 1, 0, j // 2 - 1)
                    if j in (5, 7):
                        split_high(dve, grp + 1, 1, j // 2 - 2)
                    if j == 6:
                        split_low(dve, grp + 1, 1, 0)
                if between and u == 0 and j == 1:
                    between()
            if end and tail and LO_ON[GROUP - 1] == "dve":
                low(dve, n, GROUP - 1)

        def gpsimd_group(pool, b, grp, u, first, tail, end, between=None):
            for j in range(GROUP):
                if LO_ON[j] == "pool":
                    low(pool, EXPERTS * b + GROUP * grp + j, j)

        def sequence(eng, group, b, first=False, end=False, between=None):
            for u in range(2):
                group(eng, b, u, u, first, False, end, between)
            with eng.Fori(1, GROUPS // 2 - 1) as pair:
                for u in range(2):
                    group(eng, b, 2 * pair + u, u, first, False, end)
            for u in range(2):
                group(eng, b, GROUPS - 2 + u, u, first, u == 1, end)

        block = ctx.enter_context(nc.Block())

        @block.sync
        def _(sp):
            sp.sem_inc(stored, BIAS)

            def load(g, layer, i):
                sp.wait_ge(split_lo, SPLITS * g + 2 * layer + i - 1)
                sp.dma_start(*weight_load(stage, w1, w2, g, layer, i)).then_inc(stage_in[i], 16)

            for i in range(2):
                load(0, 1, i)
            with sp.Fori(1, GROUPS) as g:
                for layer in range(LAYERS):
                    for i in range(2):
                        load(g, layer, i)
            rows = out.rearrange("b t d -> (b t) d")
            with sp.Fori(0, SEQS) as b:
                sp.wait_ge(rows_ready, done(b))
                sp.dma_start(rows[bass.ds(b * T, 2 * P), :].rearrange("(n p) d -> p n d", p=P), o_rows[:, 0:2, :]
                             ).then_inc(stored, 16)
                sp.dma_start(rows[bass.ds(b * T + 2 * P, T - 2 * P), :], o_rows[0:T - 2 * P, 2, :]).then_inc(stored, 16)
            sp.wait_ge(stored, 16 * STORES * SEQS + BIAS)

        @block.gpsimd
        def _(pool):
            pool.sem_inc(lo_ready["pool"], BIAS)
            pool.memset(sel_raw[:], 0.0).then_inc(sel_zeroed, 1)
            for i in range(2):
                pool.wait_ge(sel_zeroed if i == 0 else sel_made, 1)
                pool.affine_select(out=sel_raw[:], in_=sel_raw[:], compare_op=ALU.not_equal, fill=SELSCALE,
                                   base=-(EXPERTS - 1) - EXPERTS * i, pattern=[[1, EXPERTS]], channel_multiplier=1
                                   ).then_inc(sel_made, 1)
            pool.wait_ge(sel_made, 2)
            UNITS = P // GROUP
            for a, z in ((0, GROUP), (GROUP, EXPERTS)):
                pool.tensor_copy(sel[:, a * UNITS:z * UNITS].rearrange("p (e r) -> p e r", r=UNITS),
                                 sel_raw[:, a:z].unsqueeze(2).broadcast_to([P, z - a, UNITS])).then_inc(sel_ready, 1)
            sequence(pool, gpsimd_group, 0, first=True)
            with pool.Fori(1, SEQS - 1) as b:
                sequence(pool, gpsimd_group, b)
            sequence(pool, gpsimd_group, SEQS - 1, end=True)

        @block.tensor
        def _(pe):
            for s in (*up_ready, cast_ready, down_done, o_flipped):
                pe.sem_inc(s, BIAS)
            pe.wait_ge(sel_ready, 1)
            pe.wait_ge(b2_ready, 1)
            spread(pe, 0, 0, 0)
            pe.wait_ge(split_lo, 2)
            for j in range(LAG):
                up(pe, 0, 0, j)
            sequence(pe, tensor_group, 0, first=True)
            with pe.Fori(1, SEQS - 1) as b:
                sequence(pe, tensor_group, b, between=lambda: turn_back(pe, b - 1))
            sequence(pe, tensor_group, SEQS - 1, end=True, between=lambda: turn_back(pe, SEQS - 2))
            turn_back(pe, SEQS - 1)

        @block.scalar
        def _(act):
            def copy_rows(b):
                act.wait_ge(o_flipped, done(b))
                act.wait_ge(stored, 16 * STORES * b + BIAS)
                act.copy(o_rows[:, 0:2, :], turned[:, 0:2 * P].rearrange("p (n d) -> p n d", d=P))
                act.copy(o_rows[0:T - 2 * P, 2, :], turned[0:T - 2 * P, 2 * P:3 * P]).then_inc(rows_ready, 1)

            for s in (gelu_done, hi_ready, rows_ready):
                act.sem_inc(s, BIAS)
            act.wait_ge(first_in, FIRST_IN)
            for i in range(2):
                split_high(act, 0, 0, i)
            act.copy(b2_hi[:], b2_in[:]).then_inc(b2_hi_ready, 1)
            act.preload_act_table_set("gelu_and_others")
            sequence(act, scalar_group, 0, first=True)
            with act.Fori(1, SEQS - 1) as b:
                sequence(act, scalar_group, b, between=lambda: copy_rows(b - 1))
            sequence(act, scalar_group, SEQS - 1, end=True, between=lambda: copy_rows(SEQS - 2))
            copy_rows(SEQS - 1)

        @block.vector
        def _(dve):
            def add_up(b):
                dve.wait_ge(down_done, done(EXPERTS * b + EXPERTS - 1))
                dve.wait_ge(o_flipped, done(b - 1))
                dve.scalar_tensor_tensor(out=o_T[:], in0=y[:, 0:T], scalar=1 / CSCALE, in1=tokens(hT, b),
                                         op0=ALU.mult, op1=ALU.add).then_inc(o_ready, 1)

            for s in (m_ready, lo_ready["dve"], o_ready):
                dve.sem_inc(s, BIAS)
            dve.wait_ge(first_in, FIRST_IN)
            for i in range(2):
                split_low(dve, 0, 0, i)
            dve.wait_ge(b2_hi_ready, 1)
            dve.tensor_tensor(b2_lo[:], b2_in[:], b2_hi[:], ALU.subtract).then_inc(b2_ready, 1)
            sequence(dve, vector_group, 0, first=True)
            with dve.Fori(1, SEQS - 1) as b:
                sequence(dve, vector_group, b, between=lambda: add_up(b - 1))
            sequence(dve, vector_group, SEQS - 1, end=True, between=lambda: add_up(SEQS - 2))
            add_up(SEQS - 1)


_INS = ["x", "L0_tok_W", "L0_tok_b", "L0_tok_gamma", "L0_tok_beta", "L0_attn_in_proj_w", "L0_attn_x_proj_w",
        "L0_attn_dt_w", "L0_attn_dt_b", "L0_attn_conv_w", "L0_attn_conv_b", "L0_attn_A_log", "L0_attn_D_param",
        "L0_attn_out_w", "L0_attn_ln_g", "L0_attn_ln_b", "L0_ffn_w1", "L0_ffn_b1", "L0_ffn_w2", "L0_ffn_b2",
        "L0_ffn_router_w", "L0_ffn_router_b"]

_COLUMNS = ["L0_tok_b", "L0_tok_gamma", "L0_tok_beta", "L0_attn_dt_b", "L0_attn_conv_b", "L0_attn_D_param",
            "L0_attn_ln_g", "L0_attn_ln_b"]


def kernel(**inputs):
    import concourse.bacc as _bacc
    from concourse.bass_utils import run_bass_kernel_spmd as _run

    nc = _bacc.Bacc("TRN2", target_bir_lowering=False, num_devices=1)
    arrays, args = {}, []
    for name in _INS:
        a = np.ascontiguousarray(inputs[name])
        if name in ("L0_ffn_router_w", "L0_ffn_router_b", "L0_ffn_b2"):
            axis = 0 if name == "L0_ffn_b2" else a.ndim - 1
            a = np.ascontiguousarray(np.flip(a, axis=axis))
        if name in _COLUMNS:
            a = np.ascontiguousarray(a.reshape(-1, P).T)
        if name == "L0_attn_dt_w":
            a = a.reshape(1, -1)
        arrays[f"in_{name}_dram"] = a
        args.append(nc.dram_tensor(f"in_{name}_dram", a.shape, mybir.dt.from_np(a.dtype), kind="ExternalInput").ap())
    result = nc.dram_tensor("out_0_dram", (SEQS, T, DIM), F32, kind="ExternalOutput").ap()
    build(nc, *args, result)
    r = _run(nc, [arrays], core_ids=[0])
    return r.results[0]["out_0_dram"]
```
